# Optimizing a Trainium2 kernel written in Bass

```python
import numpy as np
import jax
import jax.numpy as jnp

def _softmax(x, axis=-1):
    return jax.nn.softmax(x, axis=axis)

def _gelu(x):
    return jax.nn.gelu(x, approximate=True)

def _silu(x):
    return jax.nn.silu(x)

def _sigmoid(x):
    return jax.nn.sigmoid(x)

def _layernorm(x, axis=-1, eps=1e-05):
    m = jnp.mean(x, axis=axis, keepdims=True)
    v = jnp.var(x, axis=axis, keepdims=True)
    return (x - m) / jnp.sqrt(v + eps)

def _scatter_add(tgt, idx, src, axis=0):
    return tgt.at[idx].add(src)

def _segment_sum(src, seg, n):
    return jax.ops.segment_sum(src, seg, n)
kernel_name = 'mk_pixart_resid_d2_seqx_r8_7bfd85'

def setup_inputs(seed: int=0):
    np.random.seed(seed)
    _w = jnp.asarray

    def _rec_inputs():
        import jax
        import jax.numpy as jnp
        _rk = jax.random.key(seed)
        x = -0.0002928 + 1 * jax.random.normal(jax.random.fold_in(_rk, 1), (2, 512, 128), jnp.float32)
        _lenS = 512 - jax.random.randint(jax.random.fold_in(_rk, 7), (2,), 0, max(1, 512 // 4) + 1, jnp.int32)
        _lenS2 = 154 - jax.random.randint(jax.random.fold_in(_rk, 8), (2,), 0, max(1, 154 // 4) + 1, jnp.int32)
        cond_1024 = 0.0061147 + 1.02565 * jax.random.normal(jax.random.fold_in(_rk, 11), (2, 128), jnp.float32)
        _ctx_1024P = jax.random.normal(jax.random.fold_in(_rk, 12), (2, 16, 128), jnp.float32)
        _ctx_1024c = jax.random.dirichlet(jax.random.fold_in(_rk, 512), 0.3 * jnp.ones((16,), jnp.float32), (2, 154))
        _ctx_1024t = jnp.einsum('bsk,bkd->bsd', _ctx_1024c, _ctx_1024P)
        _ctx_1024t = _ctx_1024t * jax.lax.rsqrt(jnp.mean(jnp.square(_ctx_1024t)) + 1e-12) * 0.953939
        ctx_1024 = 0.00086875 + 0.999764 * (_ctx_1024t + 0.3 * jax.random.normal(jax.random.fold_in(_rk, 612), (2, 154, 128), jnp.float32))
        _validS = jnp.arange(512)[None, :] < _lenS[:, None]
        _validS2 = jnp.arange(154)[None, :] < _lenS2[:, None]
        _causal = jnp.tril(jnp.ones((512, 512), dtype=bool))
        mask_BxS_bf0 = jnp.logical_not(jnp.ones((2, 512), dtype=bool))
        mask_BxS2_bf0 = jnp.logical_not(jnp.ones((2, 154), dtype=bool))
        return (x, cond_1024, ctx_1024, mask_BxS_bf0, mask_BxS2_bf0)
    x, cond_1024, ctx_1024, mask_BxS_bf0, mask_BxS2_bf0 = _rec_inputs()

    def _L0_xcond_setup():
        import jax, jax.numpy as jnp
        import numpy as np
        NL, D, H, DFF = (6, 128, 16, 512)
        HD = D // H

        def _rope(x):
            L = x.shape[1]
            half = HD // 2
            inv = 1.0 / 10000.0 ** (jnp.arange(half, dtype=jnp.float32) / half)
            ang = jnp.arange(L, dtype=jnp.float32)[:, None] * inv
            cos = jnp.cos(ang)[None, :, None, :]
            sin = jnp.sin(ang)[None, :, None, :]
            x1, x2 = (x[..., :half], x[..., half:])
            return jnp.concatenate([x1 * cos - x2 * sin, x1 * sin + x2 * cos], axis=-1)

        def _ln(x, eps=1e-05):
            m = jnp.mean(x, axis=-1, keepdims=True)
            v = jnp.var(x, axis=-1, keepdims=True)
            return (x - m) * jax.lax.rsqrt(v + eps)

        def _adaln(x, emb, w, b):
            gb = emb[:, 0, :] @ w.T + b
            g, be = jnp.split(gb, 2, axis=-1)
            return _ln(x) * (1.0 + g[:, None, :]) + be[:, None, :]

        def _attn(q, k, v, mask):
            scores = jnp.einsum('bqhd,bkhd->bhqk', q, k) / np.float32(np.sqrt(HD))
            scores = jnp.where(mask[:, None, None, :], jnp.float32(-jnp.inf), scores)
            w = jax.nn.softmax(scores, axis=-1)
            return jnp.einsum('bhqk,bkhd->bqhd', w, v)
        key = jax.random.key(seed)
        ks = jax.random.split(key, 20)
        B, L, LC = (4, 128, 64)
        s = 0.02
        inp = {'x': jax.random.normal(ks[0], (B, L, D), jnp.float32), 'noise_emb': jax.random.normal(ks[1], (B, 1, D), jnp.float32), 'context': jax.random.normal(ks[2], (B, LC, D), jnp.float32), 'src_mask': jnp.zeros((B, L), bool), 'ctx_mask': jnp.zeros((B, LC), bool), 'n1_w': jax.random.normal(ks[3], (NL, 2 * D, D), jnp.float32) * s, 'n1_b': jnp.zeros((NL, 2 * D), jnp.float32), 'n2_w': jax.random.normal(ks[4], (NL, 2 * D, D), jnp.float32) * s, 'n2_b': jnp.zeros((NL, 2 * D), jnp.float32), 'n3_w': jax.random.normal(ks[5], (NL, 2 * D, D), jnp.float32) * s, 'n3_b': jnp.zeros((NL, 2 * D), jnp.float32), 'qkv_w': jax.random.normal(ks[6], (NL, 3 * D, D), jnp.float32) * s, 'so_w': jax.random.normal(ks[7], (NL, D, D), jnp.float32) * s, 'cq_w': jax.random.normal(ks[8], (NL, D, D), jnp.float32) * s, 'ck_w': jax.random.normal(ks[9], (NL, D, D), jnp.float32) * s, 'cv_w': jax.random.normal(ks[10], (NL, D, D), jnp.float32) * s, 'co_w': jax.random.normal(ks[11], (NL, D, D), jnp.float32) * s, 'f1_w': jax.random.normal(ks[12], (NL, DFF, D), jnp.float32) * s, 'f1_b': jnp.zeros((NL, DFF), jnp.float32), 'f2_w': jax.random.normal(ks[13], (NL, D, DFF), jnp.float32) * s, 'f2_b': jnp.zeros((NL, D), jnp.float32)}
        return inp
    _L0_xcond_all = _L0_xcond_setup()
    _L0_xcond_in = {k: v for k, v in _L0_xcond_all.items() if k in ('n1_w', 'n1_b', 'n2_w', 'n2_b', 'n3_w', 'n3_b', 'qkv_w', 'so_w', 'cq_w', 'ck_w', 'cv_w', 'co_w', 'f1_w', 'f1_b', 'f2_w', 'f2_b')}
    del _L0_xcond_all

    def _L0_ffn_setup():
        import jax, jax.numpy as jnp
        import numpy as np
        E = 8
        K = 2
        C = 128
        F = 256
        EPS = 1e-05
        key = jax.random.key(seed)
        ks = jax.random.split(key, 6)
        x = jax.random.normal(ks[0], (2, 128, C), dtype=jnp.float32)
        ln_gamma = 1.0 + 0.02 * jax.random.normal(ks[1], (C,), dtype=jnp.float32)
        ln_beta = 0.02 * jax.random.normal(ks[2], (C,), dtype=jnp.float32)
        gate_w = jax.random.normal(ks[3], (E, C), dtype=jnp.float32) / np.sqrt(C)
        w1 = jax.random.normal(ks[4], (E, F, C), dtype=jnp.float32) / np.sqrt(C)
        w2 = jax.random.normal(ks[5], (E, C, F), dtype=jnp.float32) / np.sqrt(F)
        return {'x': x, 'ln_gamma': ln_gamma, 'ln_beta': ln_beta, 'gate_w': gate_w, 'w1': w1, 'w2': w2}
    _L0_ffn_all = _L0_ffn_setup()
    _L0_ffn_in = {k: v for k, v in _L0_ffn_all.items() if k in ('ln_gamma', 'ln_beta', 'gate_w', 'w1', 'w2')}
    del _L0_ffn_all

    def _L1_xcond_setup():
        import jax, jax.numpy as jnp
        import numpy as np
        B, T, S, H, E = (128, 32, 32, 128, 128)
        key = jax.random.key(seed)
        ks = jax.random.split(key, 8)
        sc = lambda n: 1.0 / np.sqrt(n)
        return dict(dec_seq=jax.random.normal(ks[0], (B, T, E), jnp.float32), enc_hiddens=jax.random.normal(ks[1], (B, S, H), jnp.float32), last_hidden=jax.random.normal(ks[2], (B, H), jnp.float32), W_att=jax.random.normal(ks[3], (2 * H, H), jnp.float32) * sc(2 * H), V_att=jax.random.normal(ks[4], (H, 1), jnp.float32) * sc(H), Wi=jax.random.normal(ks[5], (E + H, 3 * H), jnp.float32) * sc(E + H), Uh=jax.random.normal(ks[6], (H, 3 * H), jnp.float32) * sc(H), b=jnp.zeros((3 * H,), jnp.float32))
    _L1_xcond_all = _L1_xcond_setup()
    _L1_xcond_in = {k: v for k, v in _L1_xcond_all.items() if k in ('W_att', 'V_att', 'Wi', 'Uh', 'b')}
    del _L1_xcond_all

    def _L1_ffn_setup():
        import jax, jax.numpy as jnp
        import numpy as np
        H = 128
        I = 256
        E = 8
        B, S = (2, 128)

        def _swiglu(x, wg, wu, wd):
            return jax.nn.silu(x @ wg) * (x @ wu) @ wd
        key = jax.random.key(seed)
        ks = jax.random.split(key, 8)
        sc_h = 1.0 / np.sqrt(H)
        sc_i = 1.0 / np.sqrt(I)
        return {'hidden_states': jax.random.normal(ks[0], (B, S, H), jnp.float32), 'gate_w': jax.random.normal(ks[1], (H, E), jnp.float32) * sc_h, 'sh_gate': jax.random.normal(ks[2], (H, I), jnp.float32) * sc_h, 'sh_up': jax.random.normal(ks[3], (H, I), jnp.float32) * sc_h, 'sh_down': jax.random.normal(ks[4], (I, H), jnp.float32) * sc_i, 'rt_gate': jax.random.normal(ks[5], (E, H, I), jnp.float32) * sc_h, 'rt_up': jax.random.normal(ks[6], (E, H, I), jnp.float32) * sc_h, 'rt_down': jax.random.normal(ks[7], (E, I, H), jnp.float32) * sc_i}
    _L1_ffn_all = _L1_ffn_setup()
    _L1_ffn_in = {k: v for k, v in _L1_ffn_all.items() if k in ('gate_w', 'sh_gate', 'sh_up', 'sh_down', 'rt_gate', 'rt_up', 'rt_down')}
    del _L1_ffn_all
    return {'x': x, 'cond_1024': cond_1024, 'ctx_1024': ctx_1024, 'mask_BxS_bf0': mask_BxS_bf0, 'mask_BxS2_bf0': mask_BxS2_bf0, 'L0_xcond_n1_w': _L0_xcond_in['n1_w'], 'L0_xcond_n1_b': _L0_xcond_in['n1_b'], 'L0_xcond_n2_w': _L0_xcond_in['n2_w'], 'L0_xcond_n2_b': _L0_xcond_in['n2_b'], 'L0_xcond_n3_w': _L0_xcond_in['n3_w'], 'L0_xcond_n3_b': _L0_xcond_in['n3_b'], 'L0_xcond_qkv_w': _L0_xcond_in['qkv_w'], 'L0_xcond_so_w': _L0_xcond_in['so_w'], 'L0_xcond_cq_w': _L0_xcond_in['cq_w'], 'L0_xcond_ck_w': _L0_xcond_in['ck_w'], 'L0_xcond_cv_w': _L0_xcond_in['cv_w'], 'L0_xcond_co_w': _L0_xcond_in['co_w'], 'L0_xcond_f1_w': _L0_xcond_in['f1_w'], 'L0_xcond_f1_b': _L0_xcond_in['f1_b'], 'L0_xcond_f2_w': _L0_xcond_in['f2_w'], 'L0_xcond_f2_b': _L0_xcond_in['f2_b'], 'L0_ffn_ln_gamma': _L0_ffn_in['ln_gamma'], 'L0_ffn_ln_beta': _L0_ffn_in['ln_beta'], 'L0_ffn_gate_w': _L0_ffn_in['gate_w'], 'L0_ffn_w1': _L0_ffn_in['w1'], 'L0_ffn_w2': _L0_ffn_in['w2'], 'L1_xcond_W_att': _L1_xcond_in['W_att'], 'L1_xcond_V_att': _L1_xcond_in['V_att'], 'L1_xcond_Wi': _L1_xcond_in['Wi'], 'L1_xcond_Uh': _L1_xcond_in['Uh'], 'L1_xcond_b': _L1_xcond_in['b'], 'L1_ffn_gate_w': _L1_ffn_in['gate_w'], 'L1_ffn_sh_gate': _L1_ffn_in['sh_gate'], 'L1_ffn_sh_up': _L1_ffn_in['sh_up'], 'L1_ffn_sh_down': _L1_ffn_in['sh_down'], 'L1_ffn_rt_gate': _L1_ffn_in['rt_gate'], 'L1_ffn_rt_up': _L1_ffn_in['rt_up'], 'L1_ffn_rt_down': _L1_ffn_in['rt_down']}

def reference(x, cond_1024, ctx_1024, mask_BxS_bf0, mask_BxS2_bf0, L0_xcond_n1_w, L0_xcond_n1_b, L0_xcond_n2_w, L0_xcond_n2_b, L0_xcond_n3_w, L0_xcond_n3_b, L0_xcond_qkv_w, L0_xcond_so_w, L0_xcond_cq_w, L0_xcond_ck_w, L0_xcond_cv_w, L0_xcond_co_w, L0_xcond_f1_w, L0_xcond_f1_b, L0_xcond_f2_w, L0_xcond_f2_b, L0_ffn_ln_gamma, L0_ffn_ln_beta, L0_ffn_gate_w, L0_ffn_w1, L0_ffn_w2, L1_xcond_W_att, L1_xcond_V_att, L1_xcond_Wi, L1_xcond_Uh, L1_xcond_b, L1_ffn_gate_w, L1_ffn_sh_gate, L1_ffn_sh_up, L1_ffn_sh_down, L1_ffn_rt_gate, L1_ffn_rt_up, L1_ffn_rt_down):
    import jax
    import jax.numpy as jnp

    def _L0_xcond_ref(x, noise_emb, context, src_mask, ctx_mask, n1_w, n1_b, n2_w, n2_b, n3_w, n3_b, qkv_w, so_w, cq_w, ck_w, cv_w, co_w, f1_w, f1_b, f2_w, f2_b):
        import jax, jax.numpy as jnp
        import numpy as np
        NL, D, H, DFF = (6, 128, 16, 512)
        HD = D // H

        def _rope(x):
            L = x.shape[1]
            half = HD // 2
            inv = 1.0 / 10000.0 ** (jnp.arange(half, dtype=jnp.float32) / half)
            ang = jnp.arange(L, dtype=jnp.float32)[:, None] * inv
            cos = jnp.cos(ang)[None, :, None, :]
            sin = jnp.sin(ang)[None, :, None, :]
            x1, x2 = (x[..., :half], x[..., half:])
            return jnp.concatenate([x1 * cos - x2 * sin, x1 * sin + x2 * cos], axis=-1)

        def _ln(x, eps=1e-05):
            m = jnp.mean(x, axis=-1, keepdims=True)
            v = jnp.var(x, axis=-1, keepdims=True)
            return (x - m) * jax.lax.rsqrt(v + eps)

        def _adaln(x, emb, w, b):
            gb = emb[:, 0, :] @ w.T + b
            g, be = jnp.split(gb, 2, axis=-1)
            return _ln(x) * (1.0 + g[:, None, :]) + be[:, None, :]

        def _attn(q, k, v, mask):
            scores = jnp.einsum('bqhd,bkhd->bhqk', q, k) / np.float32(np.sqrt(HD))
            scores = jnp.where(mask[:, None, None, :], jnp.float32(-jnp.inf), scores)
            w = jax.nn.softmax(scores, axis=-1)
            return jnp.einsum('bhqk,bkhd->bqhd', w, v)
        B, L, _ = x.shape
        LC = context.shape[1]
        for i in range(NL):
            xn = _adaln(x, noise_emb, n1_w[i], n1_b[i])
            qkv = xn @ qkv_w[i].T
            q, k, v = jnp.split(qkv, 3, axis=-1)
            q = _rope(q.reshape(B, L, H, HD))
            k = _rope(k.reshape(B, L, H, HD))
            v = v.reshape(B, L, H, HD)
            a = _attn(q, k, v, src_mask).reshape(B, L, D) @ so_w[i].T
            x = x + a
            xn = _adaln(x, noise_emb, n2_w[i], n2_b[i])
            q = _rope((xn @ cq_w[i].T).reshape(B, L, H, HD))
            k = _rope((context @ ck_w[i].T).reshape(B, LC, H, HD))
            v = (context @ cv_w[i].T).reshape(B, LC, H, HD)
            a = _attn(q, k, v, ctx_mask).reshape(B, L, D) @ co_w[i].T
            x = x + a
            xn = _adaln(x, noise_emb, n3_w[i], n3_b[i])
            h = jax.nn.gelu(xn @ f1_w[i].T + f1_b[i], approximate=False)
            x = x + (h @ f2_w[i].T + f2_b[i])
        return x

    def _L0_ffn_ref(x, ln_gamma, ln_beta, gate_w, w1, w2):
        import jax, jax.numpy as jnp
        import numpy as np
        E = 8
        K = 2
        C = 128
        F = 256
        EPS = 1e-05
        B, T, Cc = x.shape
        xf = x.reshape(-1, Cc)
        mu = jnp.mean(xf, axis=-1, keepdims=True)
        var = jnp.var(xf, axis=-1, keepdims=True)
        rn = (xf - mu) * jax.lax.rsqrt(var + EPS) * ln_gamma + ln_beta
        logits = rn @ gate_w.T
        probs = jax.nn.softmax(logits, axis=-1)
        rw, sel = jax.lax.top_k(probs, K)
        comb = jnp.sum(jax.nn.one_hot(sel, E, dtype=xf.dtype) * rw[..., None], axis=1)
        h = jax.nn.gelu(jnp.einsum('nc,efc->enf', xf, w1), approximate=False)
        y = jnp.einsum('enf,ecf->enc', h, w2)
        out = jnp.einsum('enc,ne->nc', y, comb)
        return out.reshape(B, T, Cc)

    def _L1_xcond_ref(dec_seq, enc_hiddens, last_hidden, W_att, V_att, Wi, Uh, b):
        import jax, jax.numpy as jnp
        import numpy as np
        B, T, S, H, E = (128, 32, 32, 128, 128)
        Bn, Sn, Hn = enc_hiddens.shape

        def step(h, x_t):
            hid = jnp.broadcast_to(h[:, None, :], (Bn, Sn, Hn))
            combined = jnp.concatenate([hid, enc_hiddens], axis=2)
            score = jnp.tanh(jnp.einsum('bsk,kh->bsh', combined, W_att))
            score = jnp.einsum('bsh,h->bs', score, V_att[:, 0])
            attn = jax.nn.softmax(score, axis=-1)
            context = jnp.einsum('bs,bsh->bh', attn, enc_hiddens)
            inp = jnp.concatenate([x_t, context], axis=1)
            gz, gr, gh = jnp.split(inp @ Wi + b, 3, axis=1)
            rz, rr, rh = jnp.split(h @ Uh, 3, axis=1)
            z = jax.nn.sigmoid(gz + rz)
            r = jax.nn.sigmoid(gr + rr)
            hh = jnp.tanh(gh + r * rh)
            h_new = z * h + (1.0 - z) * hh
            return (h_new, h_new)
        _, outs = jax.lax.scan(step, last_hidden, jnp.swapaxes(dec_seq, 0, 1))
        return jnp.swapaxes(outs, 0, 1)

    def _L1_ffn_ref(hidden_states, gate_w, sh_gate, sh_up, sh_down, rt_gate, rt_up, rt_down):
        import jax, jax.numpy as jnp
        import numpy as np
        H = 128
        I = 256
        E = 8
        B, S = (2, 128)

        def _swiglu(x, wg, wu, wd):
            return jax.nn.silu(x @ wg) * (x @ wu) @ wd
        b, s, h = hidden_states.shape
        x = hidden_states.reshape(-1, h)
        logits = x @ gate_w
        top_val = jnp.max(logits, axis=-1, keepdims=True)
        top_id = jnp.argmax(logits, axis=-1)
        score = jax.nn.sigmoid(top_val)
        xs = x * score
        g = jnp.einsum('th,ehi->eti', xs, rt_gate)
        u = jnp.einsum('th,ehi->eti', xs, rt_up)
        act = jax.nn.silu(g) * u
        y = jnp.einsum('eti,eih->eth', act, rt_down)
        onehot = jax.nn.one_hot(top_id, E, dtype=x.dtype)
        routed = jnp.einsum('eth,te->th', y, onehot)
        shared = _swiglu(x, sh_gate, sh_up, sh_down)
        return (shared + routed).reshape(b, s, h)
    x = x + _L0_xcond_ref(_layernorm(x, axis=-1), cond_1024[:, None, :], ctx_1024, mask_BxS_bf0, mask_BxS2_bf0, L0_xcond_n1_w, L0_xcond_n1_b, L0_xcond_n2_w, L0_xcond_n2_b, L0_xcond_n3_w, L0_xcond_n3_b, L0_xcond_qkv_w, L0_xcond_so_w, L0_xcond_cq_w, L0_xcond_ck_w, L0_xcond_cv_w, L0_xcond_co_w, L0_xcond_f1_w, L0_xcond_f1_b, L0_xcond_f2_w, L0_xcond_f2_b)
    x = x + _L0_ffn_ref(_layernorm(x, axis=-1), L0_ffn_ln_gamma, L0_ffn_ln_beta, L0_ffn_gate_w, L0_ffn_w1, L0_ffn_w2)
    x = x + _L1_xcond_ref(_layernorm(x, axis=-1), ctx_1024, cond_1024, L1_xcond_W_att, L1_xcond_V_att, L1_xcond_Wi, L1_xcond_Uh, L1_xcond_b)
    x = x + _L1_ffn_ref(_layernorm(x, axis=-1), L1_ffn_gate_w, L1_ffn_sh_gate, L1_ffn_sh_up, L1_ffn_sh_down, L1_ffn_rt_gate, L1_ffn_rt_up, L1_ffn_rt_down)
    return x

_drawn_inputs = setup_inputs


def setup_inputs(seed=0):
    import zlib

    import numpy as np

    out = dict(_drawn_inputs(seed))
    spreads = {'L0_xcond_n1_b': (0.0, 0.379),
     'L0_xcond_n2_b': (0.0, 0.8),
     'L0_xcond_n3_b': (0.0, 0.333),
     'L0_xcond_f1_b': (0.0, 0.1),
     'L0_xcond_f2_b': (0.0, 0.1),
     'L1_xcond_b': (0.0, 0.1)}
    factors = {'L0_xcond_n2_w': 8.0,
     'L0_xcond_cq_w': 8.0,
     'L0_xcond_ck_w': 8.0,
     'L0_ffn_ln_gamma': 77.821,
     'L0_ffn_ln_beta': 60.641}
    for name, (base, spread) in spreads.items():
        noise = np.random.default_rng([zlib.crc32(name.encode()), seed]).standard_normal(out[name].shape)
        drawn = base * np.exp(spread * noise) if base else spread * noise
        out[name] = jnp.asarray(drawn.astype(out[name].dtype))
    for name, factor in factors.items():
        out[name] = (out[name] * factor).astype(out[name].dtype)
    return out
```

```python
from contextlib import ExitStack

import numpy as np
import concourse.bass as bass
from concourse import mybir

FP32 = mybir.dt.float32
BF16 = mybir.dt.bfloat16
ALU = mybir.AluOpType
ACT = mybir.ActivationFunctionType
AX = mybir.AxisListType

P = 128
B, S, S2, D = 2, 512, 154, 128
NL, H, HD = 6, 16, 8
DFF = 512
NE, FE = 8, 256
EPS = 1e-5
NT = B * S // P
TB = S // P
TAIL = 32
SC = P + TAIL
NEG = -1.0e30
ONES = float(np.array([0x3F803F80], np.uint32).view(np.float32)[0])
SCALE = 1.0 / float(np.sqrt(np.float32(HD)))

Q_PART = [0, 1, 2, 0, 1, 0]
K_PART = [0, 0, 0, 1, 1, 2]
NSLOT = len(Q_PART)
MASK_ROW = NSLOT * HD
MAX_ROW = MASK_ROW + 1
ROWS1 = MASK_ROW + 1
ROWS2 = MAX_ROW + 2

WQ, WQR, WK, WKR, WV, WO, CQ, CQR, CK, CKR, CV, CO = range(12)

LEAD = 6
UH = 4
NU = B * H // UH
NPT = 3
U = 32

LN_L, XN_L, TP_L = 3, 3 * NT, 3 * B
PARTS_L = 5
ITEMS = [(0, "k", 0), (1, "q", 0), (1, "k", 0), (2, "q", 1), (2, "k", 1), (3, "q", 0), (4, "q", 1)]
ITEM_L = len(ITEMS)
RD_L, RD_AT = 7, [1, 3, 5, 6, 7]
S1_L = B * H * TB + B * H * 2
S2_L = B * H * TB + B * H + NU
V_L, VR_L, UNIT_L = 4, 7, 2 * NU
PV_L = B * H + NU
DVE_L = 35


def build(nc, x_d, cond_d, ctx_d, mask_d, mask2_d, rot_d, ident_d, rev_d, nw_d, nb_d, wa_d, wf_d, f1b_d, f2b_d,
          gb_d, mg_d, w1_d, w2_d, watt_d, vatt_d, wi_d, uh_d, sb_d, rgate_d, eg_d, eu_d, ed_d, out_d):
    ctx = ExitStack()
    with ctx:
        def sb(name, shape, dt=FP32):
            return ctx.enter_context(nc.sbuf_tensor(name, shape, dt))

        def sem(name):
            return ctx.enter_context(nc.semaphore(name))

        bank = [ctx.enter_context(nc.psum_tensor(f"bank{i}", [P, 512], FP32)) for i in range(8)]
        scratch = nc.dram_tensor("stack_scratch", (2, NSLOT, P, 2, S), BF16, kind="Internal").ap()

        ident = sb("ident", [P, P])
        rot = sb("rot", [P, 2, S])
        rev = sb("rev", [P, NT, NE])
        half = sb("half", [P, NT])
        XI = sb("XI", [P, NT, D])
        Y = sb("Y", [P, NT, D])
        XN = sb("XN", [P, NT, D])
        XT = sb("XT", [P, B * S])
        condT = sb("condT", [P, B])
        ctxT = sb("ctxT", [P, B, SC])
        stats = sb("stats", [P, NT, 6])
        mv = sb("mv", [P, NT, 2])
        vpe = sb("vpe", [P, NT])
        rstd = sb("rstd", [P, NT])
        stacks = sb("stacks", [P, 2, H * B * S // 2])
        share = sb("share", [P, 3 * NL * 2 * D])
        NW = share[:, :].rearrange("p (n k) -> p n k", k=2 * D)
        NB = sb("NB", [P, 3 * NL, 2])
        AD = sb("AD", [P, NL, 3, 2, B])
        ADL = sb("ADL", [P, 3, 2, B])
        WA = sb("WA", [P, 12 * D])
        WF = sb("WF", [P, 2 * DFF])
        F1B = sb("F1B", [P, 4])
        F2B = sb("F2B", [P, D])
        QS = stacks[0:ROWS2, 0, :].bitcast(BF16).rearrange("p (b h t) -> p b h t", b=B, h=H)
        KS = stacks[0:ROWS2, 1, :].bitcast(BF16).rearrange("p (b h t) -> p b h t", b=B, h=H)
        cstack = sb("cstack", [P, H * B * SC // 2])
        KC = cstack[0:ROWS2, :].bitcast(BF16).rearrange("p (h t) -> p h t", h=H)
        parts = sb("parts", [P, 2, 2, 3, S], BF16)
        work = sb("work", [P, 9 * S])
        rA, rB, rF = [work[:, 3 * S * i:3 * S * (i + 1)].rearrange("p (r t) -> p r t", r=3) for i in range(3)]
        VP = sb("VP", [P, NT, H, HD + 1])
        VC = sb("VC", [P, B, H, HD + 1])
        VT = sb("VT", [P, B, H // UH, UH, HD + 1])
        nmax = sb("nmax", [P, 2, UH * TB])
        mrow = sb("mrow", [UH * TB, 2, 2, P], BF16)
        ring = sb("ring", [P, NPT * TB * S])
        PT = ring[:, :].rearrange("p (n k q) -> p n k q", n=NPT, k=TB)
        PTT = sb("PTT", [P, 2, S])
        mask_row = PTT[0:1, :, :].rearrange("p a n -> p (a n)").bitcast(BF16)[:, 0:B * S + B * SC]
        mask_words = XN[0:1, :, :].rearrange("p a n -> p (a n)").bitcast(mybir.dt.int32)[:, 0:(B * S + B * S2) // 4]
        mask_raw = mask_words.bitcast(mybir.dt.uint8)
        orec = sb("orec", [P, 2, UH, TB])
        att = sb("att", [P, NT, D])
        attT = XT
        HL = share[:, 0:4 * B * S].rearrange("p (n t) -> p n t", t=S)
        H0 = stacks[:, :, :].rearrange("p a n -> p (a n)").rearrange("p (n t) -> p n t", t=S)
        HT = stacks[:, :, :].rearrange("p a n -> p (a n)")[:, 0:(2 * NE + 2) * S].rearrange("p (n t) -> p n t", t=S)
        RT = att[:, :, :].rearrange("p t d -> p (t d)")
        sg = PTT
        gb = sb("gb", [P, 2])
        mg = sb("mg", [P, 2, NE])
        EWA = ring[:, 0:(NE + 1) * FE].rearrange("p (e f) -> p e f", f=FE)
        EWB = ring[:, (NE + 1) * FE:2 * (NE + 1) * FE].rearrange("p (e f) -> p e f", f=FE)
        EWD = cstack[:, 0:2 * (NE + 1) * D].rearrange("p (n d) -> p n d", d=D)
        lg = sb("lg", [P, 10, NT, NE])
        small = sb("small", [P, 8, NT])
        watt = sb("watt", [P, 2, D])
        vatt = sb("vatt", [P, 1])
        vrep = sb("vrep", [P, P])
        wi = sb("wi", [P, 2, 3 * D])
        uh = sb("uh", [P, 3 * D])
        sbias = sb("sbias", [P, 3])
        KB = B * S2
        EP = work[:, 0:KB].rearrange("p (b s) -> p b s", b=B)
        th = work[:, KB:2 * KB].rearrange("p (b s) -> p b s", b=B)
        ex = work[:, 2 * KB:3 * KB].rearrange("p (b s) -> p b s", b=B)
        EW = work[:, 3 * KB:6 * KB].rearrange("p (b g s) -> p b g s", b=B, g=3)
        prod = work[:, 6 * KB:9 * KB].rearrange("p (g b s) -> p g b s", b=B, g=3)
        GX = share[:, 0:(S + U) * 4 * B].rearrange("p (t g b) -> p t g b", g=4, b=B)
        GS = sb("GS", [P, U, 4, B])
        HR = sb("HR", [P, U, B])
        HO = att[:, :, :].rearrange("p (b t) d -> p b (t d)", b=B)
        ub = sb("ub", [P, B])
        nm = sb("nm", [P, B])
        esum = sb("esum", [P, B])
        erec = sb("erec", [P, B])
        hb = sb("hb", [P, 4, B])
        gr = sb("gr", [P, 3, B])
        hhalf = sb("hhalf", [P, B])
        tr = sb("tr", [P, B])
        tz = sb("tz", [P, B])
        qq = sb("qq", [P, B])
        ca = sb("ca", [P, B])
        pre = sb("pre", [P, B])
        cand = sb("cand", [P, B])
        omz = sb("omz", [P, B])
        zt = sb("zt", [P, B])
        zh = sb("zh", [P, B])
        hz = sb("hz", [P, B])

        small_in = sem("small_in")
        scan_in = sem("scan_in")
        expert_in = sem("expert_in")
        expert2_in = sem("expert2_in")
        wa_in, wf_in = sem("wa_in"), sem("wf_in")
        const_ready, stack_ones = sem("const_ready"), sem("stack_ones")
        mask_ready, mask_dma = sem("mask_ready"), sem("mask_dma")
        ad_ps, ad_ready, adl_ready = sem("ad_ps"), sem("ad_ready"), sem("adl_ready")
        dve_step = sem("dve_step")
        pool_step = sem("pool_step")
        ln_st, ln_rs, ln_xn = sem("ln_st"), sem("ln_rs"), sem("ln_xn")
        tp_ps, xt_ready = sem("tp_ps"), sem("xt_ready")
        qk_ps, rot_done, hi_done, r1_done, mid_done, lo_done = [
            sem(n) for n in ("qk_ps", "rot_done", "hi_done", "r1_done", "mid_done", "lo_done")]
        stack_wr, stack_rd = sem("stack_wr"), sem("stack_rd")
        v_ps, v_ready = sem("v_ps"), sem("v_ready")
        s1_ps, s1_max, m_ps, m_ready, m_dma = [sem(n) for n in ("s1_ps", "s1_max", "m_ps", "m_ready", "m_dma")]
        s2_ps, s2_exp, pv_done, att_ready = [sem(n) for n in ("s2_ps", "s2_exp", "pv_done", "att_ready")]
        at_ps, at_ready, pr_ps, x_ready = [sem(n) for n in ("at_ps", "at_ready", "pr_ps", "x_ready")]
        f1_ps, h_ready, f2_ps = [sem(n) for n in ("f1_ps", "h_ready", "f2_ps")]
        layer_done = sem("layer_done")
        out_done, x_done = sem("out_done"), sem("x_done")
        rt_ready, rt_step, rt_exp, lg_ps = [sem(n) for n in ("rt_ready", "rt_step", "rt_exp", "lg_ps")]
        up_ps, up_ready, hid_ready, down_ps, weighed = [sem(n) for n in ("up_ps", "up_ready", "hid_ready", "down_ps", "weighed")]
        ep_ps, ep_ready, gx_ps, gx_ready, gx_zero, gs_ready, ho_ready, ho_ps = [
            sem(n) for n in ("ep_ps", "ep_ready", "gx_ps", "gx_ready", "gx_zero", "gs_ready", "ho_ready", "ho_ps")]
        u_ps, u_ready, h_new, gate_ps, hb_ready = [sem(n) for n in ("u_ps", "u_ready", "h_new", "gate_ps", "hb_ready")]
        th_ready, score_ps, max_ready, ex_ready = [[sem(f"{n}{b}") for b in range(B)]
                                                   for n in ("th_ready", "score_ps", "max_ready", "ex_ready")]
        dot_ready = [sem(f"dot_ready{g}") for g in range(3)]
        erec_ready, r_scaled, r_pre, r_ready, z_scaled, z_pre, z_ready = [
            sem(n) for n in ("erec_ready", "r_scaled", "r_pre", "r_ready", "z_scaled", "z_pre", "z_ready")]
        hh_ready, q_ready, ca_ready, c_pre, c_ready, zt_ready, omz_ready, zh_ready, hz_ready = [
            sem(n) for n in ("hh_ready", "q_ready", "ca_ready", "c_pre", "c_ready", "zt_ready", "omz_ready", "zh_ready", "hz_ready")]
        apart_dve, apart_pe, apart_sp = sem("apart_dve"), sem("apart_pe"), sem("apart_sp")

        block = ctx.enter_context(nc.Block())
        NSMALL = 10

        def wcol(k):
            return WA[:, k * D:(k + 1) * D]

        LN0, XN0, TP0 = 1 + NL * LN_L, NT * (1 + NL * LN_L), NL * TP_L
        N0 = 2 * NE
        N1 = 2 * (NE + 1)

        def post_gpsimd(g, inverse_root):
            inverse_root(LN0 + 1)
            inverse_root(LN0 + 2)
            nc.gpsimd.memset(GX[:, :, 3, :], 0.0)
            nc.gpsimd.memset(GX[:, S:S + U, 0:3, :], 0.0).then_inc(gx_zero, 1)
            inverse_root(LN0 + 3)
            g.wait_ge(gx_ready, 3 * B)
            g.wait_ge(gx_zero, 1)
            nc.gpsimd.tensor_copy(GS[:, :, :, :], GX[:, 0:U, :, :]).then_inc(gs_ready, 2)
            half_u = U // 2
            with g.Fori(0, S // U) as blk:
                for k in range(2):
                    g.wait_ge(h_new, blk * U + (k + 1) * half_u + 1)
                    nc.gpsimd.tensor_copy(HO[:, :, bass.ds(blk * U + k * half_u, half_u)],
                                          HR[:, k * half_u:(k + 1) * half_u, :].rearrange("p u b -> p b u")).then_inc(ho_ready, 1)
                    g.wait_ge(hb_ready, blk * U + (k + 1) * half_u)
                    nc.gpsimd.tensor_copy(GS[:, k * half_u:(k + 1) * half_u, :, :],
                                          GX[:, bass.ds(blk * U + (U + k * half_u), half_u), :, :]).then_inc(gs_ready, 1)
            inverse_root(LN0 + 4)

        def post_scalar(act, turned):
            turned(TP0)
            for b in range(B):
                act.wait_ge(tp_ps, TP0 + B + b + 1)
                nc.scalar.activation(RT[:, b * S:(b + 1) * S], bank[b][:, :], ACT.Identity, scale=gb[:, 0:1],
                                     bias=gb[:, 1:2]).then_inc(rt_ready, 1)
            act.wait_ge(rt_step, 1)
            nc.scalar.activation(lg[:, 2, :, :], lg[:, 1, :, :], ACT.Exp).then_inc(rt_exp, 1)
            for n in range(B * N0):
                act.wait_ge(up_ps, n + 1)
                nc.scalar.activation(H0[:, n, :], bank[2 + n % 4][:, :], ACT.Gelu).then_inc(up_ready, 1)
            turned(TP0 + 2 * B)
            act.wait_ge(ep_ps, 1)
            nc.scalar.copy(EP, bank[0][:, 0:B * S2].rearrange("p (b s) -> p b s", b=B)).then_inc(ep_ready, 1)
            for b in range(B):
                nc.scalar.copy(EW[:, b, :, :], bank[1 + 6 * b][:, 0:3 * S2].rearrange("p (g s) -> p g s", g=3)).then_inc(ep_ready, 1)
            for n in range(3 * B):
                b, gate = n // 3, n % 3
                act.wait_ge(gx_ps, n + 1)
                nc.scalar.activation(GX[:, 0:S, gate, b], bank[2 + n % 5][:, :], ACT.Identity,
                                     bias=sbias[:, gate:gate + 1]).then_inc(gx_ready, 1)
            with act.Fori(0, S // U) as blk:
                for k in range(U):
                    n = blk * U + (k + 1)
                    act.wait_ge(u_ready, n)
                    for b in range(B):
                        nc.scalar.activation(th[:, b, :], EP[:, b, :], ACT.Tanh, bias=ub[:, b:b + 1]).then_inc(th_ready[b], 1)
                    for b in range(B):
                        act.wait_ge(max_ready[b], n)
                        nc.scalar.activation(ex[:, b, :], bank[b][:, 0:S2], ACT.Exp, bias=nm[:, b:b + 1],
                                             accum_out=esum[:, b:b + 1]).then_inc(ex_ready[b], 1)
                    act.wait_ge(r_pre, n)
                    nc.scalar.activation(tr[:, :], gr[:, 1, :], ACT.Tanh).then_inc(r_ready, 1)
                    act.wait_ge(z_pre, n)
                    nc.scalar.activation(tz[:, :], gr[:, 0, :], ACT.Tanh).then_inc(z_ready, 1)
                    act.wait_ge(c_pre, n)
                    nc.scalar.activation(cand[:, :], pre[:, :], ACT.Tanh).then_inc(c_ready, 1)
            turned(TP0 + 3 * B)
            act.wait_ge(rt_step, 2)
            nc.scalar.activation(small[:, 1, :], small[:, 0, :], ACT.Tanh, scale=0.5).then_inc(rt_exp, 1)
            for b in range(B):
                act.wait_ge(tp_ps, TP0 + 4 * B + b + 1)
                nc.scalar.copy(RT[:, b * S:(b + 1) * S], bank[b][:, :]).then_inc(rt_ready, 1)
            for n in range(B * N1):
                act.wait_ge(up_ps, B * N0 + n + 1)
                if n >= 2:
                    act.wait_ge(hid_ready, n - 1)
                nc.scalar.activation(sg[:, n % 2, :], bank[2 + 2 * (n % 2)][:, :], ACT.Silu).then_inc(up_ready, 1)

        def post_vector(v, link, run_norm):
            V = nc.vector

            def wide(a):
                return a.unsqueeze(2).to_broadcast([P, NT, NE])

            def greatest(src, dst):
                link(V.tensor_reduce(dst, src, AX.X, ALU.max))

            def first_greatest(p, best, eq, at, hot):
                greatest(p, best)
                link(V.tensor_tensor(eq, p, wide(best), ALU.is_equal))
                link(V.tensor_tensor(eq, eq, rev[:, :, :], ALU.mult))
                greatest(eq, at)
                link(V.tensor_tensor(hot, eq, wide(at), ALU.is_equal))

            def weigh(n_experts, comb, done):
                groups = -(-n_experts // 4)
                for j in range(NT):
                    for q in range(groups):
                        v.wait_ge(down_ps, done + j * groups + q + 1)
                        for e in range(4 * q, min(4 * q + 4, n_experts)):
                            src = bank[6 + (j * groups + q) % 2][:, (e % 4) * D:(e % 4 + 1) * D]
                            if e < NE:
                                ins = V.scalar_tensor_tensor(out=XI[:, j, :], in0=src, scalar=comb[:, j, e:e + 1],
                                                             in1=XI[:, j, :], op0=ALU.mult, op1=ALU.add)
                            else:
                                ins = V.tensor_tensor(XI[:, j, :], XI[:, j, :], src, ALU.add)
                            link(ins)
                        v.sem_inc(weighed, 1)

            link(V.tensor_tensor(XI[:, :, :], XI[:, :, :], Y[:, :, :], ALU.add))
            run_norm(XI, Y, LN0 + 1)
            v.wait_ge(ln_xn, XN0 + NT)
            run_norm(Y, XN, LN0 + 2)
            v.wait_ge(lg_ps, 1)
            link(V.tensor_copy(lg[:, 0, :, :], bank[7][:, 0:NT * NE].rearrange("p (j e) -> p j e", e=NE)))
            greatest(lg[:, 0, :, :], small[:, 0, :])
            V.tensor_tensor(lg[:, 1, :, :], lg[:, 0, :, :], wide(small[:, 0, :]), ALU.subtract).then_inc(rt_step, 1)
            v.wait_ge(rt_exp, 1)
            link(V.tensor_reduce(small[:, 1, :], lg[:, 2, :, :], AX.X, ALU.add))
            link(V.reciprocal(small[:, 2, :], small[:, 1, :]))
            link(V.tensor_tensor(lg[:, 3, :, :], lg[:, 2, :, :], wide(small[:, 2, :]), ALU.mult))
            first_greatest(lg[:, 3, :, :], small[:, 3, :], lg[:, 4, :, :], small[:, 4, :], lg[:, 5, :, :])
            link(V.scalar_tensor_tensor(out=lg[:, 6, :, :], in0=lg[:, 5, :, :], scalar=-2.0, in1=lg[:, 3, :, :],
                                        op0=ALU.mult, op1=ALU.add))
            first_greatest(lg[:, 6, :, :], small[:, 5, :], lg[:, 7, :, :], small[:, 6, :], lg[:, 8, :, :])
            link(V.tensor_tensor(lg[:, 5, :, :], lg[:, 5, :, :], lg[:, 8, :, :], ALU.add))
            link(V.tensor_tensor(lg[:, 9, :, :], lg[:, 5, :, :], lg[:, 3, :, :], ALU.mult))
            v.wait_ge(scan_in, 16 * 7)
            V.tensor_copy(vrep[:, :], vatt[:, 0:1].to_broadcast([P, P]))
            V.tensor_scalar(uh[:, :], uh[:, :], 0.5, None, ALU.mult)
            V.tensor_scalar(wi[:, :, 0:2 * D], wi[:, :, 0:2 * D], 0.5, None, ALU.mult)
            V.tensor_scalar(sbias[:, 0:2], sbias[:, 0:2], 0.5, None, ALU.mult)
            V.tensor_copy(HR[:, U - 1, :], condT[:, :]).then_inc(h_new, 1)
            weigh(NE, lg[:, 9, :, :], 0)
            run_norm(XI, XN, LN0 + 3)
            scan_vector(v)
            for b in range(B):
                v.wait_ge(ho_ps, b + 1)
                x = XI[:, TB * b:TB * (b + 1), :]
                link(V.tensor_tensor(x, x, bank[b][:, :].rearrange("p (t d) -> p t d", t=TB), ALU.add))
            run_norm(XI, XN, LN0 + 4)
            v.wait_ge(lg_ps, 2)
            link(V.tensor_copy(lg[:, 0, :, :], bank[7][:, 0:NT * NE].rearrange("p (j e) -> p j e", e=NE)))
            first_greatest(lg[:, 0, :, :], small[:, 0, :], lg[:, 1, :, :], small[:, 2, :], lg[:, 9, :, :])
            v.sem_inc(rt_step, 1)
            v.wait_ge(rt_exp, 2)
            link(V.tensor_scalar(small[:, 3, :], small[:, 1, :], 0.5, 0.5, ALU.mult, ALU.add))
            for j in range(NT):
                V.tensor_scalar(Y[:, j, :], XN[:, j, :], small[:, 3, j:j + 1], None, ALU.mult).then_inc(ln_xn, 1)
            for b in range(B):
                for n in range(b * N1, (b + 1) * N1):
                    v.wait_ge(up_ready, B * N0 + n + 1)
                    if n == N1:
                        v.wait_ge(down_ps, 2 * NT + 3 * TB)
                    V.tensor_tensor(HT[:, n % N1, :], sg[:, n % 2, :], bank[3 + 2 * (n % 2)][:, :], ALU.mult).then_inc(hid_ready, 1)
                for j in range(TB * b, TB * (b + 1)):
                    for q in range(3):
                        v.wait_ge(down_ps, 2 * NT + j * 3 + q + 1)
                        for e in range(4 * q, min(4 * q + 4, NE + 1)):
                            src = bank[6 + (j * 3 + q) % 2][:, (e % 4) * D:(e % 4 + 1) * D]
                            if e < NE:
                                ins = V.scalar_tensor_tensor(out=XI[:, j, :], in0=src, scalar=lg[:, 9, j, e:e + 1],
                                                             in1=XI[:, j, :], op0=ALU.mult, op1=ALU.add)
                            else:
                                ins = V.tensor_tensor(XI[:, j, :], XI[:, j, :], src, ALU.add)
                            link(ins)
                        v.sem_inc(weighed, 1)
                v.sem_inc(x_done, 1)

        def scan_vector(v):
            V, TT = nc.vector, nc.vector.tensor_tensor
            half_u = U // 2
            v.wait_ge(ep_ready, 3)
            with v.Fori(0, S // U) as blk:
                for k in range(U):
                    n = blk * U + (k + 1)
                    before = HR[:, (k - 1) % U, :]

                    def dot(gate, b, scale):
                        V.scalar_tensor_tensor(out=prod[:, gate, b, :], in0=ex[:, b, :], scalar=scale, in1=EW[:, b, gate, :],
                                               op0=ALU.mult, op1=ALU.mult, accum_out=gr[:, gate, b:b + 1]).then_inc(dot_ready[gate], 1)

                    v.wait_ge(u_ps, n)
                    V.tensor_copy(ub[:, :], bank[3][:, 0:B]).then_inc(u_ready, 1)
                    v.wait_ge(h_new, n)
                    V.tensor_scalar(hhalf[:, :], before, 0.5, None, ALU.mult).then_inc(hh_ready, 1)
                    for b in range(B):
                        v.wait_ge(score_ps[b], n)
                        V.tensor_reduce(nm[:, b:b + 1], bank[b][:, 0:S2], AX.X, ALU.max, negate=True).then_inc(max_ready[b], 1)
                    v.wait_ge(ex_ready[0], n)
                    dot(1, 0, 1.0)
                    dot(0, 0, 1.0)
                    v.wait_ge(gate_ps, n)
                    if k % half_u == 0:
                        v.wait_ge(gs_ready, blk * 2 + (k // half_u + 1))
                    TT(hb[:, :, :], bank[2][:, 0:4 * B].rearrange("p (g b) -> p g b", b=B), GS[:, k, :, :], ALU.add).then_inc(hb_ready, 1)
                    v.wait_ge(ex_ready[1], n)
                    dot(1, 1, 1.0)
                    V.reciprocal(erec[:, :], esum[:, :]).then_inc(erec_ready, 1)
                    dot(0, 1, 1.0)
                    v.wait_ge(erec_ready, n)
                    v.wait_ge(dot_ready[1], n * 2)
                    TT(gr[:, 1, :], gr[:, 1, :], erec[:, :], ALU.mult).then_inc(r_scaled, 1)
                    dot(2, 0, erec[:, 0:1])
                    v.wait_ge(r_scaled, n)
                    v.wait_ge(hb_ready, n)
                    TT(gr[:, 1, :], gr[:, 1, :], hb[:, 1, :], ALU.add).then_inc(r_pre, 1)
                    v.wait_ge(dot_ready[0], n * 2)
                    TT(gr[:, 0, :], gr[:, 0, :], erec[:, :], ALU.mult).then_inc(z_scaled, 1)
                    dot(2, 1, erec[:, 1:2])
                    v.wait_ge(z_scaled, n)
                    TT(gr[:, 0, :], gr[:, 0, :], hb[:, 0, :], ALU.add).then_inc(z_pre, 1)
                    v.wait_ge(r_ready, n)
                    TT(qq[:, :], tr[:, :], hb[:, 3, :], ALU.mult).then_inc(q_ready, 1)
                    v.wait_ge(dot_ready[2], n * 2)
                    TT(ca[:, :], gr[:, 2, :], hb[:, 2, :], ALU.add).then_inc(ca_ready, 1)
                    v.wait_ge(q_ready, n)
                    v.wait_ge(ca_ready, n)
                    TT(pre[:, :], qq[:, :], ca[:, :], ALU.add).then_inc(c_pre, 1)
                    v.wait_ge(hh_ready, n)
                    v.wait_ge(z_ready, n)
                    TT(zt[:, :], tz[:, :], hhalf[:, :], ALU.mult).then_inc(zt_ready, 1)
                    V.tensor_scalar(omz[:, :], tz[:, :], -0.5, 0.5, ALU.mult, ALU.add).then_inc(omz_ready, 1)
                    v.wait_ge(zt_ready, n)
                    TT(zh[:, :], zt[:, :], hhalf[:, :], ALU.add).then_inc(zh_ready, 1)
                    v.wait_ge(c_ready, n)
                    v.wait_ge(omz_ready, n)
                    TT(hz[:, :], cand[:, :], omz[:, :], ALU.mult).then_inc(hz_ready, 1)
                    if k == half_u:
                        v.wait_ge(ho_ready, blk * 2 + 1)
                    v.wait_ge(hz_ready, n)
                    v.wait_ge(zh_ready, n)
                    TT(HR[:, k, :], hz[:, :], zh[:, :], ALU.add).then_inc(h_new, 1)

        def post_tensor(pe, turn):
            mm = nc.tensor.matmul

            def logits(rt, which):
                for j in range(NT):
                    ins = mm(bank[7][:, j * NE:(j + 1) * NE], rt[:, j * P:(j + 1) * P], mg[:, which, :], start=True, stop=True)
                ins.then_inc(lg_ps, 1)

            def down(b, hidden, n_experts, done):
                groups = -(-n_experts // 4)
                for t in range(TB):
                    for q in range(groups):
                        k = (TB * b + t) * groups + q
                        if k >= 2 or done:
                            pe.wait_ge(weighed, done + k - 1)
                        for e in range(4 * q, min(4 * q + 4, n_experts)):
                            for c in range(2):
                                ins = mm(bank[6 + k % 2][:, (e % 4) * D:(e % 4 + 1) * D], hidden[:, 2 * e + c, t * P:(t + 1) * P],
                                         EWD[:, 2 * e + c, :], start=(c == 0), stop=(c == 1))
                        ins.then_inc(down_ps, 1)

            turn(Y, XN0)
            for b in range(B):
                pe.wait_ge(xt_ready, TP0 + b + 1)
            turn(XN, XN0 + NT)
            pe.wait_ge(rt_ready, B)
            pe.wait_ge(scan_in, 16 * 7)
            logits(RT, 0)
            pe.wait_ge(expert_in, 32)
            for b in range(B):
                for n in range(b * N0, (b + 1) * N0):
                    if n >= 4:
                        pe.wait_ge(up_ready, n - 3)
                    c = n % N0
                    mm(bank[2 + n % 4][:, :], EWA[:, c // 2, (c % 2) * P:(c % 2 + 1) * P], XT[:, b * S:(b + 1) * S],
                       start=True, stop=True).then_inc(up_ps, 1)
            pe.wait_ge(rt_step, 1)
            for b in range(B):
                pe.wait_ge(up_ready, (b + 1) * N0)
                down(b, H0[:, b * N0:(b + 1) * N0, :], NE, 0)
            turn(XN, XN0 + 2 * NT)
            pe.wait_ge(h_new, 1)
            for b in range(B):
                pe.wait_ge(xt_ready, TP0 + B + b + 1)
            for b in range(B):
                mm(bank[0][:, b * S2:(b + 1) * S2], watt[:, 1, :], ctxT[:, b, 0:S2], start=True, stop=True)
            for b in range(B):
                for gate in range(3):
                    ins = mm(bank[1 + 6 * b][:, gate * S2:(gate + 1) * S2], wi[:, 1, gate * D:(gate + 1) * D], ctxT[:, b, 0:S2],
                             start=True, stop=True)
            ins.then_inc(ep_ps, 1)
            for n in range(3 * B):
                b, gate = n // 3, n % 3
                if n >= 5:
                    pe.wait_ge(gx_ready, n - 4)
                mm(bank[2 + n % 5][:, :], wi[:, 0, gate * D:(gate + 1) * D], XT[:, b * S:(b + 1) * S],
                   start=True, stop=True).then_inc(gx_ps, 1)
            pe.wait_ge(ep_ready, 3)
            pe.wait_ge(gx_ready, 3 * B)
            with pe.Fori(0, S // U) as blk:
                for k in range(U):
                    n = blk * U + (k + 1)
                    h = HR[:, (k - 1) % U, :]
                    pe.wait_ge(h_new, n)
                    mm(bank[3][:, 0:B], watt[:, 0, :], h, start=True, stop=True).then_inc(u_ps, 1)
                    mm(bank[2][:, 0:B], uh[:, 0:D], h, start=True, stop=True)
                    for b in range(B):
                        pe.wait_ge(th_ready[b], n)
                        mm(bank[b][:, 0:S2], vrep[:, :], th[:, b, :], start=True, stop=True).then_inc(score_ps[b], 1)
                    mm(bank[2][:, B:2 * B], uh[:, D:2 * D], h, start=True, stop=True)
                    mm(bank[2][:, 2 * B:4 * B], uh[:, 2 * D:3 * D], HR[:, (k - 1) % U:(k - 1) % U + 1, :].to_broadcast([P, 2, B]),
                       start=True, stop=True).then_inc(gate_ps, 1)
            pe.wait_ge(ho_ready, 2 * (S // U))
            for b in range(B):
                for t in range(TB):
                    ins = nc.tensor.transpose(bank[b][:, t * P:(t + 1) * P], HO[:, b, t * P:(t + 1) * P], ident[:, :])
                ins.then_inc(ho_ps, 1)
            turn(XN, XN0 + 3 * NT)
            pe.wait_ge(xt_ready, TP0 + 3 * B)
            logits(XT, 1)
            turn(Y, XN0 + 4 * NT)
            pe.wait_ge(rt_ready, 2 * B)
            pe.wait_ge(rt_step, 2)
            pe.wait_ge(expert_in, 32 + 48)
            for b in range(B):
                for n in range(b * N1, (b + 1) * N1):
                    if n >= 2:
                        pe.wait_ge(hid_ready, n - 1)
                    c = n % N1
                    cols = slice((c % 2) * P, (c % 2 + 1) * P)
                    src = (RT if c < 2 * NE else XT)[:, b * S:(b + 1) * S]
                    mm(bank[2 + 2 * (n % 2)][:, :], EWA[:, c // 2, cols], src, start=True, stop=True)
                    mm(bank[3 + 2 * (n % 2)][:, :], EWB[:, c // 2, cols], src, start=True, stop=True).then_inc(up_ps, 1)
                pe.wait_ge(hid_ready, (b + 1) * N1)
                down(b, HT, NE + 1, 2 * NT)

        @block.sync
        def _(sp):
            for dst, src in ((XI[:, :, :], x_d.rearrange("b (t p) d -> p (b t) d", p=P)),
                             (ident[:, :], ident_d), (condT[:, :], cond_d), (rot[:, :, :], rot_d),
                             (ctxT[:, :, 0:S2], ctx_d.rearrange("b d s -> d b s")),
                             (rev[:, :, :], rev_d), (NW[:, :, :], nw_d), (NB[:, :, :], nb_d),
                             (mask_words[0:1, 0:B * S // 4], mask_d),
                             (mask_words[0:1, B * S // 4:(B * S + B * S2) // 4], mask2_d)):
                sp.dma_start(dst, src).then_inc(small_in, 16)
            sp.wait_ge(mask_ready, 3)
            sp.wait_ge(const_ready, 1)
            sp.wait_ge(stack_ones, 1)
            for h in range(H):
                for b in range(B):
                    sp.dma_start(KS[MASK_ROW:MASK_ROW + 1, b, h, :], mask_row[0:1, b * S:(b + 1) * S]).then_inc(mask_dma, 16)
                sp.dma_start(KC[MASK_ROW:MASK_ROW + 1, h, :], mask_row[0:1, B * S:]).then_inc(mask_dma, 16)
            for dst, src in ((gb[:, :], gb_d), (mg[:, :, :], mg_d), (watt[:, :, :], watt_d), (vatt[:, :], vatt_d),
                             (wi[:, :, :], wi_d), (uh[:, :], uh_d), (sbias[:, :], sb_d)):
                sp.dma_start(dst, src).then_inc(scan_in, 16)

            def stack(l, i, n, kinds):
                j = i % 2
                sp.wait_ge(lo_done, l * ITEM_L + RD_AT[i])
                sp.sem_inc(apart_sp, 1)
                k0 = 0 if kinds[0][0] == "q" else 1
                for s in range(NSLOT):
                    if len(kinds) == 2:
                        src = parts[:, j, :, :, :].rearrange("p k c t -> p (k c) t")
                        step = 3 + K_PART[s] - Q_PART[s]
                        src = src[:, Q_PART[s]:Q_PART[s] + step + 1:step, 0:n]
                        dst = scratch[j, s, :, :, 0:n]
                    else:
                        src = parts[:, j, k0, (Q_PART, K_PART)[k0][s], 0:n]
                        dst = scratch[j, s, :, k0, 0:n]
                    sp.dma_start(dst, src).then_inc(stack_wr, 16)
                sp.wait_ge(stack_wr, (l * PARTS_L + i + 1) * NSLOT * 16)
                sp.sem_inc(apart_sp, 1)
                for kind, dst in kinds:
                    sp.dma_start(dst, scratch[j, :, :, 0 if kind == "q" else 1, 0:n].rearrange(
                        "s (d h) t -> (s d) h t", h=H)).then_inc(stack_rd, 16)
                sp.wait_ge(stack_rd, (l * RD_L + RD_AT[i]) * 16)
                sp.sem_inc(apart_sp, 1)

            def maxima(l, u):
                b, h0 = (u % NU) // (H // UH), UH * (u % (H // UH))
                sp.wait_ge(m_ready, (l * UNIT_L + u + 1) * 2)
                sp.sem_inc(apart_sp, 1)
                for r in range(2):
                    sp.dma_start(QS[MAX_ROW + r:MAX_ROW + r + 1, b, h0:h0 + UH, :].rearrange("p h t -> p (h t)"),
                                 mrow[:, u % 2, r, :]).then_inc(m_dma, 16)
                sp.wait_ge(m_dma, (l * UNIT_L + u + 1) * 32)
                sp.sem_inc(apart_sp, 1)

            with sp.Fori(0, NL) as l:
                sp.wait_ge(ln_st, l * LN_L + 1)
                sp.sem_inc(apart_sp, 1)
                sp.dma_start(WA[:, :], wa_d[bass.ds(l, 1), :, :].rearrange("a p n -> p (a n)")).then_inc(wa_in, 16)
                sp.wait_ge(layer_done, l + 1)
                sp.sem_inc(apart_sp, 1)
                for dst, src in ((WF, wf_d), (F1B, f1b_d), (F2B, f2b_d)):
                    sp.dma_start(dst[:, :], src[bass.ds(l, 1), :, :].rearrange("a p n -> p (a n)")).then_inc(wf_in, 16)
                stack(l, 0, B * SC, [("k", KC[0:MASK_ROW, :, :])])
                for b in range(B):
                    stack(l, 1 + b, S, [("q", QS[0:MASK_ROW, b, :, :]), ("k", KS[0:MASK_ROW, b, :, :])])
                for u in range(NU):
                    maxima(l, u)
                for b in range(B):
                    stack(l, 3 + b, S, [("q", QS[0:MASK_ROW, b, :, :])])
                for u in range(NU, 2 * NU):
                    maxima(l, u)
            sp.wait_ge(layer_done, NL + 1)
            sp.dma_start(EWA[:, 0:NE, :], w1_d).then_inc(expert_in, 16)
            sp.dma_start(EWD[:, 0:2 * NE, :], w2_d).then_inc(expert_in, 16)
            sp.wait_ge(down_ps, 2 * NT)
            for dst, src in ((EWA, eg_d), (EWB, eu_d), (EWD, ed_d)):
                sp.dma_start(dst, src).then_inc(expert_in, 16)
            for b in range(B):
                sp.wait_ge(x_done, b + 1)
                sp.dma_start(out_d[b].rearrange("(t p) d -> p t d", p=P), XI[:, TB * b:TB * (b + 1), :]).then_inc(out_done, 16)
            sp.wait_ge(out_done, 16 * B)

        @block.gpsimd
        def _(g):
            nc.gpsimd.memset(cstack[0:ROWS2, :], ONES)
            nc.gpsimd.memset(stacks[0:ROWS2, 0, :], ONES).then_inc(const_ready, 1)
            nc.gpsimd.memset(half[:, :], -0.5)
            nc.gpsimd.memset(VP[:, :, :, :], 1.0)
            nc.gpsimd.memset(VC[:, :, :, :], 1.0)
            nc.gpsimd.memset(VT[:, :, :, :, :], 0.0).then_inc(pool_step, 1)
            g.wait_ge(pool_step, 1)
            for r in range(UH):
                nc.gpsimd.memset(VT[TAIL * r:TAIL * (r + 1), :, :, r, HD:HD + 1], 1.0).then_inc(pool_step, 1)
                g.wait_ge(pool_step, r + 2)
            nc.gpsimd.memset(ctxT[:, :, S2:SC], 0.0).then_inc(const_ready, 1)
            g.wait_ge(const_ready, 2)

            def inverse_root(n):
                g.wait_ge(ln_st, n)
                nc.gpsimd.tensor_tensor(rstd[:, :], vpe[:, :], half[:, :], ALU.pow).then_inc(ln_rs, 1)

            inverse_root(1)
            g.wait_ge(ad_ready, 2)
            with g.Fori(0, NL) as l:
                g.wait_ge(layer_done, l + 1)
                nc.gpsimd.tensor_copy(ADL[:, :, :, :].rearrange("p n k b -> p (n k b)"),
                                      AD[:, bass.ds(l, 1), :, :, :].rearrange("p l n k b -> p (l n k b)")).then_inc(adl_ready, 1)
                for n in range(LN_L):
                    inverse_root(l * LN_L + n + 2)
            post_gpsimd(g, inverse_root)

        @block.scalar
        def _(act):
            def turned(n, scale=None, bias=None, pre=None):
                for b in range(B):
                    act.wait_ge(tp_ps, n + b + 1)
                    kw = {}
                    if scale is not None:
                        kw = dict(scale=scale(b), bias=bias(b))
                    nc.scalar.activation(XT[:, b * S:(b + 1) * S], bank[b][:, :], ACT.Identity, **kw).then_inc(xt_ready, 1)

            with act.Fori(0, NL) as l:
                def item_cols(m):
                    i, kind, b = ITEMS[m]
                    return i % 2, 0 if kind == "q" else 1, B * SC if i == 0 else S

                def high(m):
                    j, k, n = item_cols(m)
                    act.wait_ge(rot_done, l * ITEM_L + m + 1)
                    if ITEMS[m][0] >= 2:
                        act.wait_ge(stack_wr, (l * PARTS_L + ITEMS[m][0] - 1) * NSLOT * 16)
                    nc.scalar.copy(parts[:, j, k, 0, 0:n], rF[:, m % 3, 0:n]).then_inc(hi_done, 1)

                def middle(m):
                    j, k, n = item_cols(m)
                    act.wait_ge(r1_done, l * ITEM_L + m + 1)
                    nc.scalar.copy(parts[:, j, k, 1, 0:n], rA[:, m % 3, 0:n]).then_inc(mid_done, 1)

                def rotations(ms, between={}):
                    for k in range(len(ms) + 1):
                        if k < len(ms):
                            high(ms[k])
                        if k in between:
                            between[k]()
                        if k >= 1:
                            middle(ms[k - 1])

                def norm(n):
                    act.wait_ge(adl_ready, l + 1)
                    turned(l * TP_L + n * B, lambda b: ADL[:, n, 0, b:b + 1], lambda b: ADL[:, n, 1, b:b + 1])

                act.wait_ge(v_ps, l * V_L + 1)
                nc.scalar.copy(VC[:, :, :, 0:HD], bank[6][:, 0:B * D].rearrange("p (b h d) -> p b h d", b=B, h=H)).then_inc(v_ready, 1)
                act.wait_ge(v_ps, l * V_L + 2)
                for r in range(UH):
                    rows = slice(TAIL * r, TAIL * (r + 1))
                    nc.scalar.copy(VT[rows, :, :, r, 0:HD],
                                   bank[7][rows, 0:B * D].rearrange("p (b u r d) -> p b u r d", b=B, u=H // UH, r=UH)[:, :, :, r, :]
                                   ).then_inc(v_ready, 1)
                norm(0)

                def self_values(b):
                    act.wait_ge(v_ps, l * V_L + 3 + b)
                    nc.scalar.copy(VP[:, TB * b:TB * (b + 1), :, 0:HD],
                                   bank[6 + b][:, :].rearrange("p (t h d) -> p t h d", t=TB, h=H)).then_inc(v_ready, 1)

                rotations([0, 1, 2, 3, 4], {3: lambda: self_values(0)})
                self_values(1)

                def attention(kind):
                    def attended(b):
                        act.wait_ge(at_ps, l * 2 * B + kind * B + b + 1)
                        nc.scalar.copy(attT[:, b * S:(b + 1) * S], bank[b][:, :]).then_inc(at_ready, 1)

                    for slot in range(B * H + LEAD + 3):
                        j = slot - LEAD
                        if slot == 26:
                            attended(0)
                        if not 0 <= j < B * H:
                            continue
                        head = kind * B * H + j
                        u = j // UH
                        if kind == 0:
                            for kc in range(TB):
                                act.wait_ge(s2_ps, l * S2_L + TB * j + kc + 1)
                                if kc == 0 and head >= NPT:
                                    act.wait_ge(pv_done, l * PV_L + head - NPT + 1)
                                nc.scalar.activation(PT[:, j % NPT, kc, :], bank[4 + kc % 2][:, :], ACT.Exp,
                                                     scale=SCALE).then_inc(s2_exp, 1)
                        else:
                            base = B * H * TB + (UH + 1) * u
                            if j % UH == 0:
                                act.wait_ge(s2_ps, l * S2_L + base + 1)
                                if u >= 2:
                                    act.wait_ge(pv_done, l * PV_L + B * H + u - 1)
                                nc.scalar.activation(PTT[:, u % 2, :], bank[4 + base % 2][:, :], ACT.Exp,
                                                     scale=SCALE).then_inc(s2_exp, 1)
                            n = base + 1 + j % UH
                            act.wait_ge(s2_ps, l * S2_L + n + 1)
                            if u >= NPT:
                                act.wait_ge(pv_done, l * PV_L + B * H + u - NPT + 1)
                            else:
                                act.wait_ge(pv_done, l * PV_L + B * H)
                            nc.scalar.activation(PT[:, u % NPT, j % UH, :], bank[4 + n % 2][:, :], ACT.Exp,
                                                 scale=SCALE).then_inc(s2_exp, 1)
                    attended(1)

                attention(0)
                norm(1)
                rotations([5, 6])
                attention(1)
                norm(2)
                act.wait_ge(wf_in, (l + 1) * 48)
                for n in range(B * 4):
                    act.wait_ge(f1_ps, l * 8 + n + 1)
                    nc.scalar.activation(HL[:, n, :], bank[2 + n % 4][:, :], ACT.Gelu, bias=F1B[:, n % 4:n % 4 + 1]).then_inc(h_ready, 1)
            post_scalar(act, turned)

        @block.vector
        def _(v):
            chain = {"base": 0, "n": 0}
            V = nc.vector

            def link(ins):
                chain["n"] += 1
                ins.then_inc(dve_step, 1)
                v.wait_ge(dve_step, chain["base"] + chain["n"])

            def layer_norm(src, dst):
                for j in range(NT):
                    ins = V.bn_stats(stats[:, j, :], src[:, j, :])
                link(ins)
                v.sem_inc(apart_dve, 1)
                for j in range(NT):
                    ins = V.bn_aggr(mv[:, j, :], stats[:, j, :])
                link(ins)
                V.tensor_scalar(vpe[:, :], mv[:, :, 1], EPS, None, ALU.add).then_inc(ln_st, 1)
                yield
                for j in range(NT):
                    V.tensor_scalar(dst[:, j, :], src[:, j, :], mv[:, j, 0:1], rstd[:, j:j + 1],
                                    ALU.subtract, ALU.mult).then_inc(ln_xn, 1)
                yield

            def run_norm(src, dst, n):
                steps = layer_norm(src, dst)
                next(steps)
                v.wait_ge(ln_rs, n)
                next(steps)

            V.memset(stacks[0:ROWS2, 1, :], ONES).then_inc(stack_ones, 1)
            v.wait_ge(small_in, 16 * NSMALL)
            v.wait_ge(const_ready, 2)
            link(V.memset(mask_row[:, :], NEG))
            V.tensor_scalar(mask_row[0:1, 0:B * S], mask_raw[0:1, 0:B * S], NEG, None, ALU.mult).then_inc(mask_ready, 1)
            for b in range(B):
                V.tensor_scalar(mask_row[0:1, B * S + b * SC:B * S + b * SC + S2],
                                mask_raw[0:1, B * S + b * S2:B * S + (b + 1) * S2], NEG, None, ALU.mult).then_inc(mask_ready, 1)
            run_norm(XI, Y, 1)
            v.wait_ge(ad_ps, 1)
            ad = AD[:, :, :, :, :].rearrange("p l n k b -> p (l n) k b")
            link(V.tensor_tensor(ad, bank[7][:, 0:3 * NL * 4].rearrange("p (n k b) -> p n k b", k=2, b=B),
                                 NB[:, :, :].unsqueeze(3).to_broadcast([P, 3 * NL, 2, B]), ALU.add))
            V.tensor_scalar(ad[:, :, 0, :], ad[:, :, 0, :], 1.0, None, ALU.add).then_inc(ad_ready, 2)
            v.wait_ge(ln_xn, NT)
            v.sem_inc(layer_done, 1)
            before = chain["n"]

            with v.Fori(0, NL) as l:
                chain["base"] = l * DVE_L + before
                chain["n"] = 0

                def item_cols(m):
                    i, kind, b = ITEMS[m]
                    return i % 2, 0 if kind == "q" else 1, B * SC if i == 0 else S

                def rotate(m):
                    j, k, n = item_cols(m)
                    r = m % 3
                    c = 2 + 2 * (m % 2)
                    if m >= 3:
                        v.wait_ge(lo_done, l * ITEM_L + m - 2)
                    v.wait_ge(qk_ps, l * ITEM_L + m + 1)
                    for t, src, dst in ((0, bank[c], rA), (1, bank[c + 1], rB)):
                        if ITEMS[m][0] == 0:
                            for b in range(B):
                                ins = V.tensor_tensor(dst[:, r, b * SC:(b + 1) * SC], src[:, b * SC:(b + 1) * SC],
                                                      rot[:, t, 0:SC], ALU.mult)
                        else:
                            ins = V.tensor_tensor(dst[:, r, 0:n], src[:, 0:n], rot[:, t, 0:n], ALU.mult)
                    link(ins)
                    V.tensor_tensor(rF[:, r, 0:n], rA[:, r, 0:n], rB[:, r, 0:n], ALU.add).then_inc(rot_done, 1)

                def residue(m):
                    j, k, n = item_cols(m)
                    v.wait_ge(hi_done, l * ITEM_L + m + 1)
                    v.wait_ge(rot_done, l * ITEM_L + m + 1)
                    V.tensor_tensor(rA[:, m % 3, 0:n], rF[:, m % 3, 0:n], parts[:, j, k, 0, 0:n], ALU.subtract).then_inc(r1_done, 1)

                def low(m):
                    j, k, n = item_cols(m)
                    v.wait_ge(mid_done, l * ITEM_L + m + 1)
                    v.wait_ge(r1_done, l * ITEM_L + m + 1)
                    ins = V.tensor_tensor(parts[:, j, k, 2, 0:n], rA[:, m % 3, 0:n], parts[:, j, k, 1, 0:n], ALU.subtract)
                    ins.then_inc(lo_done, 1)

                def rotations(ms):
                    for k in range(len(ms) + 2):
                        if k < len(ms):
                            rotate(ms[k])
                        if 0 <= k - 1 < len(ms):
                            residue(ms[k - 1])
                        if k >= 2:
                            low(ms[k - 2])

                def update(kind, b):
                    v.wait_ge(pr_ps, l * 2 * B + kind * B + b + 1)
                    y = Y[:, TB * b:TB * (b + 1), :]
                    ins = V.tensor_tensor(y, y, bank[b][:, :].rearrange("p (t d) -> p t d", t=TB), ALU.add)
                    return ins

                def attention(kind):
                    def normalise(u):
                        ku = kind * NU + u
                        b, h0 = u // (H // UH), UH * (u % (H // UH))
                        v.wait_ge(pv_done, l * PV_L + (UH * (u + 1) if kind == 0 else B * H + u + 1))
                        o = bank[6 + u % 2][:, 0:UH * TB * (HD + 1)].rearrange(
                            "p (h t c) -> p h t c", h=UH, t=TB)
                        link(V.reciprocal(orec[:, u % 2, :, :], o[:, :, :, HD]))
                        V.tensor_tensor(att[:, TB * b:TB * (b + 1), h0 * HD:(h0 + UH) * HD].rearrange("p t (h d) -> p h t d", h=UH),
                                        o[:, :, :, 0:HD],
                                        orec[:, u % 2, :, :].unsqueeze(3).to_broadcast([P, UH, TB, HD]),
                                        ALU.mult).then_inc(att_ready, 1)

                    def maxima(u):
                        ku = kind * NU + u
                        v.wait_ge(m_ps, l * UNIT_L + ku + 1)
                        if ku >= 2:
                            v.wait_ge(m_dma, (l * UNIT_L + ku - 1) * 32)
                        m = bank[6 + u % 2][0:UH * TB, 256:256 + P]
                        V.tensor_copy(mrow[:, u % 2, 0, :], m).then_inc(m_ready, 1)
                        v.wait_ge(m_ready, (l * UNIT_L + ku) * 2 + 1)
                        V.tensor_tensor(mrow[:, u % 2, 1, :], m, mrow[:, u % 2, 0, :], ALU.subtract).then_inc(m_ready, 1)

                    for slot in range(B * H + LEAD + 3):
                        if slot >= 5 and slot % UH == 5 % UH and (slot - 5) // UH < NU:
                            maxima((slot - 5) // UH)
                        if slot < B * H:
                            u, hl = slot // UH, slot % UH
                            if hl == 0 and kind * NU + u >= 2:
                                v.wait_ge(m_ps, l * UNIT_L + kind * NU + u - 1)
                            if kind == 0:
                                for qt in range(TB):
                                    n = TB * slot + qt
                                    v.wait_ge(s1_ps, l * S1_L + n + 1)
                                    V.tensor_reduce(nmax[:, u % 2, hl * TB + qt:hl * TB + qt + 1], bank[2 + n % 2][:, :],
                                                    AX.X, ALU.max, negate=True).then_inc(s1_max, 1)
                            else:
                                for qp in range(2):
                                    n = B * H * TB + 2 * slot + qp
                                    v.wait_ge(s1_ps, l * S1_L + n + 1)
                                    V.tensor_reduce(nmax[:, u % 2, hl * TB + 2 * qp:hl * TB + 2 * qp + 2],
                                                    bank[2 + n % 2][:, :].rearrange("p (t k) -> p t k", t=2)[:, :, 0:S2],
                                                    AX.X, ALU.max, negate=True).then_inc(s1_max, 1)
                        if slot >= 11 and slot % UH == 11 % UH:
                            normalise((slot - 11) // UH)
                        if slot == 28:
                            update(kind, 0).then_inc(x_ready, 1)
                    link(update(kind, 1))
                    v.wait_ge(x_ready, l * 2 + kind + 1)

                run_norm(Y, XN, l * LN_L + 2)
                rotations([0, 1, 2, 3, 4])
                attention(0)
                run_norm(Y, XN, l * LN_L + 3)
                rotations([5, 6])
                attention(1)
                run_norm(Y, XN, l * LN_L + 4)
                v.wait_ge(wf_in, (l + 1) * 48)
                for b in range(B):
                    v.wait_ge(f2_ps, l * B + b + 1)
                    y = Y[:, TB * b:TB * (b + 1), :]
                    link(V.tensor_tensor(y, y, bank[6 + b][:, :].rearrange("p (t d) -> p t d", t=TB), ALU.add))
                    link(V.tensor_tensor(y, y, F2B[:, :].unsqueeze(1).to_broadcast([P, TB, D]), ALU.add))
                v.sem_inc(layer_done, 1)
                assert chain["n"] == DVE_L, chain["n"]
            chain["base"], chain["n"] = NL * DVE_L + before, 0
            post_vector(v, link, run_norm)

        @block.tensor
        def _(pe):
            mm = nc.tensor.matmul
            pe.wait_ge(small_in, 16 * NSMALL)
            for i in range(3 * NL):
                for k in range(2):
                    c = (2 * i + k) * B
                    ins = mm(bank[7][:, c:c + B], NW[:, i, k * D:(k + 1) * D], condT[:, :], start=True, stop=True)
            ins.then_inc(ad_ps, 1)
            pe.wait_ge(const_ready, 2)
            pe.wait_ge(ad_ready, 2)

            def turn(src, xn_before, dst=bank, after=None):
                for b in range(B):
                    for t in range(TB):
                        j = TB * b + t
                        pe.wait_ge(ln_xn, xn_before + j + 1)
                        ins = nc.tensor.transpose(bank[b][:, t * P:(t + 1) * P], src[:, j, :], ident[:, :])
                    ins.then_inc(tp_ps, 1)

            pe.wait_ge(mask_dma, 48 * H)
            with pe.Fori(0, NL) as l:
                def project(m, pair, src):
                    i, kind, b = ITEMS[m]
                    c = 2 + 2 * (m % 2)
                    if m >= 2:
                        pe.wait_ge(rot_done, l * ITEM_L + m - 1)
                    n = B * SC if i == 0 else S
                    mm(bank[c][:, 0:n], wcol(pair[0]), src, start=True, stop=True)
                    mm(bank[c + 1][:, 0:n], wcol(pair[1]), src, start=True, stop=True).then_inc(qk_ps, 1)

                def attention(kind):
                    k_stack = KS if kind == 0 else KC

                    def first(j, i):
                        b, h = j // H, j % H
                        if kind == 0:
                            n = TB * j + i
                            if n >= 2:
                                pe.wait_ge(s1_max, l * S1_L + n - 1)
                            mm(bank[2 + n % 2][:, :], QS[0:ROWS1, b, h, i * P:(i + 1) * P],
                               KS[0:ROWS1, b, h, :], start=True, stop=True).then_inc(s1_ps, 1)
                        else:
                            n = B * H * TB + 2 * j + i // 2
                            if i % 2 == 0:
                                pe.wait_ge(s1_max, l * S1_L + n - 1)
                            ins = mm(bank[2 + n % 2][:, 256 * (i % 2):256 * (i % 2) + S2],
                                     QS[0:ROWS1, b, h, i * P:(i + 1) * P],
                                     KC[0:ROWS1, h, b * SC:b * SC + S2], start=True, stop=True)
                            if i % 2:
                                ins.then_inc(s1_ps, 1)

                    def second(j, i):
                        b, h, u = j // H, j % H, j // UH
                        q = QS[0:ROWS2, b, h, :]
                        if j % UH == 0 and i == 0:
                            pe.wait_ge(m_dma, (l * UNIT_L + kind * NU + u + 1) * 32)
                        if kind == 0:
                            n = TB * j + i
                            if n >= 2:
                                pe.wait_ge(s2_exp, l * S2_L + n - 1)
                            mm(bank[4 + n % 2][:, :], KS[0:ROWS2, b, h, i * P:(i + 1) * P], q,
                               start=True, stop=True).then_inc(s2_ps, 1)
                        elif i == 0:
                            n = B * H * TB + (UH + 1) * u
                            if j % UH == 0:
                                pe.wait_ge(s2_exp, l * S2_L + n - 1)
                                pe.sem_inc(apart_pe, 1)
                                for hl in range(UH):
                                    ins = mm(bank[4 + n % 2][TAIL * hl:TAIL * (hl + 1), :],
                                             KC[0:ROWS2, h + hl, b * SC + P:(b + 1) * SC],
                                             QS[0:ROWS2, b, h + hl, :], start=True, stop=True)
                                ins.then_inc(s2_ps, 1)
                            n += 1 + j % UH
                            pe.wait_ge(s2_exp, l * S2_L + n - 1)
                            mm(bank[4 + n % 2][:, :], KC[0:ROWS2, h, b * SC:b * SC + P], q,
                               start=True, stop=True).then_inc(s2_ps, 1)

                    def values(j, qt):
                        b, h, u, hl = j // H, j % H, j // UH, j % UH
                        ku = kind * NU + u
                        cols = slice(qt * P, (qt + 1) * P)
                        o = bank[6 + u % 2][:, 0:UH * TB * (HD + 1)].rearrange("p (h t c) -> p h t c", h=UH, t=TB)
                        if kind == 0:
                            if qt == 0:
                                if hl == 0:
                                    pe.wait_ge(m_ready, (l * UNIT_L + ku + 1) * 2)
                                pe.wait_ge(s2_exp, l * S2_L + TB * (j + 1))
                            for kc in range(TB):
                                ins = mm(o[:, hl, qt, :], PT[:, j % NPT, kc, cols], VP[:, TB * b + kc, h, :],
                                         start=(kc == 0), stop=(kc == TB - 1))
                            if qt == TB - 1:
                                ins.then_inc(pv_done, 1)
                        elif hl == UH - 1:
                            if qt == 0:
                                pe.wait_ge(m_ready, (l * UNIT_L + ku + 1) * 2)
                                pe.wait_ge(s2_exp, l * S2_L + B * H * TB + (UH + 1) * (u + 1))
                            mm(o[:, :, qt, :], PTT[:, u % 2, cols], VT[:, b, u % (H // UH), :, :], start=True, stop=False)
                            for r in range(UH):
                                ins = mm(o[:, r, qt, :], PT[:, u % NPT, r, cols], VC[:, b, h - hl + r, :],
                                         start=False, stop=(r == UH - 1))
                            if qt == TB - 1:
                                ins.then_inc(pv_done, 1)

                    def attended(b):
                        pe.wait_ge(att_ready, l * UNIT_L + kind * NU + (b + 1) * (H // UH))
                        for t in range(TB):
                            ins = nc.tensor.transpose(bank[b][:, t * P:(t + 1) * P], att[:, TB * b + t, :], ident[:, :])
                        ins.then_inc(at_ps, 1)

                    def output(b):
                        pe.wait_ge(at_ready, l * 2 * B + kind * B + b + 1)
                        for t in range(TB):
                            ins = mm(bank[b][:, t * P:(t + 1) * P], attT[:, b * S + t * P:b * S + (t + 1) * P],
                                     wcol(WO if kind == 0 else CO), start=True, stop=True)
                        ins.then_inc(pr_ps, 1)

                    for slot in range(B * H + LEAD + 3):
                        if slot == 25:
                            attended(0)
                        if slot == 27:
                            output(0)
                        for i in range(TB):
                            if slot < B * H:
                                if i == 0 and slot % H == 0:
                                    at = RD_AT[(1 if kind == 0 else 3) + slot // H]
                                    pe.wait_ge(stack_rd, (l * RD_L + at) * 16)
                                first(slot, i)
                            if 0 <= slot - LEAD < B * H:
                                second(slot - LEAD, i)
                            if 0 <= slot - LEAD - 1 < B * H:
                                values(slot - LEAD - 1, i)
                        if slot >= UH and slot % UH == 0 and slot // UH <= NU:
                            u = slot // UH - 1
                            ku = kind * NU + u
                            pe.wait_ge(s1_max, l * S1_L + (TB * UH * (u + 1) if kind == 0 else B * H * TB + 2 * UH * (u + 1)))
                            if ku >= 2:
                                pe.wait_ge(att_ready, l * UNIT_L + ku - 1)
                            nc.tensor.transpose(bank[6 + u % 2][0:UH * TB, 256:256 + P], nmax[:, u % 2, :],
                                                ident[:, :]).then_inc(m_ps, 1)
                    attended(1)
                    output(1)

                pe.wait_ge(wa_in, (l + 1) * 16)
                project(0, (CK, CKR), ctxT[:, :, :].rearrange("p b s -> p (b s)"))
                for b in range(B):
                    ins = mm(bank[6][:, b * D:(b + 1) * D], ctxT[:, b, 0:P], wcol(CV), start=True, stop=True)
                ins.then_inc(v_ps, 1)
                for b in range(B):
                    for j in range(4):
                        ins = mm(bank[7][TAIL * j:TAIL * (j + 1), b * D:(b + 1) * D], ctxT[:, b, P:SC], wcol(CV),
                                 start=True, stop=True)
                ins.then_inc(v_ps, 1)
                turn(XN, l * XN_L + NT)
                for b in range(B):
                    pe.wait_ge(xt_ready, l * TP_L + b + 1)
                    xt = XT[:, b * S:(b + 1) * S]
                    project(1 + 2 * b, (WQ, WQR), xt)
                    project(2 + 2 * b, (WK, WKR), xt)
                    pe.wait_ge(v_ready, l * VR_L + 1 + UH * b)
                    for t in range(TB):
                        ins = mm(bank[6 + b][:, t * P:(t + 1) * P], XT[:, b * S + t * P:b * S + (t + 1) * P], wcol(WV),
                                 start=True, stop=True)
                    ins.then_inc(v_ps, 1)
                pe.wait_ge(rot_done, l * ITEM_L + 5)
                pe.wait_ge(v_ready, l * VR_L + VR_L)
                attention(0)
                turn(XN, l * XN_L + 2 * NT)
                for b in range(B):
                    pe.wait_ge(xt_ready, l * TP_L + B + b + 1)
                    project(5 + b, (CQ, CQR), XT[:, b * S:(b + 1) * S])
                pe.wait_ge(rot_done, l * ITEM_L + 7)
                attention(1)
                turn(XN, l * XN_L + 3 * NT)
                pe.wait_ge(wf_in, (l + 1) * 48)
                for b in range(B):
                    pe.wait_ge(xt_ready, l * TP_L + 2 * B + b + 1)
                    for fc in range(4):
                        n = 4 * b + fc
                        if n >= 4:
                            pe.wait_ge(h_ready, l * 8 + n - 3)
                        mm(bank[2 + n % 4][:, :], WF[:, fc * P:(fc + 1) * P], XT[:, b * S:(b + 1) * S],
                           start=True, stop=True).then_inc(f1_ps, 1)
                for b in range(B):
                    pe.wait_ge(h_ready, l * 8 + 4 * (b + 1))
                    for t in range(TB):
                        for fc in range(4):
                            ins = mm(bank[6 + b][:, t * P:(t + 1) * P], HL[:, 4 * b + fc, t * P:(t + 1) * P],
                                     WF[:, DFF + fc * D:DFF + (fc + 1) * D], start=(fc == 0), stop=(fc == 3))
                    ins.then_inc(f2_ps, 1)
                pe.wait_ge(layer_done, l + 2)
            post_tensor(pe, turn)


def tables():
    half = HD // 2
    inv = (1.0 / 10000.0 ** (np.arange(half, dtype=np.float32) / half)).astype(np.float32)
    ang = np.arange(S, dtype=np.float32)[:, None] * inv
    cos, sin = np.cos(ang).astype(np.float32), np.sin(ang).astype(np.float32)
    rot = np.zeros((HD, H, 2, S), np.float32)
    for d in range(HD):
        rot[d, :, 0] = cos[:, d % half]
        rot[d, :, 1] = -sin[:, d] if d < half else sin[:, d - half]
    rev = np.broadcast_to(NE - np.arange(NE, dtype=np.float32), (P, NT, NE))
    return rot.reshape(P, 2, S), np.eye(P, dtype=np.float32), np.ascontiguousarray(rev)


def layout(a):
    def turned(w):
        return np.swapaxes(w, -1, -2)

    def by_channel(w, swap=False):
        w = w.reshape(NL, H, HD, D)
        if swap:
            w = np.concatenate([w[:, :, HD // 2:], w[:, :, :HD // 2]], axis=2)
        return turned(w.transpose(0, 2, 1, 3).reshape(NL, D, D))

    qkv, cq, ck = a["L0_xcond_qkv_w"], a["L0_xcond_cq_w"], a["L0_xcond_ck_w"]
    wq, wk, wv = qkv[:, :D], qkv[:, D:2 * D], qkv[:, 2 * D:]
    wa = np.concatenate([by_channel(wq), by_channel(wq, True), by_channel(wk), by_channel(wk, True), turned(wv),
                         turned(a["L0_xcond_so_w"]), by_channel(cq), by_channel(cq, True), by_channel(ck),
                         by_channel(ck, True), turned(a["L0_xcond_cv_w"]), turned(a["L0_xcond_co_w"])], axis=2)
    f1, f2 = turned(a["L0_xcond_f1_w"]), turned(a["L0_xcond_f2_w"])
    wf = np.concatenate([f1, f2.reshape(NL, 4, P, D).transpose(0, 2, 1, 3).reshape(NL, P, 4 * D)], axis=2)
    nw = np.stack([turned(a[f"L0_xcond_n{n}_w"]) for n in (1, 2, 3)], axis=1).reshape(3 * NL, D, 2 * D).transpose(1, 0, 2)
    nb = np.stack([a[f"L0_xcond_n{n}_b"] for n in (1, 2, 3)], axis=1).reshape(3 * NL, 2, D).transpose(2, 0, 1)
    rot, ident, rev = tables()
    f2b = np.broadcast_to(a["L0_xcond_f2_b"][:, None, :], (NL, P, D))
    w1 = a["L0_ffn_w1"].transpose(2, 0, 1)
    w2 = turned(a["L0_ffn_w2"]).reshape(NE, 2, P, D).transpose(2, 0, 1, 3).reshape(P, 2 * NE, D)
    eg = np.concatenate([a["L1_ffn_rt_gate"], a["L1_ffn_sh_gate"][None]]).transpose(1, 0, 2)
    eu = np.concatenate([a["L1_ffn_rt_up"], a["L1_ffn_sh_up"][None]]).transpose(1, 0, 2)
    ed = np.concatenate([a["L1_ffn_rt_down"], a["L1_ffn_sh_down"][None]]).reshape(NE + 1, 2, P, D)
    ed = ed.transpose(2, 0, 1, 3).reshape(P, 2 * (NE + 1), D)
    return {
        "x": a["x"], "cond": a["cond_1024"].T, "ctx": turned(a["ctx_1024"]), "mask": a["mask_BxS_bf0"].reshape(-1).view(np.int32)[None],
        "mask2": a["mask_BxS2_bf0"].reshape(-1).view(np.int32)[None], "rot": rot, "ident": ident, "rev": rev, "nw": nw, "nb": nb,
        "wa": wa, "wf": wf, "f1b": a["L0_xcond_f1_b"].reshape(NL, 4, P).transpose(0, 2, 1), "f2b": f2b,
        "gb": np.stack([a["L0_ffn_ln_gamma"], a["L0_ffn_ln_beta"]], axis=1),
        "mg": np.stack([a["L0_ffn_gate_w"].T, a["L1_ffn_gate_w"]], axis=1), "w1": w1, "w2": w2,
        "watt": a["L1_xcond_W_att"].reshape(2, D, D).transpose(1, 0, 2), "vatt": a["L1_xcond_V_att"],
        "wi": a["L1_xcond_Wi"].reshape(2, D, 3 * D).transpose(1, 0, 2), "uh": a["L1_xcond_Uh"],
        "sb": a["L1_xcond_b"].reshape(3, D).T, "rgate": a["L1_ffn_gate_w"], "eg": eg, "eu": eu, "ed": ed,
    }


def kernel(**inputs):
    import concourse.bacc as bacc
    from concourse.bass_utils import run_bass_kernel_spmd

    nc = bacc.Bacc("TRN2", target_bir_lowering=False, num_devices=1)
    arrays, args = {}, []
    for name, a in layout({k: np.asarray(v) for k, v in inputs.items()}).items():
        a = np.ascontiguousarray(a)
        arrays[f"in_{name}"] = a
        args.append(nc.dram_tensor(f"in_{name}", a.shape, mybir.dt.from_np(a.dtype), kind="ExternalInput").ap())
    args.append(nc.dram_tensor("out", (B, S, D), FP32, kind="ExternalOutput").ap())
    build(nc, *args)
    return run_bass_kernel_spmd(nc, [arrays], core_ids=[0]).results[0]["out"]
```

```python
from contextlib import ExitStack

import numpy as np
import concourse.bass as bass
from concourse import mybir

FP32 = mybir.dt.float32
BF16 = mybir.dt.bfloat16
ALU = mybir.AluOpType
ACT = mybir.ActivationFunctionType
AX = mybir.AxisListType

P = 128
B, S, S2, D = 2, 512, 154, 128
NL, H, HD = 6, 16, 8
DFF = 512
NE, FE = 8, 256
EPS = 1e-5
NT = B * S // P
TB = S // P
TAIL = 32
SC = P + TAIL
NEG = -1.0e30
ONES = float(np.array([0x3F803F80], np.uint32).view(np.float32)[0])
SCALE = 1.0 / float(np.sqrt(np.float32(HD)))

Q_PART = [0, 1, 2, 0, 1, 0]
K_PART = [0, 0, 0, 1, 1, 2]
NSLOT = len(Q_PART)
PROD = NSLOT * HD
MASK_ROW = 64
MAX_ROW = 96
ROWS1 = MAX_ROW

WQ, WQR, WK, WKR, WV, WO, CQ, CQR, CK, CKR, CV, CO = range(12)

LEAD = [6, 8]
UH = 4
NU = B * H // UH
NPT = 3
PT_AT = [0, 2, 5, 9]
PT_TILES = 14
HC = 32
U = 32

LN_L, XN_L, TP_L = 3, 3 * NT, 3 * B
PARTS_L = 5
ITEMS = [(0, "k", 0), (1, "q", 0), (1, "k", 0), (2, "q", 1), (2, "k", 1), (3, "q", 0), (4, "q", 1)]
ITEM_L = len(ITEMS)
RD_L, RD_AT = 7, [1, 3, 5, 6, 7]
S1_L = B * H * TB + B * H * 2
S2_L = B * H * TB + B * H + NU
V_L, VR_L, UNIT_L = 4, 7, 2 * NU
STEPS = B * H + TB - 1
PV_L = STEPS + NU
DVE_L = 35


def build(nc, x_d, cond_d, ctx_d, mask_d, mask2_d, rot_d, ident_d, rev_d, nw_d, nb_d, wa_d, wf_d, f1b_d, f2b_d,
          gb_d, mg_d, w1_d, w2_d, watt_d, vatt_d, wi_d, uh_d, sb_d, rgate_d, eg_d, eu_d, ed_d, out_d):
    ctx = ExitStack()
    with ctx:
        def sb(name, shape, dt=FP32):
            return ctx.enter_context(nc.sbuf_tensor(name, shape, dt))

        def sem(name):
            return ctx.enter_context(nc.semaphore(name))

        bank = [ctx.enter_context(nc.psum_tensor(f"bank{i}", [P, 512], FP32)) for i in range(8)]
        scratch = nc.dram_tensor("stack_scratch", (2, NSLOT, P, 2, S), BF16, kind="Internal").ap()

        ident = sb("ident", [P, P])
        rot = sb("rot", [P, 2, S])
        rev = sb("rev", [P, NT, NE])
        half = sb("half", [P, NT])
        XI = sb("XI", [P, NT, D])
        Y = sb("Y", [P, NT, D])
        XN = sb("XN", [P, NT, D])
        XT = sb("XT", [P, B * S])
        condT = sb("condT", [P, B])
        ctxT = sb("ctxT", [P, B, SC])
        stats = sb("stats", [P, NT, 6])
        mv = sb("mv", [P, NT, 2])
        vpe = sb("vpe", [P, NT])
        rstd = sb("rstd", [P, NT])
        stacks = sb("stacks", [P, 2, H * B * S // 2])
        share = sb("share", [P, 3 * NL * 2 * D])
        NW = share[:, :].rearrange("p (n k) -> p n k", k=2 * D)
        NB = sb("NB", [P, 3 * NL, 2])
        AD = sb("AD", [P, NL, 3, 2, B])
        ADL = sb("ADL", [P, 3, 2, B])
        WA = sb("WA", [P, 12 * D])
        WF = sb("WF", [P, 2 * DFF])
        F1B = sb("F1B", [P, 4])
        F2B = sb("F2B", [P, D])
        QS = stacks[0:P, 0, :].bitcast(BF16).rearrange("p (b h t) -> p b h t", b=B, h=H)
        KS = stacks[0:P, 1, :].bitcast(BF16).rearrange("p (b h t) -> p b h t", b=B, h=H)
        cstack = sb("cstack", [P, H * B * SC // 2])
        KC = cstack[0:P, :].bitcast(BF16).rearrange("p (h t) -> p h t", h=H)
        parts = sb("parts", [P, 2, 2, 3, S], BF16)
        work = sb("work", [P, 9 * S])
        rA, rB, rF = [work[:, 3 * S * i:3 * S * (i + 1)].rearrange("p (r t) -> p r t", r=3) for i in range(3)]
        VP = sb("VP", [P, NT, H, HD + 1])
        VC = sb("VC", [P, B, H, HD + 1])
        VT = sb("VT", [P, B, H // UH, UH, HC])
        nmax = sb("nmax", [P, 2, UH * TB])
        mrow = sb("mrow", [UH * TB, 2, 2, P], BF16)
        ring = sb("ring", [P, PT_TILES * S])
        PT = ring[:, :].rearrange("p (n q) -> p n q", q=S)
        OT = XN[:, :, :].rearrange("p (u t) d -> p u (t d)", u=2)
        PTT = sb("PTT", [P, 2, S])
        mask_row = PTT[0:1, :, :].rearrange("p a n -> p (a n)").bitcast(BF16)[:, 0:B * S + B * SC]
        mask_words = XN[0:1, :, :].rearrange("p a n -> p (a n)").bitcast(mybir.dt.int32)[:, 0:(B * S + B * S2) // 4]
        mask_raw = mask_words.bitcast(mybir.dt.uint8)
        orec = sb("orec", [P, 2, UH, TB])
        att = sb("att", [P, NT, D])
        attT = XT
        HL = share[:, 0:4 * B * S].rearrange("p (n t) -> p n t", t=S)
        H0 = stacks[:, :, :].rearrange("p a n -> p (a n)").rearrange("p (n t) -> p n t", t=S)
        HT = stacks[:, :, :].rearrange("p a n -> p (a n)")[:, 0:(2 * NE + 2) * S].rearrange("p (n t) -> p n t", t=S)
        RT = att[:, :, :].rearrange("p t d -> p (t d)")
        sg = PTT
        gb = sb("gb", [P, 2])
        mg = sb("mg", [P, 2, NE])
        EWA = ring[:, 0:(NE + 1) * FE].rearrange("p (e f) -> p e f", f=FE)
        EWB = ring[:, (NE + 1) * FE:2 * (NE + 1) * FE].rearrange("p (e f) -> p e f", f=FE)
        EWD = cstack[:, 0:2 * (NE + 1) * D].rearrange("p (n d) -> p n d", d=D)
        lg = work[:, 9 * B * S2:9 * B * S2 + 10 * NT * NE].rearrange("p (n t e) -> p n t e", n=10, t=NT)
        small = sb("small", [P, 8, NT])
        late = parts[:, :, :, :, :].rearrange("p j k c t -> p (j k c t)").bitcast(FP32)
        watt = late[:, 0:2 * D].rearrange("p (k d) -> p k d", k=2)
        vatt = sb("vatt", [P, 1])
        vrep = sb("vrep", [P, P])
        wi = late[:, 2 * D:8 * D].rearrange("p (k d) -> p k d", k=2)
        uh = late[:, 8 * D:11 * D]
        sbias = sb("sbias", [P, 3])
        KB = B * S2
        EP = work[:, 0:KB].rearrange("p (b s) -> p b s", b=B)
        th = work[:, KB:2 * KB].rearrange("p (b s) -> p b s", b=B)
        ex = work[:, 2 * KB:3 * KB].rearrange("p (b s) -> p b s", b=B)
        EW = work[:, 3 * KB:6 * KB].rearrange("p (b g s) -> p b g s", b=B, g=3)
        prod = work[:, 6 * KB:9 * KB].rearrange("p (g b s) -> p g b s", b=B, g=3)
        GX = share[:, 0:(S + U) * 4 * B].rearrange("p (t g b) -> p t g b", g=4, b=B)
        GS = sb("GS", [P, U, 4, B])
        HR = sb("HR", [P, U, B])
        HO = att[:, :, :].rearrange("p (b t) d -> p b (t d)", b=B)
        ub = sb("ub", [P, B])
        nm = sb("nm", [P, B])
        esum = sb("esum", [P, B])
        erec = sb("erec", [P, B])
        hb = sb("hb", [P, 4, B])
        gr = sb("gr", [P, 3, B])
        hhalf = sb("hhalf", [P, B])
        plus_half = sb("plus_half", [P, B])
        zm = sb("zm", [P, B])
        zeros = sb("zeros", [P, P], BF16)
        tr = sb("tr", [P, B])
        tz = sb("tz", [P, B])
        pre = sb("pre", [P, B])
        cand = sb("cand", [P, B])
        omz = sb("omz", [P, B])
        zt = sb("zt", [P, B])
        zh = sb("zh", [P, B])

        small_in = sem("small_in")
        scan_in = sem("scan_in")
        expert_in = sem("expert_in")
        expert2_in = sem("expert2_in")
        wa_in, wf_in = sem("wa_in"), sem("wf_in")
        const_ready, stack_ones = sem("const_ready"), sem("stack_ones")
        mask_ready, mask_dma = sem("mask_ready"), sem("mask_dma")
        ad_ps, ad_ready, adl_ready = sem("ad_ps"), sem("ad_ready"), sem("adl_ready")
        dve_step = sem("dve_step")
        pool_step = sem("pool_step")
        ln_st, ln_rs, ln_xn = sem("ln_st"), sem("ln_rs"), sem("ln_xn")
        tp_ps, xt_ready = sem("tp_ps"), sem("xt_ready")
        qk_ps, rot_done, hi_done, r1_done, mid_done, lo_done = [
            sem(n) for n in ("qk_ps", "rot_done", "hi_done", "r1_done", "mid_done", "lo_done")]
        stack_wr, stack_rd = sem("stack_wr"), sem("stack_rd")
        v_ps, v_ready = sem("v_ps"), sem("v_ready")
        s1_ps, s1_max, m_ps, m_ready, m_dma = [sem(n) for n in ("s1_ps", "s1_max", "m_ps", "m_ready", "m_dma")]
        s2_ps, s2_exp, pv_done, ot_ready, ot_ps, att_ready = [
            sem(n) for n in ("s2_ps", "s2_exp", "pv_done", "ot_ready", "ot_ps", "att_ready")]
        at_ps, at_ready, pr_ps, x_ready = [sem(n) for n in ("at_ps", "at_ready", "pr_ps", "x_ready")]
        f1_ps, h_ready, f2_ps = [sem(n) for n in ("f1_ps", "h_ready", "f2_ps")]
        layer_done = sem("layer_done")
        out_done, x_done = sem("out_done"), sem("x_done")
        rt_ready, rt_step, rt_exp, lg_ps = [sem(n) for n in ("rt_ready", "rt_step", "rt_exp", "lg_ps")]
        up_ps, up_ready, hid_ready, down_ps, weighed = [sem(n) for n in ("up_ps", "up_ready", "hid_ready", "down_ps", "weighed")]
        ep_ps, ep_ready, gx_ps, gx_ready, gx_zero, gs_ready, ho_ready, ho_ps = [
            sem(n) for n in ("ep_ps", "ep_ready", "gx_ps", "gx_ready", "gx_zero", "gs_ready", "ho_ready", "ho_ps")]
        u_ps, u_ready, h_new, gate_ps, hb_ready = [sem(n) for n in ("u_ps", "u_ready", "h_new", "gate_ps", "hb_ready")]
        th_ready, score_ps, max_ready, ex_ready = [[sem(f"{n}{b}") for b in range(B)]
                                                   for n in ("th_ready", "score_ps", "max_ready", "ex_ready")]
        erec_ready, r_dot, c_dot, r_ready, c_pre, c_ready = [
            [sem(f"{n}{b}") for b in range(B)] for n in ("erec_ready", "r_dot", "c_dot", "r_ready", "c_pre", "c_ready")]
        z_dot, z_scaled, z_pre, z_ready, hh_ready, zt_ready, zm_ready, omz_ready, zh_ready = [
            sem(n) for n in ("z_dot", "z_scaled", "z_pre", "z_ready", "hh_ready", "zt_ready", "zm_ready", "omz_ready", "zh_ready")]
        apart_dve, apart_pe, apart_sp = sem("apart_dve"), sem("apart_pe"), sem("apart_sp")

        block = ctx.enter_context(nc.Block())
        NSMALL = 10

        def wcol(k):
            return WA[:, k * D:(k + 1) * D]

        LN0, XN0, TP0 = 1 + NL * LN_L, NT * (1 + NL * LN_L), NL * TP_L
        N0 = 2 * NE
        N1 = 2 * (NE + 1)

        ATTENDED = B * H + 2

        def slots(kind):
            return B * H + LEAD[kind] + (6 if kind == 0 else 3)

        def evacuated(kind, slot):
            u4 = slot - LEAD[kind] - (UH + TB if kind == 0 else UH + 1)
            return u4 // UH if u4 >= 0 and u4 % UH == 0 and u4 // UH < NU else None

        def post_gpsimd(g, inverse_root):
            inverse_root(LN0 + 1)
            inverse_root(LN0 + 2)
            nc.gpsimd.memset(GX[:, :, 3, :], 0.0)
            nc.gpsimd.memset(GX[:, S:S + U, 0:3, :], 0.0).then_inc(gx_zero, 1)
            inverse_root(LN0 + 3)
            g.wait_ge(gx_ready, 3 * B)
            g.wait_ge(gx_zero, 1)
            nc.gpsimd.tensor_copy(GS[:, :, :, :], GX[:, 0:U, :, :]).then_inc(gs_ready, 2)
            half_u = U // 2
            PTT = nc.gpsimd.tensor_tensor
            with g.Fori(0, S // U) as blk:
                for k in range(U):
                    n = blk * U + (k + 1)
                    g.wait_ge(h_new, n * 2)
                    PTT(hhalf[:, :], HR[:, (k - 1) % U, :], plus_half[:, :], ALU.mult).then_inc(hh_ready, 1)
                    g.wait_ge(z_ready, n)
                    g.wait_ge(hh_ready, n)
                    PTT(zt[:, :], tz[:, :], hhalf[:, :], ALU.mult).then_inc(zt_ready, 1)
                    PTT(zm[:, :], tz[:, :], half[:, 0:B], ALU.mult).then_inc(zm_ready, 1)
                    g.wait_ge(zt_ready, n)
                    PTT(zh[:, :], zt[:, :], hhalf[:, :], ALU.add).then_inc(zh_ready, 1)
                    g.wait_ge(zm_ready, n)
                    PTT(omz[:, :], zm[:, :], plus_half[:, :], ALU.add).then_inc(omz_ready, 1)
                    if (k + 1) % half_u == 0:
                        first, q = k + 1 - half_u, k // half_u
                        g.wait_ge(hb_ready, blk * U + (k + 1))
                        nc.gpsimd.tensor_copy(GS[:, first:k + 1, :, :],
                                              GX[:, bass.ds(blk * U + (U + first), half_u), :, :]).then_inc(gs_ready, 1)
                        g.wait_ge(h_new, blk * (2 * U) + 2 * (k + 2))
                        nc.gpsimd.tensor_copy(HO[:, :, bass.ds(blk * U + first, half_u)],
                                              HR[:, first:k + 1, :].rearrange("p u b -> p b u")).then_inc(ho_ready, 1)
            inverse_root(LN0 + 4)

        def post_scalar(act, turned):
            turned(TP0)
            act.wait_ge(scan_in, 16 * 7)
            for b in range(B):
                act.wait_ge(tp_ps, TP0 + B + b + 1)
                nc.scalar.activation(RT[:, b * S:(b + 1) * S], bank[b][:, :], ACT.Identity, scale=gb[:, 0:1],
                                     bias=gb[:, 1:2]).then_inc(rt_ready, 1)
            act.wait_ge(rt_step, 1)
            nc.scalar.activation(lg[:, 2, :, :], lg[:, 1, :, :], ACT.Exp).then_inc(rt_exp, 1)
            for n in range(B * N0):
                act.wait_ge(up_ps, n + 1)
                nc.scalar.activation(H0[:, n, :], bank[2 + n % 4][:, :], ACT.Gelu).then_inc(up_ready, 1)
            turned(TP0 + 2 * B)
            act.wait_ge(ep_ps, 1)
            nc.scalar.copy(EP, bank[0][:, 0:B * S2].rearrange("p (b s) -> p b s", b=B)).then_inc(ep_ready, 1)
            for b in range(B):
                nc.scalar.copy(EW[:, b, :, :], bank[1 + 6 * b][:, 0:3 * S2].rearrange("p (g s) -> p g s", g=3)).then_inc(ep_ready, 1)
            for n in range(3 * B):
                b, gate = n // 3, n % 3
                act.wait_ge(gx_ps, n + 1)
                nc.scalar.activation(GX[:, 0:S, gate, b], bank[2 + n % 5][:, :], ACT.Identity,
                                     bias=sbias[:, gate:gate + 1]).then_inc(gx_ready, 1)
            with act.Fori(0, S // U) as blk:
                for k in range(U):
                    n = blk * U + (k + 1)
                    act.wait_ge(u_ready, n)
                    for b in range(B):
                        nc.scalar.activation(th[:, b, :], EP[:, b, :], ACT.Tanh, bias=ub[:, b:b + 1]).then_inc(th_ready[b], 1)
                    for b in range(B):
                        act.wait_ge(max_ready[b], n)
                        nc.scalar.activation(ex[:, b, :], bank[b][:, 0:S2], ACT.Exp, bias=nm[:, b:b + 1],
                                             accum_out=esum[:, b:b + 1]).then_inc(ex_ready[b], 1)
                    act.wait_ge(hb_ready, n)
                    for b in range(B):
                        act.wait_ge(erec_ready[b], n)
                        act.wait_ge(r_dot[b], n)
                        nc.scalar.activation(tr[:, b:b + 1], gr[:, 1, b:b + 1], ACT.Tanh, scale=erec[:, b:b + 1],
                                             bias=hb[:, 1, b:b + 1]).then_inc(r_ready[b], 1)
                    act.wait_ge(z_pre, n)
                    nc.scalar.activation(tz[:, :], gr[:, 0, :], ACT.Tanh).then_inc(z_ready, 1)
                    for b in range(B):
                        act.wait_ge(c_dot[b], n)
                        act.wait_ge(c_pre[b], n)
                        nc.scalar.activation(cand[:, b:b + 1], gr[:, 2, b:b + 1], ACT.Tanh, scale=erec[:, b:b + 1],
                                             bias=pre[:, b:b + 1]).then_inc(c_ready[b], 1)
            turned(TP0 + 3 * B)
            act.wait_ge(rt_step, 2)
            nc.scalar.activation(small[:, 1, :], small[:, 0, :], ACT.Tanh, scale=0.5).then_inc(rt_exp, 1)
            for b in range(B):
                act.wait_ge(tp_ps, TP0 + 4 * B + b + 1)
                nc.scalar.copy(RT[:, b * S:(b + 1) * S], bank[b][:, :]).then_inc(rt_ready, 1)
            for n in range(B * N1):
                act.wait_ge(up_ps, B * N0 + n + 1)
                if n >= 2:
                    act.wait_ge(hid_ready, n - 1)
                nc.scalar.activation(sg[:, n % 2, :], bank[2 + 2 * (n % 2)][:, :], ACT.Silu).then_inc(up_ready, 1)

        def post_vector(v, link, run_norm):
            V = nc.vector

            def wide(a):
                return a.unsqueeze(2).to_broadcast([P, NT, NE])

            def greatest(src, dst):
                link(V.tensor_reduce(dst, src, AX.X, ALU.max))

            def first_greatest(p, best, eq, at, hot):
                greatest(p, best)
                link(V.tensor_tensor(eq, p, wide(best), ALU.is_equal))
                link(V.tensor_tensor(eq, eq, rev[:, :, :], ALU.mult))
                greatest(eq, at)
                link(V.tensor_tensor(hot, eq, wide(at), ALU.is_equal))

            def weigh(n_experts, comb, done):
                groups = -(-n_experts // 4)
                for j in range(NT):
                    for q in range(groups):
                        v.wait_ge(down_ps, done + j * groups + q + 1)
                        for e in range(4 * q, min(4 * q + 4, n_experts)):
                            src = bank[6 + (j * groups + q) % 2][:, (e % 4) * D:(e % 4 + 1) * D]
                            if e < NE:
                                ins = V.scalar_tensor_tensor(out=XI[:, j, :], in0=src, scalar=comb[:, j, e:e + 1],
                                                             in1=XI[:, j, :], op0=ALU.mult, op1=ALU.add)
                            else:
                                ins = V.tensor_tensor(XI[:, j, :], XI[:, j, :], src, ALU.add)
                            link(ins)
                        v.sem_inc(weighed, 1)

            link(V.tensor_tensor(XI[:, :, :], XI[:, :, :], Y[:, :, :], ALU.add))
            run_norm(XI, Y, LN0 + 1)
            v.wait_ge(ln_xn, XN0 + NT)
            run_norm(Y, XN, LN0 + 2)
            v.wait_ge(lg_ps, 1)
            link(V.tensor_copy(lg[:, 0, :, :], bank[7][:, 0:NT * NE].rearrange("p (j e) -> p j e", e=NE)))
            greatest(lg[:, 0, :, :], small[:, 0, :])
            V.tensor_tensor(lg[:, 1, :, :], lg[:, 0, :, :], wide(small[:, 0, :]), ALU.subtract).then_inc(rt_step, 1)
            v.wait_ge(rt_exp, 1)
            link(V.tensor_reduce(small[:, 1, :], lg[:, 2, :, :], AX.X, ALU.add))
            link(V.reciprocal(small[:, 2, :], small[:, 1, :]))
            link(V.tensor_tensor(lg[:, 3, :, :], lg[:, 2, :, :], wide(small[:, 2, :]), ALU.mult))
            first_greatest(lg[:, 3, :, :], small[:, 3, :], lg[:, 4, :, :], small[:, 4, :], lg[:, 5, :, :])
            link(V.scalar_tensor_tensor(out=lg[:, 6, :, :], in0=lg[:, 5, :, :], scalar=-2.0, in1=lg[:, 3, :, :],
                                        op0=ALU.mult, op1=ALU.add))
            first_greatest(lg[:, 6, :, :], small[:, 5, :], lg[:, 7, :, :], small[:, 6, :], lg[:, 8, :, :])
            link(V.tensor_tensor(lg[:, 5, :, :], lg[:, 5, :, :], lg[:, 8, :, :], ALU.add))
            link(V.tensor_tensor(lg[:, 9, :, :], lg[:, 5, :, :], lg[:, 3, :, :], ALU.mult))
            v.wait_ge(scan_in, 16 * 7)
            V.tensor_copy(vrep[:, :], vatt[:, 0:1].to_broadcast([P, P]))
            V.tensor_scalar(uh, uh, 0.5, None, ALU.mult)
            V.tensor_scalar(wi[:, :, 0:2 * D], wi[:, :, 0:2 * D], 0.5, None, ALU.mult)
            V.tensor_scalar(sbias[:, 0:2], sbias[:, 0:2], 0.5, None, ALU.mult)
            V.tensor_copy(HR[:, U - 1, :], condT[:, :]).then_inc(h_new, 2)
            weigh(NE, lg[:, 9, :, :], 0)
            run_norm(XI, XN, LN0 + 3)
            scan_vector(v)
            for b in range(B):
                v.wait_ge(ho_ps, b + 1)
                x = XI[:, TB * b:TB * (b + 1), :]
                link(V.tensor_tensor(x, x, bank[b][:, :].rearrange("p (t d) -> p t d", t=TB), ALU.add))
            run_norm(XI, XN, LN0 + 4)
            v.wait_ge(lg_ps, 2)
            link(V.tensor_copy(lg[:, 0, :, :], bank[7][:, 0:NT * NE].rearrange("p (j e) -> p j e", e=NE)))
            first_greatest(lg[:, 0, :, :], small[:, 0, :], lg[:, 1, :, :], small[:, 2, :], lg[:, 9, :, :])
            v.sem_inc(rt_step, 1)
            v.wait_ge(rt_exp, 2)
            link(V.tensor_scalar(small[:, 3, :], small[:, 1, :], 0.5, 0.5, ALU.mult, ALU.add))
            for j in range(NT):
                V.tensor_scalar(Y[:, j, :], XN[:, j, :], small[:, 3, j:j + 1], None, ALU.mult).then_inc(ln_xn, 1)
            for b in range(B):
                for n in range(b * N1, (b + 1) * N1):
                    v.wait_ge(up_ready, B * N0 + n + 1)
                    if n == N1:
                        v.wait_ge(down_ps, 2 * NT + 3 * TB)
                    V.tensor_tensor(HT[:, n % N1, :], sg[:, n % 2, :], bank[3 + 2 * (n % 2)][:, :], ALU.mult).then_inc(hid_ready, 1)
                for j in range(TB * b, TB * (b + 1)):
                    for q in range(3):
                        v.wait_ge(down_ps, 2 * NT + j * 3 + q + 1)
                        for e in range(4 * q, min(4 * q + 4, NE + 1)):
                            src = bank[6 + (j * 3 + q) % 2][:, (e % 4) * D:(e % 4 + 1) * D]
                            if e < NE:
                                ins = V.scalar_tensor_tensor(out=XI[:, j, :], in0=src, scalar=lg[:, 9, j, e:e + 1],
                                                             in1=XI[:, j, :], op0=ALU.mult, op1=ALU.add)
                            else:
                                ins = V.tensor_tensor(XI[:, j, :], XI[:, j, :], src, ALU.add)
                            link(ins)
                        v.sem_inc(weighed, 1)
                v.sem_inc(x_done, 1)

        def scan_vector(v):
            V, TT = nc.vector, nc.vector.tensor_tensor
            half_u = U // 2
            v.wait_ge(ep_ready, 3)
            with v.Fori(0, S // U) as blk:
                for k in range(U):
                    n = blk * U + (k + 1)

                    def dot(gate, b):
                        return V.scalar_tensor_tensor(out=prod[:, gate, b, :], in0=ex[:, b, :], scalar=1.0, in1=EW[:, b, gate, :],
                                                      op0=ALU.mult, op1=ALU.mult, accum_out=gr[:, gate, b:b + 1])

                    def candidate_rest(b):
                        v.wait_ge(r_ready[b], n)
                        V.scalar_tensor_tensor(out=pre[:, b:b + 1], in0=hb[:, 3, b:b + 1], scalar=tr[:, b:b + 1],
                                               in1=hb[:, 2, b:b + 1], op0=ALU.mult, op1=ALU.add).then_inc(c_pre[b], 1)

                    v.wait_ge(u_ps, n)
                    V.tensor_copy(ub[:, :], bank[3][:, 0:B]).then_inc(u_ready, 1)
                    for b in range(B):
                        v.wait_ge(score_ps[b], n)
                        V.tensor_reduce(nm[:, b:b + 1], bank[b][:, 0:S2], AX.X, ALU.max, negate=True).then_inc(max_ready[b], 1)
                    v.wait_ge(gate_ps, n)
                    if k % half_u == 0:
                        v.wait_ge(gs_ready, blk * 2 + (k // half_u + 1))
                    TT(hb[:, :, :], bank[2][:, 0:4 * B].rearrange("p (g b) -> p g b", b=B), GS[:, k, :, :], ALU.add).then_inc(hb_ready, 1)
                    for b in range(B):
                        v.wait_ge(ex_ready[b], n)
                        dot(1, b).then_inc(r_dot[b], 1)
                        V.reciprocal(erec[:, b:b + 1], esum[:, b:b + 1]).then_inc(erec_ready[b], 1)
                        dot(0, b).then_inc(z_dot, 1)
                    v.wait_ge(hb_ready, n)
                    candidate_rest(0)
                    v.wait_ge(z_dot, n * B)
                    for b in range(B):
                        v.wait_ge(erec_ready[b], n)
                    TT(gr[:, 0, :], gr[:, 0, :], erec[:, :], ALU.mult).then_inc(z_scaled, 1)
                    dot(2, 0).then_inc(c_dot[0], 1)
                    v.wait_ge(z_scaled, n)
                    TT(gr[:, 0, :], gr[:, 0, :], hb[:, 0, :], ALU.add).then_inc(z_pre, 1)
                    candidate_rest(1)
                    dot(2, 1).then_inc(c_dot[1], 1)
                    v.wait_ge(zh_ready, n)
                    v.wait_ge(omz_ready, n)
                    if k == half_u:
                        v.wait_ge(ho_ready, blk * 2 + 1)
                    for b in range(B):
                        v.wait_ge(c_ready[b], n)
                        V.scalar_tensor_tensor(out=HR[:, k, b:b + 1], in0=cand[:, b:b + 1], scalar=omz[:, b:b + 1],
                                               in1=zh[:, b:b + 1], op0=ALU.mult, op1=ALU.add).then_inc(h_new, 1)

        def post_tensor(pe, turn):
            mm = nc.tensor.matmul

            def keep_clock(count):
                for _ in range(count):
                    mm(bank[7][:, 0:P], zeros[:, :], zeros[:, :], start=True, stop=True)

            def logits(rt, which):
                for j in range(NT):
                    ins = mm(bank[7][:, j * NE:(j + 1) * NE], rt[:, j * P:(j + 1) * P], mg[:, which, :], start=True, stop=True)
                ins.then_inc(lg_ps, 1)

            def down(b, hidden, n_experts, done):
                groups = -(-n_experts // 4)
                for t in range(TB):
                    for q in range(groups):
                        k = (TB * b + t) * groups + q
                        if k >= 2 or done:
                            pe.wait_ge(weighed, done + k - 1)
                        for e in range(4 * q, min(4 * q + 4, n_experts)):
                            for c in range(2):
                                ins = mm(bank[6 + k % 2][:, (e % 4) * D:(e % 4 + 1) * D], hidden[:, 2 * e + c, t * P:(t + 1) * P],
                                         EWD[:, 2 * e + c, :], start=(c == 0), stop=(c == 1))
                        ins.then_inc(down_ps, 1)

            turn(Y, XN0)
            for b in range(B):
                pe.wait_ge(xt_ready, TP0 + b + 1)
            turn(XN, XN0 + NT)
            pe.wait_ge(rt_ready, B)
            pe.wait_ge(scan_in, 16 * 7)
            logits(RT, 0)
            pe.wait_ge(expert_in, 32)
            for b in range(B):
                for n in range(b * N0, (b + 1) * N0):
                    if n >= 4:
                        pe.wait_ge(up_ready, n - 3)
                    c = n % N0
                    mm(bank[2 + n % 4][:, :], EWA[:, c // 2, (c % 2) * P:(c % 2 + 1) * P], XT[:, b * S:(b + 1) * S],
                       start=True, stop=True).then_inc(up_ps, 1)
            pe.wait_ge(rt_step, 1)
            for b in range(B):
                pe.wait_ge(up_ready, (b + 1) * N0)
                down(b, H0[:, b * N0:(b + 1) * N0, :], NE, 0)
            turn(XN, XN0 + 2 * NT)
            pe.wait_ge(h_new, 2)
            for b in range(B):
                pe.wait_ge(xt_ready, TP0 + B + b + 1)
            for b in range(B):
                mm(bank[0][:, b * S2:(b + 1) * S2], watt[:, 1, :], ctxT[:, b, 0:S2], start=True, stop=True)
            for b in range(B):
                for gate in range(3):
                    ins = mm(bank[1 + 6 * b][:, gate * S2:(gate + 1) * S2], wi[:, 1, gate * D:(gate + 1) * D], ctxT[:, b, 0:S2],
                             start=True, stop=True)
            ins.then_inc(ep_ps, 1)
            for n in range(3 * B):
                b, gate = n // 3, n % 3
                if n >= 5:
                    pe.wait_ge(gx_ready, n - 4)
                mm(bank[2 + n % 5][:, :], wi[:, 0, gate * D:(gate + 1) * D], XT[:, b * S:(b + 1) * S],
                   start=True, stop=True).then_inc(gx_ps, 1)
            pe.wait_ge(ep_ready, 3)
            pe.wait_ge(gx_ready, 3 * B)
            with pe.Fori(0, S // U) as blk:
                for k in range(U):
                    n = blk * U + (k + 1)
                    h = HR[:, (k - 1) % U, :]
                    pe.wait_ge(h_new, n * 2)
                    mm(bank[3][:, 0:B], watt[:, 0, :], h, start=True, stop=True).then_inc(u_ps, 1)
                    mm(bank[2][:, 0:B], uh[:, 0:D], h, start=True, stop=True)
                    mm(bank[2][:, B:2 * B], uh[:, D:2 * D], h, start=True, stop=True)
                    mm(bank[2][:, 2 * B:4 * B], uh[:, 2 * D:3 * D], HR[:, (k - 1) % U:(k - 1) % U + 1, :].to_broadcast([P, 2, B]),
                       start=True, stop=True).then_inc(gate_ps, 1)
                    keep_clock(3)
                    for b in range(B):
                        pe.wait_ge(th_ready[b], n)
                        mm(bank[b][:, 0:S2], vrep[:, :], th[:, b, :], start=True, stop=True).then_inc(score_ps[b], 1)
                    keep_clock(6)
                    for done, count in ((max_ready[0], 8), (ex_ready[0], 6), (r_dot[1], 8), (r_ready[1], 8), (c_dot[1], 8),
                                        (c_pre[1], 4)):
                        pe.wait_ge(done, n)
                        keep_clock(count)
            pe.wait_ge(ho_ready, 2 * (S // U))
            for b in range(B):
                for t in range(TB):
                    ins = nc.tensor.transpose(bank[b][:, t * P:(t + 1) * P], HO[:, b, t * P:(t + 1) * P], ident[:, :])
                ins.then_inc(ho_ps, 1)
            turn(XN, XN0 + 3 * NT)
            pe.wait_ge(xt_ready, TP0 + 3 * B)
            logits(XT, 1)
            turn(Y, XN0 + 4 * NT)
            pe.wait_ge(rt_ready, 2 * B)
            pe.wait_ge(rt_step, 2)
            pe.wait_ge(expert_in, 32 + 48)
            for b in range(B):
                for n in range(b * N1, (b + 1) * N1):
                    if n >= 2:
                        pe.wait_ge(hid_ready, n - 1)
                    c = n % N1
                    cols = slice((c % 2) * P, (c % 2 + 1) * P)
                    src = (RT if c < 2 * NE else XT)[:, b * S:(b + 1) * S]
                    mm(bank[2 + 2 * (n % 2)][:, :], EWA[:, c // 2, cols], src, start=True, stop=True)
                    mm(bank[3 + 2 * (n % 2)][:, :], EWB[:, c // 2, cols], src, start=True, stop=True).then_inc(up_ps, 1)
                pe.wait_ge(hid_ready, (b + 1) * N1)
                down(b, HT, NE + 1, 2 * NT)

        @block.sync
        def _(sp):
            for dst, src in ((XI[:, :, :], x_d.rearrange("b (t p) d -> p (b t) d", p=P)),
                             (ident[:, :], ident_d), (condT[:, :], cond_d), (rot[:, :, :], rot_d),
                             (ctxT[:, :, 0:S2], ctx_d.rearrange("b d s -> d b s")),
                             (rev[:, :, :], rev_d), (NW[:, :, :], nw_d), (NB[:, :, :], nb_d),
                             (mask_words[0:1, 0:B * S // 4], mask_d),
                             (mask_words[0:1, B * S // 4:(B * S + B * S2) // 4], mask2_d)):
                sp.dma_start(dst, src).then_inc(small_in, 16)
            sp.wait_ge(mask_ready, 3)
            sp.wait_ge(const_ready, 1)
            sp.wait_ge(stack_ones, 1)
            for b in range(B):
                sp.dma_start(KS[MASK_ROW:MASK_ROW + 1, b, :, :],
                             mask_row[0:1, b * S:(b + 1) * S].unsqueeze(1).to_broadcast([1, H, S])).then_inc(mask_dma, 16)
            sp.dma_start(KC[MASK_ROW:MASK_ROW + 1, :, :],
                         mask_row[0:1, B * S:].unsqueeze(1).to_broadcast([1, H, B * SC])).then_inc(mask_dma, 16)

            def stack(l, i, n, kinds):
                j = i % 2
                sp.wait_ge(lo_done, l * ITEM_L + RD_AT[i])
                sp.sem_inc(apart_sp, 1)
                k0 = 0 if kinds[0][0] == "q" else 1
                for s in range(NSLOT):
                    if len(kinds) == 2:
                        src = parts[:, j, :, :, :].rearrange("p k c t -> p (k c) t")
                        step = 3 + K_PART[s] - Q_PART[s]
                        src = src[:, Q_PART[s]:Q_PART[s] + step + 1:step, 0:n]
                        dst = scratch[j, s, :, :, 0:n]
                    else:
                        src = parts[:, j, k0, (Q_PART, K_PART)[k0][s], 0:n]
                        dst = scratch[j, s, :, k0, 0:n]
                    sp.dma_start(dst, src).then_inc(stack_wr, 16)
                sp.wait_ge(stack_wr, (l * PARTS_L + i + 1) * NSLOT * 16)
                sp.sem_inc(apart_sp, 1)
                for kind, dst in kinds:
                    sp.dma_start(dst, scratch[j, :, :, 0 if kind == "q" else 1, 0:n].rearrange(
                        "s (d h) t -> (s d) h t", h=H)).then_inc(stack_rd, 16)
                sp.wait_ge(stack_rd, (l * RD_L + RD_AT[i]) * 16)
                sp.sem_inc(apart_sp, 1)

            def maxima(l, u):
                b, h0 = (u % NU) // (H // UH), UH * (u % (H // UH))
                sp.wait_ge(m_ready, (l * UNIT_L + u + 1) * 2)
                sp.sem_inc(apart_sp, 1)
                for r in range(2):
                    sp.dma_start(QS[MAX_ROW + r:MAX_ROW + r + 1, b, h0:h0 + UH, :].rearrange("p h t -> p (h t)"),
                                 mrow[:, u % 2, r, :]).then_inc(m_dma, 16)
                sp.wait_ge(m_dma, (l * UNIT_L + u + 1) * 32)
                sp.sem_inc(apart_sp, 1)

            with sp.Fori(0, NL) as l:
                sp.wait_ge(ln_st, l * LN_L + 1)
                sp.sem_inc(apart_sp, 1)
                sp.dma_start(WA[:, :], wa_d[bass.ds(l, 1), :, :].rearrange("a p n -> p (a n)")).then_inc(wa_in, 16)
                sp.wait_ge(layer_done, l + 1)
                sp.sem_inc(apart_sp, 1)
                for dst, src in ((WF, wf_d), (F1B, f1b_d), (F2B, f2b_d)):
                    sp.dma_start(dst[:, :], src[bass.ds(l, 1), :, :].rearrange("a p n -> p (a n)")).then_inc(wf_in, 16)
                stack(l, 0, B * SC, [("k", KC[0:PROD, :, :])])
                for b in range(B):
                    stack(l, 1 + b, S, [("q", QS[0:PROD, b, :, :]), ("k", KS[0:PROD, b, :, :])])
                for u in range(NU):
                    maxima(l, u)
                for b in range(B):
                    stack(l, 3 + b, S, [("q", QS[0:PROD, b, :, :])])
                for u in range(NU, 2 * NU):
                    maxima(l, u)
            sp.wait_ge(layer_done, NL + 1)
            sp.dma_start(EWA[:, 0:NE, :], w1_d).then_inc(expert_in, 16)
            for dst, src in ((gb[:, :], gb_d), (mg[:, :, :], mg_d), (watt[:, :, :], watt_d), (vatt[:, :], vatt_d),
                             (wi[:, :, :], wi_d), (uh, uh_d), (sbias[:, :], sb_d)):
                sp.dma_start(dst, src).then_inc(scan_in, 16)
            sp.dma_start(EWD[:, 0:2 * NE, :], w2_d).then_inc(expert_in, 16)
            sp.wait_ge(down_ps, 2 * NT)
            for dst, src in ((EWA, eg_d), (EWB, eu_d), (EWD, ed_d)):
                sp.dma_start(dst, src).then_inc(expert_in, 16)
            for b in range(B):
                sp.wait_ge(x_done, b + 1)
                sp.dma_start(out_d[b].rearrange("(t p) d -> p t d", p=P), XI[:, TB * b:TB * (b + 1), :]).then_inc(out_done, 16)
            sp.wait_ge(out_done, 16 * B)

        @block.gpsimd
        def _(g):
            done = {"n": 0}

            def settled(ins):
                done["n"] += 1
                ins.then_inc(pool_step, 1)
                g.wait_ge(pool_step, done["n"])

            settled(nc.gpsimd.memset(stacks[MASK_ROW:MAX_ROW, 0, :], ONES))
            settled(nc.gpsimd.memset(stacks[MAX_ROW:P, 0, :], 0.0))
            settled(nc.gpsimd.memset(cstack[MAX_ROW:P, :], ONES))
            settled(nc.gpsimd.memset(cstack[0:MAX_ROW, :], 0.0))
            nc.gpsimd.memset(half[:, :], -0.5)
            nc.gpsimd.memset(plus_half[:, :], 0.5)
            nc.gpsimd.memset(zeros[:, :], 0.0)
            nc.gpsimd.memset(VP[:, :, :, :], 1.0)
            nc.gpsimd.memset(VC[:, :, :, :], 1.0)
            settled(nc.gpsimd.memset(VT[:, :, :, :, :], 0.0))
            for r in range(UH):
                settled(nc.gpsimd.memset(VT[TAIL * r:TAIL * (r + 1), :, :, r, HD:HD + 1], 1.0))
            nc.gpsimd.memset(ctxT[:, :, S2:SC], 0.0).then_inc(const_ready, 2)
            g.wait_ge(const_ready, 2)

            def inverse_root(n):
                g.wait_ge(ln_st, n)
                nc.gpsimd.tensor_tensor(rstd[:, :], vpe[:, :], half[:, :], ALU.pow).then_inc(ln_rs, 1)

            inverse_root(1)
            g.wait_ge(ad_ready, 2)
            with g.Fori(0, NL) as l:
                g.wait_ge(layer_done, l + 1)
                nc.gpsimd.tensor_copy(ADL[:, :, :, :].rearrange("p n k b -> p (n k b)"),
                                      AD[:, bass.ds(l, 1), :, :, :].rearrange("p l n k b -> p (l n k b)")).then_inc(adl_ready, 1)
                for n in range(LN_L):
                    inverse_root(l * LN_L + n + 2)
            post_gpsimd(g, inverse_root)

        @block.scalar
        def _(act):
            def turned(n, scale=None, bias=None, pre=None):
                for b in range(B):
                    act.wait_ge(tp_ps, n + b + 1)
                    kw = {}
                    if scale is not None:
                        kw = dict(scale=scale(b), bias=bias(b))
                    nc.scalar.activation(XT[:, b * S:(b + 1) * S], bank[b][:, :], ACT.Identity, **kw).then_inc(xt_ready, 1)

            with act.Fori(0, NL) as l:
                def item_cols(m):
                    i, kind, b = ITEMS[m]
                    return i % 2, 0 if kind == "q" else 1, B * SC if i == 0 else S

                def high(m):
                    j, k, n = item_cols(m)
                    act.wait_ge(rot_done, l * ITEM_L + m + 1)
                    if ITEMS[m][0] >= 2:
                        act.wait_ge(stack_wr, (l * PARTS_L + ITEMS[m][0] - 1) * NSLOT * 16)
                    nc.scalar.copy(parts[:, j, k, 0, 0:n], rF[:, m % 3, 0:n]).then_inc(hi_done, 1)

                def middle(m):
                    j, k, n = item_cols(m)
                    act.wait_ge(r1_done, l * ITEM_L + m + 1)
                    nc.scalar.copy(parts[:, j, k, 1, 0:n], rA[:, m % 3, 0:n]).then_inc(mid_done, 1)

                def rotations(ms, between={}):
                    for k in range(len(ms) + 1):
                        if k < len(ms):
                            high(ms[k])
                        if k in between:
                            between[k]()
                        if k >= 1:
                            middle(ms[k - 1])

                def norm(n):
                    act.wait_ge(adl_ready, l + 1)
                    turned(l * TP_L + n * B, lambda b: ADL[:, n, 0, b:b + 1], lambda b: ADL[:, n, 1, b:b + 1])

                act.wait_ge(v_ps, l * V_L + 1)
                nc.scalar.copy(VC[:, :, :, 0:HD], bank[6][:, 0:B * D].rearrange("p (b h d) -> p b h d", b=B, h=H)).then_inc(v_ready, 1)
                act.wait_ge(v_ps, l * V_L + 2)
                for r in range(UH):
                    rows = slice(TAIL * r, TAIL * (r + 1))
                    nc.scalar.copy(VT[rows, :, :, r, 0:HD],
                                   bank[7][rows, 0:B * D].rearrange("p (b u r d) -> p b u r d", b=B, u=H // UH, r=UH)[:, :, :, r, :]
                                   ).then_inc(v_ready, 1)
                norm(0)

                def self_values(b):
                    act.wait_ge(v_ps, l * V_L + 3 + b)
                    nc.scalar.copy(VP[:, TB * b:TB * (b + 1), :, 0:HD],
                                   bank[6 + b][:, :].rearrange("p (t h d) -> p t h d", t=TB, h=H)).then_inc(v_ready, 1)

                rotations([0, 1, 2, 3, 4], {3: lambda: self_values(0)})
                self_values(1)

                def attention(kind):
                    def attended(b):
                        act.wait_ge(at_ps, l * 2 * B + kind * B + b + 1)
                        nc.scalar.copy(attT[:, b * S:(b + 1) * S], bank[1 - b][:, :]).then_inc(at_ready, 1)

                    for slot in range(slots(kind)):
                        j = slot - LEAD[kind]
                        u = evacuated(kind, slot)
                        if u is not None:
                            ku = kind * NU + u
                            act.wait_ge(pv_done, l * PV_L + (UH * u + UH + TB - 1 if kind == 0 else STEPS + u + 1))
                            if ku >= 2:
                                act.wait_ge(ot_ps, l * UNIT_L + ku - 1)
                            nc.scalar.copy(OT[:, u % 2, :], bank[6 + u % 2][:, :]).then_inc(ot_ready, 1)
                        if slot == ATTENDED + 1:
                            attended(0)
                        if not 0 <= j < B * H:
                            continue
                        u = j // UH
                        if kind == 0:
                            for kc in range(TB):
                                act.wait_ge(s2_ps, l * S2_L + TB * j + kc + 1)
                                if kc == 0 and j >= 2:
                                    act.wait_ge(pv_done, l * PV_L + j - 1)
                                nc.scalar.activation(PT[:, PT_AT[kc] + j % (kc + 2), :], bank[4 + kc % 2][:, :], ACT.Exp,
                                                     scale=SCALE).then_inc(s2_exp, 1)
                        else:
                            base = B * H * TB + (UH + 1) * u
                            if j % UH == 0:
                                act.wait_ge(s2_ps, l * S2_L + base + 1)
                                if u >= 2:
                                    act.wait_ge(pv_done, l * PV_L + STEPS + u - 1)
                                nc.scalar.activation(PTT[:, u % 2, :], bank[4 + base % 2][:, :], ACT.Exp,
                                                     scale=SCALE).then_inc(s2_exp, 1)
                            n = base + 1 + j % UH
                            act.wait_ge(s2_ps, l * S2_L + n + 1)
                            if u >= NPT:
                                act.wait_ge(pv_done, l * PV_L + STEPS + u - NPT + 1)
                            else:
                                act.wait_ge(pv_done, l * PV_L + STEPS)
                            nc.scalar.activation(PT[:, u % NPT * UH + j % UH, :], bank[4 + n % 2][:, :], ACT.Exp,
                                                 scale=SCALE).then_inc(s2_exp, 1)
                    attended(1)

                attention(0)
                norm(1)
                rotations([5, 6])
                attention(1)
                norm(2)
                act.wait_ge(wf_in, (l + 1) * 48)
                for n in range(B * 4):
                    act.wait_ge(f1_ps, l * 8 + n + 1)
                    nc.scalar.activation(HL[:, n, :], bank[2 + n % 4][:, :], ACT.Gelu, bias=F1B[:, n % 4:n % 4 + 1]).then_inc(h_ready, 1)
            post_scalar(act, turned)

        @block.vector
        def _(v):
            chain = {"base": 0, "n": 0}
            V = nc.vector

            def link(ins):
                chain["n"] += 1
                ins.then_inc(dve_step, 1)
                v.wait_ge(dve_step, chain["base"] + chain["n"])

            def layer_norm(src, dst):
                for j in range(NT):
                    ins = V.bn_stats(stats[:, j, :], src[:, j, :])
                link(ins)
                v.sem_inc(apart_dve, 1)
                for j in range(NT):
                    ins = V.bn_aggr(mv[:, j, :], stats[:, j, :])
                link(ins)
                V.tensor_scalar(vpe[:, :], mv[:, :, 1], EPS, None, ALU.add).then_inc(ln_st, 1)
                yield
                for j in range(NT):
                    V.tensor_scalar(dst[:, j, :], src[:, j, :], mv[:, j, 0:1], rstd[:, j:j + 1],
                                    ALU.subtract, ALU.mult).then_inc(ln_xn, 1)
                yield

            def run_norm(src, dst, n):
                steps = layer_norm(src, dst)
                next(steps)
                v.wait_ge(ln_rs, n)
                next(steps)

            V.memset(stacks[32:MASK_ROW, 0, :], 0.0)
            V.memset(stacks[0:MAX_ROW, 1, :], 0.0)
            V.memset(stacks[MAX_ROW:P, 1, :], ONES).then_inc(stack_ones, 1)
            v.wait_ge(small_in, 16 * NSMALL)
            v.wait_ge(const_ready, 2)
            link(V.memset(mask_row[:, :], NEG))
            V.tensor_scalar(mask_row[0:1, 0:B * S], mask_raw[0:1, 0:B * S], NEG, None, ALU.mult).then_inc(mask_ready, 1)
            for b in range(B):
                V.tensor_scalar(mask_row[0:1, B * S + b * SC:B * S + b * SC + S2],
                                mask_raw[0:1, B * S + b * S2:B * S + (b + 1) * S2], NEG, None, ALU.mult).then_inc(mask_ready, 1)
            run_norm(XI, Y, 1)
            v.wait_ge(ad_ps, 1)
            ad = AD[:, :, :, :, :].rearrange("p l n k b -> p (l n) k b")
            link(V.tensor_tensor(ad, bank[7][:, 0:3 * NL * 4].rearrange("p (n k b) -> p n k b", k=2, b=B),
                                 NB[:, :, :].unsqueeze(3).to_broadcast([P, 3 * NL, 2, B]), ALU.add))
            V.tensor_scalar(ad[:, :, 0, :], ad[:, :, 0, :], 1.0, None, ALU.add).then_inc(ad_ready, 2)
            v.wait_ge(ln_xn, NT)
            v.sem_inc(layer_done, 1)
            before = chain["n"]

            with v.Fori(0, NL) as l:
                chain["base"] = l * DVE_L + before
                chain["n"] = 0

                def item_cols(m):
                    i, kind, b = ITEMS[m]
                    return i % 2, 0 if kind == "q" else 1, B * SC if i == 0 else S

                def rotate(m):
                    j, k, n = item_cols(m)
                    r = m % 3
                    c = 2 + 2 * (m % 2)
                    if m >= 3:
                        v.wait_ge(lo_done, l * ITEM_L + m - 2)
                    v.wait_ge(qk_ps, l * ITEM_L + m + 1)
                    for t, src, dst in ((0, bank[c], rA), (1, bank[c + 1], rB)):
                        if ITEMS[m][0] == 0:
                            for b in range(B):
                                ins = V.tensor_tensor(dst[:, r, b * SC:(b + 1) * SC], src[:, b * SC:(b + 1) * SC],
                                                      rot[:, t, 0:SC], ALU.mult)
                        else:
                            ins = V.tensor_tensor(dst[:, r, 0:n], src[:, 0:n], rot[:, t, 0:n], ALU.mult)
                    link(ins)
                    V.tensor_tensor(rF[:, r, 0:n], rA[:, r, 0:n], rB[:, r, 0:n], ALU.add).then_inc(rot_done, 1)

                def residue(m):
                    j, k, n = item_cols(m)
                    v.wait_ge(hi_done, l * ITEM_L + m + 1)
                    v.wait_ge(rot_done, l * ITEM_L + m + 1)
                    V.tensor_tensor(rA[:, m % 3, 0:n], rF[:, m % 3, 0:n], parts[:, j, k, 0, 0:n], ALU.subtract).then_inc(r1_done, 1)

                def low(m):
                    j, k, n = item_cols(m)
                    v.wait_ge(mid_done, l * ITEM_L + m + 1)
                    v.wait_ge(r1_done, l * ITEM_L + m + 1)
                    ins = V.tensor_tensor(parts[:, j, k, 2, 0:n], rA[:, m % 3, 0:n], parts[:, j, k, 1, 0:n], ALU.subtract)
                    ins.then_inc(lo_done, 1)

                def rotations(ms):
                    for k in range(len(ms) + 2):
                        if k < len(ms):
                            rotate(ms[k])
                        if 0 <= k - 1 < len(ms):
                            residue(ms[k - 1])
                        if k >= 2:
                            low(ms[k - 2])

                def update(kind, b):
                    v.wait_ge(pr_ps, l * 2 * B + kind * B + b + 1)
                    y = Y[:, TB * b:TB * (b + 1), :]
                    return V.tensor_tensor(y, y, bank[1 - b][:, :].rearrange("p (t d) -> p t d", t=TB), ALU.add)

                def attention(kind):
                    def normalise(u):
                        ku = kind * NU + u
                        b, h0 = u // (H // UH), UH * (u % (H // UH))
                        v.wait_ge(ot_ps, l * UNIT_L + ku + 1)
                        o = bank[0][:, :].rearrange("p (t h c) -> p h t c", h=UH, t=TB)
                        link(V.reciprocal(orec[:, u % 2, :, :], o[:, :, :, HD]))
                        V.tensor_tensor(att[:, TB * b:TB * (b + 1), h0 * HD:(h0 + UH) * HD].rearrange("p t (h d) -> p h t d", h=UH),
                                        o[:, :, :, 0:HD],
                                        orec[:, u % 2, :, :].unsqueeze(3).to_broadcast([P, UH, TB, HD]),
                                        ALU.mult).then_inc(att_ready, 1)

                    def maxima(u):
                        ku = kind * NU + u
                        v.wait_ge(m_ps, l * UNIT_L + ku + 1)
                        if ku >= 2:
                            v.wait_ge(m_dma, (l * UNIT_L + ku - 1) * 32)
                        m = bank[1][0:UH * TB, 0:P]
                        V.tensor_copy(mrow[:, u % 2, 0, :], m).then_inc(m_ready, 1)
                        v.wait_ge(m_ready, (l * UNIT_L + ku) * 2 + 1)
                        V.tensor_tensor(mrow[:, u % 2, 1, :], m, mrow[:, u % 2, 0, :], ALU.subtract).then_inc(m_ready, 1)

                    for slot in range(slots(kind)):
                        if slot >= 5 and slot % UH == 5 % UH and (slot - 5) // UH < NU:
                            maxima((slot - 5) // UH)
                        if slot < B * H:
                            u, hl = slot // UH, slot % UH
                            if hl == 0 and kind * NU + u >= 2:
                                v.wait_ge(m_ps, l * UNIT_L + kind * NU + u - 1)
                            if kind == 0:
                                for qt in range(TB):
                                    n = TB * slot + qt
                                    v.wait_ge(s1_ps, l * S1_L + n + 1)
                                    V.tensor_reduce(nmax[:, u % 2, hl * TB + qt:hl * TB + qt + 1], bank[2 + n % 2][:, :],
                                                    AX.X, ALU.max, negate=True).then_inc(s1_max, 1)
                            else:
                                for qp in range(2):
                                    n = B * H * TB + 2 * slot + qp
                                    v.wait_ge(s1_ps, l * S1_L + n + 1)
                                    V.tensor_reduce(nmax[:, u % 2, hl * TB + 2 * qp:hl * TB + 2 * qp + 2],
                                                    bank[2 + n % 2][:, :].rearrange("p (t k) -> p t k", t=2)[:, :, 0:S2],
                                                    AX.X, ALU.max, negate=True).then_inc(s1_max, 1)
                        u = evacuated(kind, slot - 1)
                        if u is not None:
                            normalise(u)
                        if slot == ATTENDED + 2:
                            update(kind, 0).then_inc(x_ready, 1)
                    link(update(kind, 1))
                    v.wait_ge(x_ready, l * 2 + kind + 1)

                run_norm(Y, XN, l * LN_L + 2)
                rotations([0, 1, 2, 3, 4])
                attention(0)
                run_norm(Y, XN, l * LN_L + 3)
                rotations([5, 6])
                attention(1)
                run_norm(Y, XN, l * LN_L + 4)
                v.wait_ge(wf_in, (l + 1) * 48)
                for b in range(B):
                    v.wait_ge(f2_ps, l * B + b + 1)
                    y = Y[:, TB * b:TB * (b + 1), :]
                    link(V.tensor_tensor(y, y, bank[6 + b][:, :].rearrange("p (t d) -> p t d", t=TB), ALU.add))
                    link(V.tensor_tensor(y, y, F2B[:, :].unsqueeze(1).to_broadcast([P, TB, D]), ALU.add))
                v.sem_inc(layer_done, 1)
                assert chain["n"] == DVE_L, chain["n"]
            chain["base"], chain["n"] = NL * DVE_L + before, 0
            post_vector(v, link, run_norm)

        @block.tensor
        def _(pe):
            mm = nc.tensor.matmul
            pe.wait_ge(small_in, 16 * NSMALL)
            for i in range(3 * NL):
                for k in range(2):
                    c = (2 * i + k) * B
                    ins = mm(bank[7][:, c:c + B], NW[:, i, k * D:(k + 1) * D], condT[:, :], start=True, stop=True)
            ins.then_inc(ad_ps, 1)
            pe.wait_ge(const_ready, 2)
            pe.wait_ge(ad_ready, 2)

            def turn(src, xn_before, dst=bank, after=None):
                for b in range(B):
                    for t in range(TB):
                        j = TB * b + t
                        pe.wait_ge(ln_xn, xn_before + j + 1)
                        ins = nc.tensor.transpose(bank[b][:, t * P:(t + 1) * P], src[:, j, :], ident[:, :])
                    ins.then_inc(tp_ps, 1)

            pe.wait_ge(mask_dma, 48)
            with pe.Fori(0, NL) as l:
                def project(m, pair, src):
                    i, kind, b = ITEMS[m]
                    c = 2 + 2 * (m % 2)
                    if m >= 2:
                        pe.wait_ge(rot_done, l * ITEM_L + m - 1)
                    n = B * SC if i == 0 else S
                    mm(bank[c][:, 0:n], wcol(pair[0]), src, start=True, stop=True)
                    mm(bank[c + 1][:, 0:n], wcol(pair[1]), src, start=True, stop=True).then_inc(qk_ps, 1)

                def attention(kind):
                    k_stack = KS if kind == 0 else KC

                    def first(j, i):
                        b, h = j // H, j % H
                        if kind == 0:
                            n = TB * j + i
                            if n >= 2:
                                pe.wait_ge(s1_max, l * S1_L + n - 1)
                            mm(bank[2 + n % 2][:, :], QS[0:ROWS1, b, h, i * P:(i + 1) * P],
                               KS[0:ROWS1, b, h, :], start=True, stop=True).then_inc(s1_ps, 1)
                        else:
                            n = B * H * TB + 2 * j + i // 2
                            if i % 2 == 0:
                                pe.wait_ge(s1_max, l * S1_L + n - 1)
                            ins = mm(bank[2 + n % 2][:, 256 * (i % 2):256 * (i % 2) + S2],
                                     QS[0:ROWS1, b, h, i * P:(i + 1) * P],
                                     KC[0:ROWS1, h, b * SC:b * SC + S2], start=True, stop=True)
                            if i % 2:
                                ins.then_inc(s1_ps, 1)

                    def second(j, i):
                        b, h, u = j // H, j % H, j // UH
                        q = QS[0:P, b, h, :]
                        if j % UH == 0 and i == 0:
                            pe.wait_ge(m_dma, (l * UNIT_L + kind * NU + u + 1) * 32)
                        if kind == 0:
                            n = TB * j + i
                            if n >= 2:
                                pe.wait_ge(s2_exp, l * S2_L + n - 1)
                            mm(bank[4 + n % 2][:, :], KS[0:P, b, h, i * P:(i + 1) * P], q,
                               start=True, stop=True).then_inc(s2_ps, 1)
                        elif i == 0:
                            n = B * H * TB + (UH + 1) * u
                            if j % UH == 0:
                                pe.wait_ge(s2_exp, l * S2_L + n - 1)
                                pe.sem_inc(apart_pe, 1)
                                for hl in range(UH):
                                    ins = mm(bank[4 + n % 2][TAIL * hl:TAIL * (hl + 1), :],
                                             KC[0:P, h + hl, b * SC + P:(b + 1) * SC],
                                             QS[0:P, b, h + hl, :], start=True, stop=True)
                                ins.then_inc(s2_ps, 1)
                            n += 1 + j % UH
                            pe.wait_ge(s2_exp, l * S2_L + n - 1)
                            mm(bank[4 + n % 2][:, :], KC[0:P, h, b * SC:b * SC + P], q,
                               start=True, stop=True).then_inc(s2_ps, 1)

                    def bank_free(u):
                        if kind * NU + u >= 2:
                            pe.wait_ge(ot_ready, l * UNIT_L + kind * NU + u - 1)

                    def values_self(step):
                        pairs = [(step - kc, kc) for kc in range(TB) if 0 <= step - kc < B * H]
                        if step % UH == 0 and step < B * H:
                            bank_free(step // UH)
                        pe.wait_ge(s2_exp, l * S2_L + max(TB * j + kc for j, kc in pairs) + 1)
                        for j, kc in pairs:
                            hl = j % UH
                            ins = mm(bank[6 + j // UH % 2][HC * hl:HC * hl + HD + 1, :], VP[:, TB * (j // H) + kc, j % H, :],
                                     PT[:, PT_AT[kc] + j % (kc + 2), :], start=(kc == 0), stop=(kc == TB - 1))
                        ins.then_inc(pv_done, 1)

                    def values_cross(u):
                        b, g = u // (H // UH), u % (H // UH)
                        bank_free(u)
                        pe.wait_ge(s2_exp, l * S2_L + B * H * TB + (UH + 1) * (u + 1))
                        mm(bank[6 + u % 2][:, :], VT[:, b, g, :, :].rearrange("p r c -> p (r c)"), PTT[:, u % 2, :],
                           start=True, stop=False)
                        for r in range(UH):
                            ins = mm(bank[6 + u % 2][HC * r:HC * r + HD + 1, :], VC[:, b, UH * g + r, :],
                                     PT[:, u % NPT * UH + r, :], start=False, stop=True)
                        ins.then_inc(pv_done, 1)

                    def turn_values(u):
                        ku = kind * NU + u
                        pe.wait_ge(ot_ready, l * UNIT_L + ku + 1)
                        if ku >= 1:
                            pe.wait_ge(att_ready, l * UNIT_L + ku)
                        for t in range(TB):
                            ins = nc.tensor.transpose(bank[0][:, t * P:(t + 1) * P], OT[:, u % 2, t * P:(t + 1) * P], ident[:, :])
                        ins.then_inc(ot_ps, 1)

                    def attended(b):
                        pe.wait_ge(att_ready, l * UNIT_L + kind * NU + (b + 1) * (H // UH))
                        if b == 0:
                            pe.wait_ge(m_ready, (l * UNIT_L + (kind + 1) * NU) * 2)
                        for t in range(TB):
                            ins = nc.tensor.transpose(bank[1 - b][:, t * P:(t + 1) * P], att[:, TB * b + t, :], ident[:, :])
                        ins.then_inc(at_ps, 1)

                    def output(b):
                        pe.wait_ge(at_ready, l * 2 * B + kind * B + b + 1)
                        for t in range(TB):
                            ins = mm(bank[1 - b][:, t * P:(t + 1) * P], attT[:, b * S + t * P:b * S + (t + 1) * P],
                                     wcol(WO if kind == 0 else CO), start=True, stop=True)
                        ins.then_inc(pr_ps, 1)

                    for slot in range(slots(kind)):
                        if slot == ATTENDED:
                            attended(0)
                        if slot == ATTENDED + 1:
                            output(0)
                        j = slot - LEAD[kind]
                        for i in range(TB):
                            if slot < B * H:
                                if i == 0 and slot % H == 0:
                                    at = RD_AT[(1 if kind == 0 else 3) + slot // H]
                                    pe.wait_ge(stack_rd, (l * RD_L + at) * 16)
                                first(slot, i)
                            if 0 <= j < B * H:
                                second(j, i)
                        if kind == 0 and 1 <= j <= STEPS:
                            values_self(j - 1)
                        if kind == 1 and j >= UH and j % UH == 0 and j // UH <= NU:
                            values_cross(j // UH - 1)
                        if slot >= UH and slot % UH == 0 and slot // UH <= NU:
                            u = slot // UH - 1
                            ku = kind * NU + u
                            pe.wait_ge(s1_max, l * S1_L + (TB * UH * (u + 1) if kind == 0 else B * H * TB + 2 * UH * (u + 1)))
                            if ku >= 1:
                                pe.wait_ge(m_ready, (l * UNIT_L + ku) * 2)
                            nc.tensor.transpose(bank[1][0:UH * TB, 0:P], nmax[:, u % 2, :], ident[:, :]).then_inc(m_ps, 1)
                        u = evacuated(kind, slot)
                        if u is not None:
                            turn_values(u)
                    attended(1)
                    output(1)

                pe.wait_ge(wa_in, (l + 1) * 16)
                project(0, (CK, CKR), ctxT[:, :, :].rearrange("p b s -> p (b s)"))
                for b in range(B):
                    ins = mm(bank[6][:, b * D:(b + 1) * D], ctxT[:, b, 0:P], wcol(CV), start=True, stop=True)
                ins.then_inc(v_ps, 1)
                for b in range(B):
                    for j in range(4):
                        ins = mm(bank[7][TAIL * j:TAIL * (j + 1), b * D:(b + 1) * D], ctxT[:, b, P:SC], wcol(CV),
                                 start=True, stop=True)
                ins.then_inc(v_ps, 1)
                turn(XN, l * XN_L + NT)
                for b in range(B):
                    pe.wait_ge(xt_ready, l * TP_L + b + 1)
                    xt = XT[:, b * S:(b + 1) * S]
                    project(1 + 2 * b, (WQ, WQR), xt)
                    project(2 + 2 * b, (WK, WKR), xt)
                    pe.wait_ge(v_ready, l * VR_L + 1 + UH * b)
                    for t in range(TB):
                        ins = mm(bank[6 + b][:, t * P:(t + 1) * P], XT[:, b * S + t * P:b * S + (t + 1) * P], wcol(WV),
                                 start=True, stop=True)
                    ins.then_inc(v_ps, 1)
                pe.wait_ge(rot_done, l * ITEM_L + 5)
                pe.wait_ge(v_ready, l * VR_L + VR_L)
                attention(0)
                turn(XN, l * XN_L + 2 * NT)
                for b in range(B):
                    pe.wait_ge(xt_ready, l * TP_L + B + b + 1)
                    project(5 + b, (CQ, CQR), XT[:, b * S:(b + 1) * S])
                pe.wait_ge(rot_done, l * ITEM_L + 7)
                attention(1)
                turn(XN, l * XN_L + 3 * NT)
                pe.wait_ge(wf_in, (l + 1) * 48)
                for b in range(B):
                    pe.wait_ge(xt_ready, l * TP_L + 2 * B + b + 1)
                    for fc in range(4):
                        n = 4 * b + fc
                        if n >= 4:
                            pe.wait_ge(h_ready, l * 8 + n - 3)
                        mm(bank[2 + n % 4][:, :], WF[:, fc * P:(fc + 1) * P], XT[:, b * S:(b + 1) * S],
                           start=True, stop=True).then_inc(f1_ps, 1)
                for b in range(B):
                    pe.wait_ge(h_ready, l * 8 + 4 * (b + 1))
                    for t in range(TB):
                        for fc in range(4):
                            ins = mm(bank[6 + b][:, t * P:(t + 1) * P], HL[:, 4 * b + fc, t * P:(t + 1) * P],
                                     WF[:, DFF + fc * D:DFF + (fc + 1) * D], start=(fc == 0), stop=(fc == 3))
                    ins.then_inc(f2_ps, 1)
                pe.wait_ge(layer_done, l + 2)
            post_tensor(pe, turn)


def tables():
    half = HD // 2
    inv = (1.0 / 10000.0 ** (np.arange(half, dtype=np.float32) / half)).astype(np.float32)
    ang = np.arange(S, dtype=np.float32)[:, None] * inv
    cos, sin = np.cos(ang).astype(np.float32), np.sin(ang).astype(np.float32)
    rot = np.zeros((HD, H, 2, S), np.float32)
    for d in range(HD):
        rot[d, :, 0] = cos[:, d % half]
        rot[d, :, 1] = -sin[:, d] if d < half else sin[:, d - half]
    rev = np.broadcast_to(NE - np.arange(NE, dtype=np.float32), (P, NT, NE))
    return rot.reshape(P, 2, S), np.eye(P, dtype=np.float32), np.ascontiguousarray(rev)


def layout(a):
    def turned(w):
        return np.swapaxes(w, -1, -2)

    def by_channel(w, swap=False):
        w = w.reshape(NL, H, HD, D)
        if swap:
            w = np.concatenate([w[:, :, HD // 2:], w[:, :, :HD // 2]], axis=2)
        return turned(w.transpose(0, 2, 1, 3).reshape(NL, D, D))

    qkv, cq, ck = a["L0_xcond_qkv_w"], a["L0_xcond_cq_w"], a["L0_xcond_ck_w"]
    wq, wk, wv = qkv[:, :D], qkv[:, D:2 * D], qkv[:, 2 * D:]
    wa = np.concatenate([by_channel(wq), by_channel(wq, True), by_channel(wk), by_channel(wk, True), turned(wv),
                         turned(a["L0_xcond_so_w"]), by_channel(cq), by_channel(cq, True), by_channel(ck),
                         by_channel(ck, True), turned(a["L0_xcond_cv_w"]), turned(a["L0_xcond_co_w"])], axis=2)
    f1, f2 = turned(a["L0_xcond_f1_w"]), turned(a["L0_xcond_f2_w"])
    wf = np.concatenate([f1, f2.reshape(NL, 4, P, D).transpose(0, 2, 1, 3).reshape(NL, P, 4 * D)], axis=2)
    nw = np.stack([turned(a[f"L0_xcond_n{n}_w"]) for n in (1, 2, 3)], axis=1).reshape(3 * NL, D, 2 * D).transpose(1, 0, 2)
    nb = np.stack([a[f"L0_xcond_n{n}_b"] for n in (1, 2, 3)], axis=1).reshape(3 * NL, 2, D).transpose(2, 0, 1)
    rot, ident, rev = tables()
    f2b = np.broadcast_to(a["L0_xcond_f2_b"][:, None, :], (NL, P, D))
    w1 = a["L0_ffn_w1"].transpose(2, 0, 1)
    w2 = turned(a["L0_ffn_w2"]).reshape(NE, 2, P, D).transpose(2, 0, 1, 3).reshape(P, 2 * NE, D)
    eg = np.concatenate([a["L1_ffn_rt_gate"], a["L1_ffn_sh_gate"][None]]).transpose(1, 0, 2)
    eu = np.concatenate([a["L1_ffn_rt_up"], a["L1_ffn_sh_up"][None]]).transpose(1, 0, 2)
    ed = np.concatenate([a["L1_ffn_rt_down"], a["L1_ffn_sh_down"][None]]).reshape(NE + 1, 2, P, D)
    ed = ed.transpose(2, 0, 1, 3).reshape(P, 2 * (NE + 1), D)
    return {
        "x": a["x"], "cond": a["cond_1024"].T, "ctx": turned(a["ctx_1024"]), "mask": a["mask_BxS_bf0"].reshape(-1).view(np.int32)[None],
        "mask2": a["mask_BxS2_bf0"].reshape(-1).view(np.int32)[None], "rot": rot, "ident": ident, "rev": rev, "nw": nw, "nb": nb,
        "wa": wa, "wf": wf, "f1b": a["L0_xcond_f1_b"].reshape(NL, 4, P).transpose(0, 2, 1), "f2b": f2b,
        "gb": np.stack([a["L0_ffn_ln_gamma"], a["L0_ffn_ln_beta"]], axis=1),
        "mg": np.stack([a["L0_ffn_gate_w"].T, a["L1_ffn_gate_w"]], axis=1), "w1": w1, "w2": w2,
        "watt": a["L1_xcond_W_att"].reshape(2, D, D).transpose(1, 0, 2), "vatt": a["L1_xcond_V_att"],
        "wi": a["L1_xcond_Wi"].reshape(2, D, 3 * D).transpose(1, 0, 2), "uh": a["L1_xcond_Uh"],
        "sb": a["L1_xcond_b"].reshape(3, D).T, "rgate": a["L1_ffn_gate_w"], "eg": eg, "eu": eu, "ed": ed,
    }


def kernel(**inputs):
    import concourse.bacc as bacc
    from concourse.bass_utils import run_bass_kernel_spmd

    nc = bacc.Bacc("TRN2", target_bir_lowering=False, num_devices=1)
    arrays, args = {}, []
    for name, a in layout({k: np.asarray(v) for k, v in inputs.items()}).items():
        a = np.ascontiguousarray(a)
        arrays[f"in_{name}"] = a
        args.append(nc.dram_tensor(f"in_{name}", a.shape, mybir.dt.from_np(a.dtype), kind="ExternalInput").ap())
    args.append(nc.dram_tensor("out", (B, S, D), FP32, kind="ExternalOutput").ap())
    build(nc, *args)
    return run_bass_kernel_spmd(nc, [arrays], core_ids=[0]).results[0]["out"]
```

```python
from contextlib import ExitStack

import numpy as np
import concourse.bass as bass
from concourse import mybir

FP32 = mybir.dt.float32
BF16 = mybir.dt.bfloat16
ALU = mybir.AluOpType
ACT = mybir.ActivationFunctionType
AX = mybir.AxisListType

P = 128
B, S, S2, D = 2, 512, 154, 128
NL, H, HD = 6, 16, 8
DFF = 512
NE, FE = 8, 256
EPS = 1e-5
NT = B * S // P
TB = S // P
TAIL = 32
SC = P + TAIL
NEG = -1.0e30
ONES = float(np.array([0x3F803F80], np.uint32).view(np.float32)[0])
SCALE = 1.0 / float(np.sqrt(np.float32(HD)))

Q_PART = [0, 1, 2, 0, 1, 0]
K_PART = [0, 0, 0, 1, 1, 2]
NSLOT = len(Q_PART)
PROD = NSLOT * HD
MASK_ROW = 64
MAX_ROW = 96
ROWS1 = MAX_ROW

WQ, WQR, WK, WKR, WV, WO, CQ, CQR, CK, CKR, CV, CO = range(12)

LEAD = [6, 12]
UH = 4
NU = B * H // UH
NPT = 3
PT_AT = [0, 2, 5, 9]
PT_TILES = 14
HC = 32
U = 32

LN_L, XN_L, TP_L = 3, 3 * NT, 3 * B
PARTS_L = 5
CTX = 2
ITEMS = [(0, "q", 0), (0, "k", 0), (1, "q", 1), (1, "k", 1), (CTX, "k", 0), (3, "q", 0), (4, "q", 1)]
ITEM_L = len(ITEMS)
RD_L, RD_AT = 7, [2, 4, 5, 6, 7]
S1_L = B * H * TB + B * H * 2
S2_L = B * H * TB + B * H + NU
V_L, VR_L, UNIT_L = 4, 7, 2 * NU
STEPS = B * H + TB - 1
PV_L = STEPS + NU
DVE_L = 41


def build(nc, x_d, cond_d, ctx_d, mask_d, mask2_d, rot_d, ident_d, rev_d, nw_d, nb_d, wa_d, wf_d, f1b_d, f2b_d,
          gb_d, mg_d, w1_d, w2_d, watt_d, vatt_d, wi_d, uh_d, sb_d, eg_d, eu_d, ed_d, out_d):
    ctx = ExitStack()
    with ctx:
        def sb(name, shape, dt=FP32):
            return ctx.enter_context(nc.sbuf_tensor(name, shape, dt))

        def sem(name):
            return ctx.enter_context(nc.semaphore(name))

        bank = [ctx.enter_context(nc.psum_tensor(f"bank{i}", [P, 512], FP32)) for i in range(8)]
        scratch = nc.dram_tensor("stack_scratch", (2, NSLOT, P, 2, S), BF16, kind="Internal").ap()

        ident = sb("ident", [P, P])
        rot = sb("rot", [P, 2, S])
        rev = sb("rev", [P, NT, NE])
        half = sb("half", [P, NT])
        XI = sb("XI", [P, NT, D])
        Y = sb("Y", [P, NT, D])
        XN = sb("XN", [P, NT, D])
        XT = sb("XT", [P, B * S])
        condT = sb("condT", [P, B])
        ctxT = sb("ctxT", [P, B, SC])
        stats = sb("stats", [P, NT, 6])
        mv = sb("mv", [P, NT, 2])
        vpe = sb("vpe", [P, NT])
        rstd = sb("rstd", [P, NT])
        stacks = sb("stacks", [P, 2, H * B * S // 2])
        share = sb("share", [P, 3 * NL * 2 * D])
        NW = share[:, :].rearrange("p (n k) -> p n k", k=2 * D)
        NB = sb("NB", [P, 3 * NL, 2])
        AD = sb("AD", [P, NL, 3, 2, B])
        ADL = sb("ADL", [P, 3, 2, B])
        WA = sb("WA", [P, 12 * D])
        WF = sb("WF", [P, 2 * DFF])
        F1B = sb("F1B", [P, 4])
        F2B = sb("F2B", [P, D])
        QS = stacks[0:P, 0, :].bitcast(BF16).rearrange("p (b h t) -> p b h t", b=B, h=H)
        KS = stacks[0:P, 1, :].bitcast(BF16).rearrange("p (b h t) -> p b h t", b=B, h=H)
        cstack = sb("cstack", [P, H * B * SC // 2])
        KC = cstack[0:P, :].bitcast(BF16).rearrange("p (h t) -> p h t", h=H)
        parts = sb("parts", [P, 2, 2, 3, S], BF16)
        work = sb("work", [P, 9 * S])
        rA, rB, rF = [work[:, 3 * S * i:3 * S * (i + 1)].rearrange("p (r t) -> p r t", r=3) for i in range(3)]
        VP = sb("VP", [P, NT, H, HD + 1])
        VC = sb("VC", [P, B, H, HD + 1])
        VT = sb("VT", [P, B, H // UH, UH, HC])
        nmax = sb("nmax", [P, 2, UH * TB])
        mrow = sb("mrow", [UH * TB, 2, 2, P], BF16)
        ring = sb("ring", [P, PT_TILES * S])
        PT = ring[:, :].rearrange("p (n q) -> p n q", q=S)
        OT = sb("OT", [P, 2, S])
        PTT = sb("PTT", [P, 2, S])
        mask_row = PTT[0:1, :, :].rearrange("p a n -> p (a n)").bitcast(BF16)[:, 0:B * S + B * SC]
        mask_words = XN[0:1, :, :].rearrange("p a n -> p (a n)").bitcast(mybir.dt.int32)[:, 0:(B * S + B * S2) // 4]
        mask_raw = mask_words.bitcast(mybir.dt.uint8)
        orec = sb("orec", [P, 2, UH, TB])
        att = sb("att", [P, NT, D])
        attT = XT
        HL = share[:, 0:4 * B * S].rearrange("p (n t) -> p n t", t=S)
        H0 = stacks[:, :, :].rearrange("p a n -> p (a n)").rearrange("p (n t) -> p n t", t=S)
        HT = stacks[:, :, :].rearrange("p a n -> p (a n)")[:, 0:(2 * NE + 2) * S].rearrange("p (n t) -> p n t", t=S)
        RT = att[:, :, :].rearrange("p t d -> p (t d)")
        sg = PTT
        gb = sb("gb", [P, 2])
        mg = sb("mg", [P, 2, NE])
        EWA = ring[:, 0:(NE + 1) * FE].rearrange("p (e f) -> p e f", f=FE)
        W1 = work[:, 0:NE * FE].rearrange("p (e f) -> p e f", f=FE)
        EWB = ring[:, (NE + 1) * FE:2 * (NE + 1) * FE].rearrange("p (e f) -> p e f", f=FE)
        EWD = cstack[:, 0:2 * (NE + 1) * D].rearrange("p (n d) -> p n d", d=D)
        lg = work[:, 9 * B * S2:9 * B * S2 + 10 * NT * NE].rearrange("p (n t e) -> p n t e", n=10, t=NT)
        small = sb("small", [P, 8, NT])
        late = parts[:, :, :, :, :].rearrange("p j k c t -> p (j k c t)").bitcast(FP32)
        watt = late[:, 0:2 * D].rearrange("p (k d) -> p k d", k=2)
        vatt = sb("vatt", [P, 1])
        vrep = late[:, 11 * D + U * 5 * B:12 * D + U * 5 * B]
        wi = late[:, 2 * D:8 * D].rearrange("p (k d) -> p k d", k=2)
        uh = late[:, 8 * D:11 * D]
        sbias = sb("sbias", [P, 3])
        KB = B * S2
        EP = work[:, 0:KB].rearrange("p (b s) -> p b s", b=B)
        th = work[:, KB:2 * KB].rearrange("p (b s) -> p b s", b=B)
        ex = work[:, 2 * KB:3 * KB].rearrange("p (b s) -> p b s", b=B)
        EW = work[:, 3 * KB:6 * KB].rearrange("p (b g s) -> p b g s", b=B, g=3)
        prod = work[:, 6 * KB:9 * KB].rearrange("p (g b s) -> p g b s", b=B, g=3)
        GX = share[:, 0:(S + U) * 4 * B].rearrange("p (t g b) -> p t g b", g=4, b=B)
        GS = late[:, 11 * D:11 * D + U * 4 * B].rearrange("p (t g b) -> p t g b", g=4, b=B)
        HR = late[:, 11 * D + U * 4 * B:11 * D + U * 5 * B].rearrange("p (t b) -> p t b", b=B)
        HO = att[:, :, :].rearrange("p (b t) d -> p b (t d)", b=B)
        ub = sb("ub", [P, B])
        nm = sb("nm", [P, B])
        esum = sb("esum", [P, B])
        erec = sb("erec", [P, B])
        hb = sb("hb", [P, 4, B])
        gr = sb("gr", [P, 3, B])
        hhalf = sb("hhalf", [P, B])
        plus_half = sb("plus_half", [P, B])
        zm = sb("zm", [P, B])
        zeros = sb("zeros", [P, P], BF16)
        tr = sb("tr", [P, B])
        tz = sb("tz", [P, B])
        pre = sb("pre", [P, B])
        cand = sb("cand", [P, B])
        omz = sb("omz", [P, B])
        zt = sb("zt", [P, B])
        zh = sb("zh", [P, B])

        small_in = sem("small_in")
        scan_in = sem("scan_in")
        w1_in, expert_in = sem("w1_in"), sem("expert_in")
        wa_in, wf_in = sem("wa_in"), sem("wf_in")
        const_ready, stack_ones = sem("const_ready"), sem("stack_ones")
        mask_ready, mask_dma = sem("mask_ready"), sem("mask_dma")
        ad_ps, ad_ready, adl_ready = sem("ad_ps"), sem("ad_ready"), sem("adl_ready")
        dve_step = sem("dve_step")
        pool_step = sem("pool_step")
        ln_st, ln_rs, ln_xn = sem("ln_st"), sem("ln_rs"), sem("ln_xn")
        tp_ps, xt_ready = sem("tp_ps"), sem("xt_ready")
        qk_ps, rot_done, hi_done, r1_done, mid_done, lo_done = [
            sem(n) for n in ("qk_ps", "rot_done", "hi_done", "r1_done", "mid_done", "lo_done")]
        stack_wr, stack_rd = sem("stack_wr"), sem("stack_rd")
        v_ps, v_ready = sem("v_ps"), sem("v_ready")
        s1_ps, s1_max, m_ps, m_ready, m_dma = [sem(n) for n in ("s1_ps", "s1_max", "m_ps", "m_ready", "m_dma")]
        s2_ps, s2_exp, pv_done, ot_ready, ot_ps, att_ready = [
            sem(n) for n in ("s2_ps", "s2_exp", "pv_done", "ot_ready", "ot_ps", "att_ready")]
        at_ps, at_ready, pr_ps, x_ready = [sem(n) for n in ("at_ps", "at_ready", "pr_ps", "x_ready")]
        f1_ps, h_ready, f2_ps = [sem(n) for n in ("f1_ps", "h_ready", "f2_ps")]
        layer_done = sem("layer_done")
        out_done, x_done = sem("out_done"), sem("x_done")
        rt_ready, rt_step, rt_exp, lg_ps = [sem(n) for n in ("rt_ready", "rt_step", "rt_exp", "lg_ps")]
        up_ps, up_ready, hid_ready, down_ps, weighed = [sem(n) for n in ("up_ps", "up_ready", "hid_ready", "down_ps", "weighed")]
        ep_ps, ep_ready, gx_ps, gx_ready, gx_zero, gs_ready, ho_ready, ho_ps = [
            sem(n) for n in ("ep_ps", "ep_ready", "gx_ps", "gx_ready", "gx_zero", "gs_ready", "ho_ready", "ho_ps")]
        u_ps, u_ready, h_new, gate_ps, hb_ready = [sem(n) for n in ("u_ps", "u_ready", "h_new", "gate_ps", "hb_ready")]
        th_ready, score_ps, max_ready, ex_ready = [[sem(f"{n}{b}") for b in range(B)]
                                                   for n in ("th_ready", "score_ps", "max_ready", "ex_ready")]
        erec_ready, r_dot, c_dot, r_ready, c_pre, c_ready = [
            [sem(f"{n}{b}") for b in range(B)] for n in ("erec_ready", "r_dot", "c_dot", "r_ready", "c_pre", "c_ready")]
        z_dot, z_scaled, z_pre, z_ready, hh_ready, zt_ready, zm_ready, omz_ready, zh_ready = [
            sem(n) for n in ("z_dot", "z_scaled", "z_pre", "z_ready", "hh_ready", "zt_ready", "zm_ready", "omz_ready", "zh_ready")]
        apart_dve, apart_pe, apart_sp = sem("apart_dve"), sem("apart_pe"), sem("apart_sp")

        block = ctx.enter_context(nc.Block())
        NSMALL = 10

        def wcol(k):
            return WA[:, k * D:(k + 1) * D]

        LN0, XN0, TP0 = 1 + NL * LN_L, NT * (1 + NL * LN_L), NL * TP_L
        N0 = 2 * NE
        EARLY = 8
        N1 = 2 * (NE + 1)

        ATTENDED = B * H + 2
        NORMED, TURNED = ATTENDED + 3, ATTENDED + 5

        def slots(kind):
            return B * H + LEAD[kind] + (6 if kind == 0 else 3)

        def evacuated(kind, slot):
            u4 = slot - LEAD[kind] - (UH + TB if kind == 0 else UH + 1)
            return u4 // UH if u4 >= 0 and u4 % UH == 0 and u4 // UH < NU else None

        def post_gpsimd(g, inverse_root):
            inverse_root(LN0 + 1)
            inverse_root(LN0 + 2)
            nc.gpsimd.memset(GX[:, :, 3, :], 0.0)
            nc.gpsimd.memset(GX[:, S:S + U, 0:3, :], 0.0).then_inc(gx_zero, 1)
            inverse_root(LN0 + 3)
            g.wait_ge(gx_ready, 3 * B)
            g.wait_ge(gx_zero, 1)
            nc.gpsimd.tensor_copy(GS[:, :, :, :], GX[:, 0:U, :, :]).then_inc(gs_ready, 2)
            half_u = U // 2
            PTT = nc.gpsimd.tensor_tensor
            with g.Fori(0, S // U) as blk:
                for k in range(U):
                    n = blk * U + (k + 1)
                    g.wait_ge(h_new, n * 2)
                    PTT(hhalf[:, :], HR[:, (k - 1) % U, :], plus_half[:, :], ALU.mult).then_inc(hh_ready, 1)
                    g.wait_ge(z_ready, n)
                    g.wait_ge(hh_ready, n)
                    PTT(zt[:, :], tz[:, :], hhalf[:, :], ALU.mult).then_inc(zt_ready, 1)
                    PTT(zm[:, :], tz[:, :], half[:, 0:B], ALU.mult).then_inc(zm_ready, 1)
                    g.wait_ge(zt_ready, n)
                    PTT(zh[:, :], zt[:, :], hhalf[:, :], ALU.add).then_inc(zh_ready, 1)
                    g.wait_ge(zm_ready, n)
                    PTT(omz[:, :], zm[:, :], plus_half[:, :], ALU.add).then_inc(omz_ready, 1)
                    if (k + 1) % half_u == 0:
                        first, q = k + 1 - half_u, k // half_u
                        g.wait_ge(hb_ready, blk * U + (k + 1))
                        nc.gpsimd.tensor_copy(GS[:, first:k + 1, :, :],
                                              GX[:, bass.ds(blk * U + (U + first), half_u), :, :]).then_inc(gs_ready, 1)
                        g.wait_ge(h_new, blk * (2 * U) + 2 * (k + 2))
                        nc.gpsimd.tensor_copy(HO[:, :, bass.ds(blk * U + first, half_u)],
                                              HR[:, first:k + 1, :].rearrange("p u b -> p b u")).then_inc(ho_ready, 1)
            inverse_root(LN0 + 4)

        def post_scalar(act, turned):
            def activated(n):
                act.wait_ge(up_ps, n + 1)
                nc.scalar.activation(H0[:, n, :], bank[2 + n % 4][:, :], ACT.Gelu).then_inc(up_ready, 1)

            turned(TP0)
            for n in range(EARLY):
                activated(n)
            act.wait_ge(scan_in, 16 * 7)
            for b in range(B):
                act.wait_ge(tp_ps, TP0 + B + b + 1)
                nc.scalar.activation(RT[:, b * S:(b + 1) * S], bank[b][:, :], ACT.Identity, scale=gb[:, 0:1],
                                     bias=gb[:, 1:2]).then_inc(rt_ready, 1)
            act.wait_ge(rt_step, 1)
            nc.scalar.activation(lg[:, 2, :, :], lg[:, 1, :, :], ACT.Exp).then_inc(rt_exp, 1)
            for n in range(EARLY, B * N0):
                activated(n)
            turned(TP0 + 2 * B)
            act.wait_ge(ep_ps, 1)
            nc.scalar.copy(EP, bank[0][:, 0:B * S2].rearrange("p (b s) -> p b s", b=B)).then_inc(ep_ready, 1)
            for b in range(B):
                nc.scalar.copy(EW[:, b, :, :], bank[1 + 6 * b][:, 0:3 * S2].rearrange("p (g s) -> p g s", g=3)).then_inc(ep_ready, 1)
            for n in range(3 * B):
                b, gate = n // 3, n % 3
                act.wait_ge(gx_ps, n + 1)
                nc.scalar.activation(GX[:, 0:S, gate, b], bank[2 + n % 5][:, :], ACT.Identity,
                                     bias=sbias[:, gate:gate + 1]).then_inc(gx_ready, 1)
            with act.Fori(0, S // U) as blk:
                for k in range(U):
                    n = blk * U + (k + 1)
                    act.wait_ge(u_ready, n)
                    for b in range(B):
                        nc.scalar.activation(th[:, b, :], EP[:, b, :], ACT.Tanh, bias=ub[:, b:b + 1]).then_inc(th_ready[b], 1)
                    for b in range(B):
                        act.wait_ge(max_ready[b], n)
                        nc.scalar.activation(ex[:, b, :], bank[b][:, 0:S2], ACT.Exp, bias=nm[:, b:b + 1],
                                             accum_out=esum[:, b:b + 1]).then_inc(ex_ready[b], 1)
                    act.wait_ge(hb_ready, n)
                    for b in range(B):
                        act.wait_ge(erec_ready[b], n)
                        act.wait_ge(r_dot[b], n)
                        nc.scalar.activation(tr[:, b:b + 1], gr[:, 1, b:b + 1], ACT.Tanh, scale=erec[:, b:b + 1],
                                             bias=hb[:, 1, b:b + 1]).then_inc(r_ready[b], 1)
                    act.wait_ge(z_pre, n)
                    nc.scalar.activation(tz[:, :], gr[:, 0, :], ACT.Tanh).then_inc(z_ready, 1)
                    for b in range(B):
                        act.wait_ge(c_dot[b], n)
                        act.wait_ge(c_pre[b], n)
                        nc.scalar.activation(cand[:, b:b + 1], gr[:, 2, b:b + 1], ACT.Tanh, scale=erec[:, b:b + 1],
                                             bias=pre[:, b:b + 1]).then_inc(c_ready[b], 1)
            turned(TP0 + 3 * B)
            act.wait_ge(rt_step, 2)
            nc.scalar.activation(small[:, 1, :], small[:, 0, :], ACT.Tanh, scale=0.5).then_inc(rt_exp, 1)
            for b in range(B):
                act.wait_ge(tp_ps, TP0 + 4 * B + b + 1)
                nc.scalar.copy(RT[:, b * S:(b + 1) * S], bank[b][:, :]).then_inc(rt_ready, 1)
            for n in range(B * N1):
                act.wait_ge(up_ps, B * N0 + n + 1)
                if n >= 2:
                    act.wait_ge(hid_ready, n - 1)
                nc.scalar.activation(sg[:, n % 2, :], bank[2 + 2 * (n % 2)][:, :], ACT.Silu).then_inc(up_ready, 1)

        def post_vector(v, link, run_norm):
            V = nc.vector

            def wide(a):
                return a.unsqueeze(2).to_broadcast([P, NT, NE])

            def greatest(src, dst):
                link(V.tensor_reduce(dst, src, AX.X, ALU.max))

            def first_greatest(p, best, eq, at, hot):
                greatest(p, best)
                link(V.tensor_tensor(eq, p, wide(best), ALU.is_equal))
                link(V.tensor_tensor(eq, eq, rev[:, :, :], ALU.mult))
                greatest(eq, at)
                link(V.tensor_tensor(hot, eq, wide(at), ALU.is_equal))

            def weigh(n_experts, comb, done):
                groups = -(-n_experts // 4)
                for j in range(NT):
                    for q in range(groups):
                        v.wait_ge(down_ps, done + j * groups + q + 1)
                        for e in range(4 * q, min(4 * q + 4, n_experts)):
                            src = bank[6 + (j * groups + q) % 2][:, (e % 4) * D:(e % 4 + 1) * D]
                            if e < NE:
                                ins = V.scalar_tensor_tensor(out=XI[:, j, :], in0=src, scalar=comb[:, j, e:e + 1],
                                                             in1=XI[:, j, :], op0=ALU.mult, op1=ALU.add)
                            else:
                                ins = V.tensor_tensor(XI[:, j, :], XI[:, j, :], src, ALU.add)
                            link(ins)
                        v.sem_inc(weighed, 1)

            link(V.tensor_tensor(XI[:, :, :], XI[:, :, :], Y[:, :, :], ALU.add))
            run_norm(XI, Y, LN0 + 1)
            v.wait_ge(ln_xn, XN0 + NT)
            run_norm(Y, XN, LN0 + 2)
            v.wait_ge(lg_ps, 1)
            link(V.tensor_copy(lg[:, 0, :, :], bank[7][:, 0:NT * NE].rearrange("p (j e) -> p j e", e=NE)))
            greatest(lg[:, 0, :, :], small[:, 0, :])
            V.tensor_tensor(lg[:, 1, :, :], lg[:, 0, :, :], wide(small[:, 0, :]), ALU.subtract).then_inc(rt_step, 1)
            v.wait_ge(rt_exp, 1)
            link(V.tensor_reduce(small[:, 1, :], lg[:, 2, :, :], AX.X, ALU.add))
            link(V.reciprocal(small[:, 2, :], small[:, 1, :]))
            link(V.tensor_tensor(lg[:, 3, :, :], lg[:, 2, :, :], wide(small[:, 2, :]), ALU.mult))
            first_greatest(lg[:, 3, :, :], small[:, 3, :], lg[:, 4, :, :], small[:, 4, :], lg[:, 5, :, :])
            link(V.scalar_tensor_tensor(out=lg[:, 6, :, :], in0=lg[:, 5, :, :], scalar=-2.0, in1=lg[:, 3, :, :],
                                        op0=ALU.mult, op1=ALU.add))
            first_greatest(lg[:, 6, :, :], small[:, 5, :], lg[:, 7, :, :], small[:, 6, :], lg[:, 8, :, :])
            link(V.tensor_tensor(lg[:, 5, :, :], lg[:, 5, :, :], lg[:, 8, :, :], ALU.add))
            link(V.tensor_tensor(lg[:, 9, :, :], lg[:, 5, :, :], lg[:, 3, :, :], ALU.mult))
            v.wait_ge(scan_in, 16 * 7)
            V.tensor_copy(vrep, vatt[:, 0:1].to_broadcast([P, P]))
            V.tensor_scalar(uh, uh, 0.5, None, ALU.mult)
            V.tensor_scalar(wi[:, :, 0:2 * D], wi[:, :, 0:2 * D], 0.5, None, ALU.mult)
            V.tensor_scalar(sbias[:, 0:2], sbias[:, 0:2], 0.5, None, ALU.mult)
            V.tensor_copy(HR[:, U - 1, :], condT[:, :]).then_inc(h_new, 2)
            weigh(NE, lg[:, 9, :, :], 0)
            run_norm(XI, XN, LN0 + 3)
            scan_vector(v)
            for b in range(B):
                v.wait_ge(ho_ps, b + 1)
                x = XI[:, TB * b:TB * (b + 1), :]
                link(V.tensor_tensor(x, x, bank[b][:, :].rearrange("p (t d) -> p t d", t=TB), ALU.add))
            run_norm(XI, XN, LN0 + 4)
            v.wait_ge(lg_ps, 2)
            link(V.tensor_copy(lg[:, 0, :, :], bank[7][:, 0:NT * NE].rearrange("p (j e) -> p j e", e=NE)))
            first_greatest(lg[:, 0, :, :], small[:, 0, :], lg[:, 1, :, :], small[:, 2, :], lg[:, 9, :, :])
            v.sem_inc(rt_step, 1)
            v.wait_ge(rt_exp, 2)
            link(V.tensor_scalar(small[:, 3, :], small[:, 1, :], 0.5, 0.5, ALU.mult, ALU.add))
            for j in range(NT):
                V.tensor_scalar(Y[:, j, :], XN[:, j, :], small[:, 3, j:j + 1], None, ALU.mult).then_inc(ln_xn, 1)
            for b in range(B):
                for n in range(b * N1, (b + 1) * N1):
                    v.wait_ge(up_ready, B * N0 + n + 1)
                    if n == N1:
                        v.wait_ge(down_ps, 2 * NT + 3 * TB)
                    V.tensor_tensor(HT[:, n % N1, :], sg[:, n % 2, :], bank[3 + 2 * (n % 2)][:, :], ALU.mult).then_inc(hid_ready, 1)
                for j in range(TB * b, TB * (b + 1)):
                    for q in range(3):
                        v.wait_ge(down_ps, 2 * NT + j * 3 + q + 1)
                        for e in range(4 * q, min(4 * q + 4, NE + 1)):
                            src = bank[6 + (j * 3 + q) % 2][:, (e % 4) * D:(e % 4 + 1) * D]
                            if e < NE:
                                ins = V.scalar_tensor_tensor(out=XI[:, j, :], in0=src, scalar=lg[:, 9, j, e:e + 1],
                                                             in1=XI[:, j, :], op0=ALU.mult, op1=ALU.add)
                            else:
                                ins = V.tensor_tensor(XI[:, j, :], XI[:, j, :], src, ALU.add)
                            link(ins)
                        v.sem_inc(weighed, 1)
                v.sem_inc(x_done, 1)

        def scan_vector(v):
            V, TT = nc.vector, nc.vector.tensor_tensor
            half_u = U // 2
            v.wait_ge(ep_ready, 3)
            with v.Fori(0, S // U) as blk:
                for k in range(U):
                    n = blk * U + (k + 1)

                    def dot(gate, b):
                        return V.scalar_tensor_tensor(out=prod[:, gate, b, :], in0=ex[:, b, :], scalar=1.0, in1=EW[:, b, gate, :],
                                                      op0=ALU.mult, op1=ALU.mult, accum_out=gr[:, gate, b:b + 1])

                    def candidate_rest(b):
                        v.wait_ge(r_ready[b], n)
                        V.scalar_tensor_tensor(out=pre[:, b:b + 1], in0=hb[:, 3, b:b + 1], scalar=tr[:, b:b + 1],
                                               in1=hb[:, 2, b:b + 1], op0=ALU.mult, op1=ALU.add).then_inc(c_pre[b], 1)

                    v.wait_ge(u_ps, n)
                    V.tensor_copy(ub[:, :], bank[3][:, 0:B]).then_inc(u_ready, 1)
                    for b in range(B):
                        v.wait_ge(score_ps[b], n)
                        V.tensor_reduce(nm[:, b:b + 1], bank[b][:, 0:S2], AX.X, ALU.max, negate=True).then_inc(max_ready[b], 1)
                    v.wait_ge(gate_ps, n)
                    if k % half_u == 0:
                        v.wait_ge(gs_ready, blk * 2 + (k // half_u + 1))
                    TT(hb[:, :, :], bank[2][:, 0:4 * B].rearrange("p (g b) -> p g b", b=B), GS[:, k, :, :], ALU.add).then_inc(hb_ready, 1)
                    for b in range(B):
                        v.wait_ge(ex_ready[b], n)
                        dot(1, b).then_inc(r_dot[b], 1)
                        V.reciprocal(erec[:, b:b + 1], esum[:, b:b + 1]).then_inc(erec_ready[b], 1)
                        dot(0, b).then_inc(z_dot, 1)
                    v.wait_ge(hb_ready, n)
                    candidate_rest(0)
                    v.wait_ge(z_dot, n * B)
                    for b in range(B):
                        v.wait_ge(erec_ready[b], n)
                    TT(gr[:, 0, :], gr[:, 0, :], erec[:, :], ALU.mult).then_inc(z_scaled, 1)
                    dot(2, 0).then_inc(c_dot[0], 1)
                    v.wait_ge(z_scaled, n)
                    TT(gr[:, 0, :], gr[:, 0, :], hb[:, 0, :], ALU.add).then_inc(z_pre, 1)
                    candidate_rest(1)
                    dot(2, 1).then_inc(c_dot[1], 1)
                    v.wait_ge(zh_ready, n)
                    v.wait_ge(omz_ready, n)
                    if k == half_u:
                        v.wait_ge(ho_ready, blk * 2 + 1)
                    for b in range(B):
                        v.wait_ge(c_ready[b], n)
                        V.scalar_tensor_tensor(out=HR[:, k, b:b + 1], in0=cand[:, b:b + 1], scalar=omz[:, b:b + 1],
                                               in1=zh[:, b:b + 1], op0=ALU.mult, op1=ALU.add).then_inc(h_new, 1)

        def post_tensor(pe, turn):
            mm = nc.tensor.matmul

            def keep_clock(count):
                for _ in range(count):
                    mm(bank[7][:, 0:P], zeros[:, :], zeros[:, :], start=True, stop=True)

            def logits(rt, which):
                for j in range(NT):
                    ins = mm(bank[7][:, j * NE:(j + 1) * NE], rt[:, j * P:(j + 1) * P], mg[:, which, :], start=True, stop=True)
                ins.then_inc(lg_ps, 1)

            def down(b, hidden, n_experts, done):
                groups = -(-n_experts // 4)
                for t in range(TB):
                    for q in range(groups):
                        k = (TB * b + t) * groups + q
                        if k >= 2 or done:
                            pe.wait_ge(weighed, done + k - 1)
                        for e in range(4 * q, min(4 * q + 4, n_experts)):
                            for c in range(2):
                                ins = mm(bank[6 + k % 2][:, (e % 4) * D:(e % 4 + 1) * D], hidden[:, 2 * e + c, t * P:(t + 1) * P],
                                         EWD[:, 2 * e + c, :], start=(c == 0), stop=(c == 1))
                        ins.then_inc(down_ps, 1)

            turn(Y, XN0)
            for b in range(B):
                pe.wait_ge(xt_ready, TP0 + b + 1)
            pe.wait_ge(w1_in, 16)

            def up(n):
                b, c = n // N0, n % N0
                if n >= 4:
                    pe.wait_ge(up_ready, n - 3)
                mm(bank[2 + n % 4][:, :], W1[:, c // 2, (c % 2) * P:(c % 2 + 1) * P], XT[:, b * S:(b + 1) * S],
                   start=True, stop=True).then_inc(up_ps, 1)

            for n in range(EARLY):
                up(n)
            turn(XN, XN0 + NT)
            pe.wait_ge(rt_ready, B)
            pe.wait_ge(scan_in, 16 * 7)
            logits(RT, 0)
            for n in range(EARLY, B * N0):
                up(n)
            pe.wait_ge(expert_in, 16)
            pe.wait_ge(rt_step, 1)
            for b in range(B):
                pe.wait_ge(up_ready, (b + 1) * N0)
                down(b, H0[:, b * N0:(b + 1) * N0, :], NE, 0)
            turn(XN, XN0 + 2 * NT)
            pe.wait_ge(h_new, 2)
            for b in range(B):
                pe.wait_ge(xt_ready, TP0 + B + b + 1)
            for b in range(B):
                mm(bank[0][:, b * S2:(b + 1) * S2], watt[:, 1, :], ctxT[:, b, 0:S2], start=True, stop=True)
            for b in range(B):
                for gate in range(3):
                    ins = mm(bank[1 + 6 * b][:, gate * S2:(gate + 1) * S2], wi[:, 1, gate * D:(gate + 1) * D], ctxT[:, b, 0:S2],
                             start=True, stop=True)
            ins.then_inc(ep_ps, 1)
            for n in range(3 * B):
                b, gate = n // 3, n % 3
                if n >= 5:
                    pe.wait_ge(gx_ready, n - 4)
                mm(bank[2 + n % 5][:, :], wi[:, 0, gate * D:(gate + 1) * D], XT[:, b * S:(b + 1) * S],
                   start=True, stop=True).then_inc(gx_ps, 1)
            pe.wait_ge(ep_ready, 3)
            pe.wait_ge(gx_ready, 3 * B)
            with pe.Fori(0, S // U) as blk:
                for k in range(U):
                    n = blk * U + (k + 1)
                    h = HR[:, (k - 1) % U, :]
                    pe.wait_ge(h_new, n * 2)
                    mm(bank[3][:, 0:B], watt[:, 0, :], h, start=True, stop=True).then_inc(u_ps, 1)
                    mm(bank[2][:, 0:B], uh[:, 0:D], h, start=True, stop=True)
                    mm(bank[2][:, B:2 * B], uh[:, D:2 * D], h, start=True, stop=True)
                    mm(bank[2][:, 2 * B:4 * B], uh[:, 2 * D:3 * D], HR[:, (k - 1) % U:(k - 1) % U + 1, :].to_broadcast([P, 2, B]),
                       start=True, stop=True).then_inc(gate_ps, 1)
                    keep_clock(3)
                    for b in range(B):
                        pe.wait_ge(th_ready[b], n)
                        mm(bank[b][:, 0:S2], vrep, th[:, b, :], start=True, stop=True).then_inc(score_ps[b], 1)
                    keep_clock(6)
                    for done, count in ((max_ready[0], 8), (ex_ready[0], 6), (r_dot[1], 8), (r_ready[1], 8), (c_dot[1], 8),
                                        (c_pre[1], 4)):
                        pe.wait_ge(done, n)
                        keep_clock(count)
            pe.wait_ge(ho_ready, 2 * (S // U))
            for b in range(B):
                for t in range(TB):
                    ins = nc.tensor.transpose(bank[b][:, t * P:(t + 1) * P], HO[:, b, t * P:(t + 1) * P], ident[:, :])
                ins.then_inc(ho_ps, 1)
            turn(XN, XN0 + 3 * NT)
            pe.wait_ge(xt_ready, TP0 + 3 * B)
            logits(XT, 1)
            turn(Y, XN0 + 4 * NT)
            pe.wait_ge(rt_ready, 2 * B)
            pe.wait_ge(rt_step, 2)
            pe.wait_ge(expert_in, 16 + 48)
            for b in range(B):
                for n in range(b * N1, (b + 1) * N1):
                    if n >= 2:
                        pe.wait_ge(hid_ready, n - 1)
                    c = n % N1
                    cols = slice((c % 2) * P, (c % 2 + 1) * P)
                    src = (RT if c < 2 * NE else XT)[:, b * S:(b + 1) * S]
                    mm(bank[2 + 2 * (n % 2)][:, :], EWA[:, c // 2, cols], src, start=True, stop=True)
                    mm(bank[3 + 2 * (n % 2)][:, :], EWB[:, c // 2, cols], src, start=True, stop=True).then_inc(up_ps, 1)
                pe.wait_ge(hid_ready, (b + 1) * N1)
                down(b, HT, NE + 1, 2 * NT)

        @block.sync
        def _(sp):
            for dst, src in ((XI[:, :, :], x_d.rearrange("b (t p) d -> p (b t) d", p=P)),
                             (ident[:, :], ident_d), (condT[:, :], cond_d), (rot[:, :, :], rot_d),
                             (ctxT[:, :, 0:S2], ctx_d.rearrange("b d s -> d b s")),
                             (rev[:, :, :], rev_d), (NW[:, :, :], nw_d), (NB[:, :, :], nb_d),
                             (mask_words[0:1, 0:B * S // 4], mask_d),
                             (mask_words[0:1, B * S // 4:(B * S + B * S2) // 4], mask2_d)):
                sp.dma_start(dst, src).then_inc(small_in, 16)
            sp.wait_ge(mask_ready, 3)
            sp.wait_ge(const_ready, 1)
            sp.wait_ge(stack_ones, 1)
            for b in range(B):
                sp.dma_start(KS[MASK_ROW:MASK_ROW + 1, b, :, :],
                             mask_row[0:1, b * S:(b + 1) * S].unsqueeze(1).to_broadcast([1, H, S])).then_inc(mask_dma, 16)
            sp.dma_start(KC[MASK_ROW:MASK_ROW + 1, :, :],
                         mask_row[0:1, B * S:].unsqueeze(1).to_broadcast([1, H, B * SC])).then_inc(mask_dma, 16)

            def stack_write(l, i, n, kinds):
                j = i % 2
                sp.wait_ge(lo_done, l * ITEM_L + RD_AT[i])
                sp.sem_inc(apart_sp, 1)
                k0 = 0 if kinds[0][0] == "q" else 1
                for s in range(NSLOT):
                    if len(kinds) == 2:
                        src = parts[:, j, :, :, :].rearrange("p k c t -> p (k c) t")
                        step = 3 + K_PART[s] - Q_PART[s]
                        src = src[:, Q_PART[s]:Q_PART[s] + step + 1:step, 0:n]
                        dst = scratch[j, s, :, :, 0:n]
                    else:
                        src = parts[:, j, k0, (Q_PART, K_PART)[k0][s], 0:n]
                        dst = scratch[j, s, :, k0, 0:n]
                    sp.dma_start(dst, src).then_inc(stack_wr, 16)

            def stack_read(l, i, n, kinds):
                j = i % 2
                sp.wait_ge(stack_wr, (l * PARTS_L + i + 1) * NSLOT * 16)
                sp.sem_inc(apart_sp, 1)
                for kind, dst in kinds:
                    sp.dma_start(dst, scratch[j, :, :, 0 if kind == "q" else 1, 0:n].rearrange(
                        "s (d h) t -> (s d) h t", h=H)).then_inc(stack_rd, 16)

            def stack_done(l, i):
                sp.wait_ge(stack_rd, (l * RD_L + RD_AT[i]) * 16)
                sp.sem_inc(apart_sp, 1)

            def maxima(l, u):
                b, h0 = (u % NU) // (H // UH), UH * (u % (H // UH))
                sp.wait_ge(m_ready, (l * UNIT_L + u + 1) * 2)
                sp.sem_inc(apart_sp, 1)
                for r in range(2):
                    sp.dma_start(QS[MAX_ROW + r:MAX_ROW + r + 1, b, h0:h0 + UH, :].rearrange("p h t -> p (h t)"),
                                 mrow[:, u % 2, r, :]).then_inc(m_dma, 16)
                sp.wait_ge(m_dma, (l * UNIT_L + u + 1) * 32)
                sp.sem_inc(apart_sp, 1)

            with sp.Fori(0, NL) as l:
                sp.wait_ge(ln_st, (l * LN_L + 1) * B)
                sp.sem_inc(apart_sp, 1)
                sp.dma_start(WA[:, :], wa_d[bass.ds(l, 1), :, :].rearrange("a p n -> p (a n)")).then_inc(wa_in, 16)
                sp.wait_ge(layer_done, l + 1)
                sp.sem_inc(apart_sp, 1)
                for dst, src in ((WF, wf_d), (F1B, f1b_d), (F2B, f2b_d)):
                    sp.dma_start(dst[:, :], src[bass.ds(l, 1), :, :].rearrange("a p n -> p (a n)")).then_inc(wf_in, 16)
                token_stacks = [(S, [("q", QS[0:PROD, b, :, :]), ("k", KS[0:PROD, b, :, :])]) for b in range(B)]
                for b in range(B):
                    stack_write(l, b, *token_stacks[b])
                    stack_read(l, b, *token_stacks[b])
                for b in range(B):
                    stack_done(l, b)
                context_stack = (B * SC, [("k", KC[0:PROD, :, :])])
                between = {2: lambda: stack_write(l, CTX, *context_stack), 3: lambda: stack_read(l, CTX, *context_stack),
                           4: lambda: stack_done(l, CTX)}
                for u in range(NU):
                    maxima(l, u)
                    if u in between:
                        between[u]()
                for b in range(B):
                    query_stack = (S, [("q", QS[0:PROD, b, :, :])])
                    stack_write(l, 3 + b, *query_stack)
                    stack_read(l, 3 + b, *query_stack)
                for b in range(B):
                    stack_done(l, 3 + b)
                for u in range(NU, 2 * NU):
                    maxima(l, u)
            sp.dma_start(W1, w1_d).then_inc(w1_in, 16)
            for dst, src in ((gb[:, :], gb_d), (mg[:, :, :], mg_d), (watt[:, :, :], watt_d), (vatt[:, :], vatt_d),
                             (wi[:, :, :], wi_d), (uh, uh_d), (sbias[:, :], sb_d)):
                sp.dma_start(dst, src).then_inc(scan_in, 16)
            sp.wait_ge(layer_done, NL + 1)
            sp.dma_start(EWD[:, 0:2 * NE, :], w2_d).then_inc(expert_in, 16)
            sp.wait_ge(down_ps, 2 * NT)
            for dst, src in ((EWA, eg_d), (EWB, eu_d), (EWD, ed_d)):
                sp.dma_start(dst, src).then_inc(expert_in, 16)
            for b in range(B):
                sp.wait_ge(x_done, b + 1)
                sp.dma_start(out_d[b].rearrange("(t p) d -> p t d", p=P), XI[:, TB * b:TB * (b + 1), :]).then_inc(out_done, 16)
            sp.wait_ge(out_done, 16 * B)

        @block.gpsimd
        def _(g):
            done = {"n": 0}

            def settled(ins):
                done["n"] += 1
                ins.then_inc(pool_step, 1)
                g.wait_ge(pool_step, done["n"])

            settled(nc.gpsimd.memset(stacks[MASK_ROW:MAX_ROW, 0, :], ONES))
            settled(nc.gpsimd.memset(stacks[MAX_ROW:P, 0, :], 0.0))
            settled(nc.gpsimd.memset(cstack[MAX_ROW:P, :], ONES))
            settled(nc.gpsimd.memset(cstack[0:MAX_ROW, :], 0.0))
            nc.gpsimd.memset(half[:, :], -0.5)
            nc.gpsimd.memset(plus_half[:, :], 0.5)
            nc.gpsimd.memset(zeros[:, :], 0.0)
            nc.gpsimd.memset(VP[:, :, :, :], 1.0)
            nc.gpsimd.memset(VC[:, :, :, :], 1.0)
            settled(nc.gpsimd.memset(VT[:, :, :, :, :], 0.0))
            for r in range(UH):
                settled(nc.gpsimd.memset(VT[TAIL * r:TAIL * (r + 1), :, :, r, HD:HD + 1], 1.0))
            nc.gpsimd.memset(ctxT[:, :, S2:SC], 0.0).then_inc(const_ready, 2)
            g.wait_ge(const_ready, 2)

            def inverse_root(n):
                for b in range(B):
                    half_b = slice(TB * b, TB * (b + 1))
                    g.wait_ge(ln_st, n * B - (B - 1 - b))
                    nc.gpsimd.tensor_tensor(rstd[:, half_b], vpe[:, half_b], half[:, half_b], ALU.pow).then_inc(ln_rs, 1)

            inverse_root(1)
            g.wait_ge(ad_ready, 2)
            with g.Fori(0, NL) as l:
                g.wait_ge(layer_done, l + 1)
                nc.gpsimd.tensor_copy(ADL[:, :, :, :].rearrange("p n k b -> p (n k b)"),
                                      AD[:, bass.ds(l, 1), :, :, :].rearrange("p l n k b -> p (l n k b)")).then_inc(adl_ready, 1)
                for n in range(LN_L):
                    inverse_root(l * LN_L + n + 2)
            post_gpsimd(g, inverse_root)

        @block.scalar
        def _(act):
            def turned(n, scale=None, bias=None):
                for b in range(B):
                    act.wait_ge(tp_ps, n + b + 1)
                    kw = {}
                    if scale is not None:
                        kw = dict(scale=scale(b), bias=bias(b))
                    nc.scalar.activation(XT[:, b * S:(b + 1) * S], bank[b][:, :], ACT.Identity, **kw).then_inc(xt_ready, 1)

            with act.Fori(0, NL) as l:
                def item_cols(m):
                    i, kind, b = ITEMS[m]
                    return i % 2, 0 if kind == "q" else 1, B * SC if i == CTX else S

                def high(m):
                    j, k, n = item_cols(m)
                    act.wait_ge(rot_done, l * ITEM_L + m + 1)
                    if ITEMS[m][0] >= 2:
                        act.wait_ge(stack_wr, (l * PARTS_L + ITEMS[m][0] - 1) * NSLOT * 16)
                    nc.scalar.copy(parts[:, j, k, 0, 0:n], rF[:, m % 3, 0:n]).then_inc(hi_done, 1)

                def middle(m):
                    j, k, n = item_cols(m)
                    act.wait_ge(r1_done, l * ITEM_L + m + 1)
                    nc.scalar.copy(parts[:, j, k, 1, 0:n], rA[:, m % 3, 0:n]).then_inc(mid_done, 1)

                def rotations(ms, between={}):
                    for k in range(len(ms) + 1):
                        if k < len(ms):
                            high(ms[k])
                        if k in between:
                            between[k]()
                        if k >= 1:
                            middle(ms[k - 1])

                def norm(n):
                    act.wait_ge(adl_ready, l + 1)
                    turned(l * TP_L + n * B, lambda b: ADL[:, n, 0, b:b + 1], lambda b: ADL[:, n, 1, b:b + 1])

                def norm_batch(n, b):
                    act.wait_ge(tp_ps, l * TP_L + n * B + b + 1)
                    nc.scalar.activation(XT[:, b * S:(b + 1) * S], bank[1][:, :], ACT.Identity, scale=ADL[:, n, 0, b:b + 1],
                                         bias=ADL[:, n, 1, b:b + 1]).then_inc(xt_ready, 1)

                def hidden(n):
                    if n == 0:
                        act.wait_ge(wf_in, (l + 1) * 48)
                    act.wait_ge(f1_ps, l * 8 + n + 1)
                    nc.scalar.activation(HL[:, n, :], bank[2 + n % 2][:, :], ACT.Gelu, bias=F1B[:, n % 4:n % 4 + 1]).then_inc(h_ready, 1)

                act.wait_ge(v_ps, l * V_L + 1)
                nc.scalar.copy(VC[:, :, :, 0:HD], bank[6][:, 0:B * D].rearrange("p (b h d) -> p b h d", b=B, h=H)).then_inc(v_ready, 1)
                act.wait_ge(v_ps, l * V_L + 2)
                for r in range(UH):
                    rows = slice(TAIL * r, TAIL * (r + 1))
                    nc.scalar.copy(VT[rows, :, :, r, 0:HD],
                                   bank[7][rows, 0:B * D].rearrange("p (b u r d) -> p b u r d", b=B, u=H // UH, r=UH)[:, :, :, r, :]
                                   ).then_inc(v_ready, 1)
                norm(0)

                def self_values(b):
                    act.wait_ge(v_ps, l * V_L + 3 + b)
                    nc.scalar.copy(VP[:, TB * b:TB * (b + 1), :, 0:HD],
                                   bank[6 + b][:, :].rearrange("p (t h d) -> p t h d", t=TB, h=H)).then_inc(v_ready, 1)

                rotations([0, 1, 2, 3, 4], {3: lambda: self_values(0)})
                self_values(1)

                def attention(kind):
                    def attended(b):
                        act.wait_ge(at_ps, l * 2 * B + kind * B + b + 1)
                        nc.scalar.copy(attT[:, b * S:(b + 1) * S], bank[1][:, :]).then_inc(at_ready, 1)

                    for slot in range(slots(kind)):
                        j = slot - LEAD[kind]
                        u = evacuated(kind, slot)
                        if u is not None:
                            ku = kind * NU + u
                            act.wait_ge(pv_done, l * PV_L + (UH * u + UH + TB - 1 if kind == 0 else STEPS + u + 1))
                            if ku >= 2:
                                act.wait_ge(ot_ps, l * UNIT_L + ku - 1)
                            nc.scalar.copy(OT[:, u % 2, :], bank[6 + u % 2][:, :]).then_inc(ot_ready, 1)
                        if slot == ATTENDED + 1:
                            attended(0)
                        if slot == TURNED + 1:
                            norm_batch(1 + kind, 0)
                        if u == NU - 1:
                            if kind == 0:
                                high(5)
                            else:
                                hidden(0)
                                hidden(1)
                        if not 0 <= j < B * H:
                            continue
                        u = j // UH
                        if kind == 0:
                            for kc in range(TB):
                                act.wait_ge(s2_ps, l * S2_L + TB * j + kc + 1)
                                if kc == 0 and j >= 2:
                                    act.wait_ge(pv_done, l * PV_L + j - 1)
                                nc.scalar.activation(PT[:, PT_AT[kc] + j % (kc + 2), :], bank[4 + kc % 2][:, :], ACT.Exp,
                                                     scale=SCALE).then_inc(s2_exp, 1)
                        else:
                            base = B * H * TB + (UH + 1) * u
                            if j % UH == 0:
                                act.wait_ge(s2_ps, l * S2_L + base + 1)
                                if u >= 2:
                                    act.wait_ge(pv_done, l * PV_L + STEPS + u - 1)
                                nc.scalar.activation(PTT[:, u % 2, :], bank[4 + base % 2][:, :], ACT.Exp,
                                                     scale=SCALE).then_inc(s2_exp, 1)
                            n = base + 1 + j % UH
                            act.wait_ge(s2_ps, l * S2_L + n + 1)
                            if u >= NPT:
                                act.wait_ge(pv_done, l * PV_L + STEPS + u - NPT + 1)
                            else:
                                act.wait_ge(pv_done, l * PV_L + STEPS)
                            nc.scalar.activation(PT[:, u % NPT * UH + j % UH, :], bank[4 + n % 2][:, :], ACT.Exp,
                                                 scale=SCALE).then_inc(s2_exp, 1)
                    attended(1)
                    if kind == 0:
                        middle(5)
                        norm_batch(1, 1)
                        rotations([6])
                    else:
                        hidden(2)
                        hidden(3)
                        norm_batch(2, 1)
                        for n in range(4, B * 4):
                            hidden(n)

                attention(0)
                attention(1)
            post_scalar(act, turned)

        @block.vector
        def _(v):
            chain = {"base": 0, "n": 0}
            V = nc.vector

            def link(ins):
                chain["n"] += 1
                ins.then_inc(dve_step, 1)
                v.wait_ge(dve_step, chain["base"] + chain["n"])

            def norm_statistics(src, b):
                tiles = range(TB * b, TB * (b + 1))
                for j in tiles:
                    ins = V.bn_stats(stats[:, j, :], src[:, j, :])
                link(ins)
                v.sem_inc(apart_dve, 1)
                for j in tiles:
                    ins = V.bn_aggr(mv[:, j, :], stats[:, j, :])
                link(ins)
                half_b = slice(TB * b, TB * (b + 1))
                V.tensor_scalar(vpe[:, half_b], mv[:, half_b, 1], EPS, None, ALU.add).then_inc(ln_st, 1)

            def norm_apply(src, dst, n, b):
                v.wait_ge(ln_rs, n * B - (B - 1 - b))
                for j in range(TB * b, TB * (b + 1)):
                    V.tensor_scalar(dst[:, j, :], src[:, j, :], mv[:, j, 0:1], rstd[:, j:j + 1],
                                    ALU.subtract, ALU.mult).then_inc(ln_xn, 1)

            def run_norm(src, dst, n):
                for b in range(B):
                    norm_statistics(src, b)
                for b in range(B):
                    norm_apply(src, dst, n, b)

            V.memset(stacks[32:MASK_ROW, 0, :], 0.0)
            V.memset(stacks[0:MAX_ROW, 1, :], 0.0)
            V.memset(stacks[MAX_ROW:P, 1, :], ONES).then_inc(stack_ones, 1)
            v.wait_ge(small_in, 16 * NSMALL)
            v.wait_ge(const_ready, 2)
            link(V.memset(mask_row[:, :], NEG))
            V.tensor_scalar(mask_row[0:1, 0:B * S], mask_raw[0:1, 0:B * S], NEG, None, ALU.mult).then_inc(mask_ready, 1)
            for b in range(B):
                V.tensor_scalar(mask_row[0:1, B * S + b * SC:B * S + b * SC + S2],
                                mask_raw[0:1, B * S + b * S2:B * S + (b + 1) * S2], NEG, None, ALU.mult).then_inc(mask_ready, 1)
            run_norm(XI, Y, 1)
            v.wait_ge(ad_ps, 1)
            ad = AD[:, :, :, :, :].rearrange("p l n k b -> p (l n) k b")
            link(V.tensor_tensor(ad, bank[7][:, 0:3 * NL * 4].rearrange("p (n k b) -> p n k b", k=2, b=B),
                                 NB[:, :, :].unsqueeze(3).to_broadcast([P, 3 * NL, 2, B]), ALU.add))
            V.tensor_scalar(ad[:, :, 0, :], ad[:, :, 0, :], 1.0, None, ALU.add).then_inc(ad_ready, 2)
            v.wait_ge(ln_xn, NT)
            v.sem_inc(layer_done, 1)
            before = chain["n"]

            with v.Fori(0, NL) as l:
                chain["base"] = l * DVE_L + before
                chain["n"] = 0

                def item_cols(m):
                    i, kind, b = ITEMS[m]
                    return i % 2, 0 if kind == "q" else 1, B * SC if i == CTX else S

                def rotate(m):
                    j, k, n = item_cols(m)
                    r = m % 3
                    c = 2 + 2 * (m % 2)
                    if m >= 3:
                        v.wait_ge(lo_done, l * ITEM_L + m - 2)
                    v.wait_ge(qk_ps, l * ITEM_L + m + 1)
                    for t, src, dst in ((0, bank[c], rA), (1, bank[c + 1], rB)):
                        if ITEMS[m][0] == CTX:
                            for b in range(B):
                                ins = V.tensor_tensor(dst[:, r, b * SC:(b + 1) * SC], src[:, b * SC:(b + 1) * SC],
                                                      rot[:, t, 0:SC], ALU.mult)
                        else:
                            ins = V.tensor_tensor(dst[:, r, 0:n], src[:, 0:n], rot[:, t, 0:n], ALU.mult)
                    link(ins)
                    V.tensor_tensor(rF[:, r, 0:n], rA[:, r, 0:n], rB[:, r, 0:n], ALU.add).then_inc(rot_done, 1)

                def residue(m):
                    j, k, n = item_cols(m)
                    v.wait_ge(hi_done, l * ITEM_L + m + 1)
                    v.wait_ge(rot_done, l * ITEM_L + m + 1)
                    V.tensor_tensor(rA[:, m % 3, 0:n], rF[:, m % 3, 0:n], parts[:, j, k, 0, 0:n], ALU.subtract).then_inc(r1_done, 1)

                def low(m):
                    j, k, n = item_cols(m)
                    v.wait_ge(mid_done, l * ITEM_L + m + 1)
                    v.wait_ge(r1_done, l * ITEM_L + m + 1)
                    ins = V.tensor_tensor(parts[:, j, k, 2, 0:n], rA[:, m % 3, 0:n], parts[:, j, k, 1, 0:n], ALU.subtract)
                    ins.then_inc(lo_done, 1)

                def rotations(ms):
                    for k in range(len(ms) + 2):
                        if k < len(ms):
                            rotate(ms[k])
                        if 0 <= k - 1 < len(ms):
                            residue(ms[k - 1])
                        if k >= 2:
                            low(ms[k - 2])

                def update(kind, b):
                    v.wait_ge(pr_ps, l * 2 * B + kind * B + b + 1)
                    y = Y[:, TB * b:TB * (b + 1), :]
                    return V.tensor_tensor(y, y, bank[1][:, :].rearrange("p (t d) -> p t d", t=TB), ALU.add)

                def attention(kind):
                    def normalise(u):
                        ku = kind * NU + u
                        b, h0 = u // (H // UH), UH * (u % (H // UH))
                        v.wait_ge(ot_ps, l * UNIT_L + ku + 1)
                        o = bank[0][:, :].rearrange("p (t h c) -> p h t c", h=UH, t=TB)
                        link(V.reciprocal(orec[:, u % 2, :, :], o[:, :, :, HD]))
                        V.tensor_tensor(att[:, TB * b:TB * (b + 1), h0 * HD:(h0 + UH) * HD].rearrange("p t (h d) -> p h t d", h=UH),
                                        o[:, :, :, 0:HD],
                                        orec[:, u % 2, :, :].unsqueeze(3).to_broadcast([P, UH, TB, HD]),
                                        ALU.mult).then_inc(att_ready, 1)

                    def maxima(u):
                        ku = kind * NU + u
                        v.wait_ge(m_ps, l * UNIT_L + ku + 1)
                        if ku >= 2:
                            v.wait_ge(m_dma, (l * UNIT_L + ku - 1) * 32)
                        m = bank[0][0:UH * TB, 0:P]
                        V.tensor_copy(mrow[:, u % 2, 0, :], m).then_inc(m_ready, 1)
                        v.wait_ge(m_ready, (l * UNIT_L + ku) * 2 + 1)
                        V.tensor_tensor(mrow[:, u % 2, 1, :], m, mrow[:, u % 2, 0, :], ALU.subtract).then_inc(m_ready, 1)

                    for slot in range(slots(kind)):
                        if slot >= 5 and slot % UH == 5 % UH and (slot - 5) // UH < NU:
                            maxima((slot - 5) // UH)
                        if slot < B * H:
                            u, hl = slot // UH, slot % UH
                            if hl == 0 and kind * NU + u >= 2:
                                v.wait_ge(m_ps, l * UNIT_L + kind * NU + u - 1)
                            if kind == 0:
                                for qt in range(TB):
                                    n = TB * slot + qt
                                    v.wait_ge(s1_ps, l * S1_L + n + 1)
                                    V.tensor_reduce(nmax[:, u % 2, hl * TB + qt:hl * TB + qt + 1], bank[1 + n % 3][:, :],
                                                    AX.X, ALU.max, negate=True).then_inc(s1_max, 1)
                            else:
                                for qp in range(2):
                                    n = B * H * TB + 2 * slot + qp
                                    v.wait_ge(s1_ps, l * S1_L + n + 1)
                                    V.tensor_reduce(nmax[:, u % 2, hl * TB + 2 * qp:hl * TB + 2 * qp + 2],
                                                    bank[1 + n % 3][:, :].rearrange("p (t k) -> p t k", t=2)[:, :, 0:S2],
                                                    AX.X, ALU.max, negate=True).then_inc(s1_max, 1)
                        u = evacuated(kind, slot - 1)
                        if u is not None:
                            normalise(u)
                        if slot == ATTENDED + 2:
                            update(kind, 0).then_inc(x_ready, 1)
                            v.wait_ge(x_ready, l * 2 + kind + 1)
                        if slot == NORMED:
                            norm_statistics(Y, 0)
                        if slot == NORMED + 1:
                            norm_apply(Y, XN, l * LN_L + 3 + kind, 0)
                        if kind == 0 and slot == TURNED + 2:
                            rotate(5)
                    if kind == 0:
                        residue(5)
                    link(update(kind, 1))
                    norm_statistics(Y, 1)
                    if kind == 0:
                        low(5)
                    norm_apply(Y, XN, l * LN_L + 3 + kind, 1)
                    if kind == 0:
                        rotations([6])

                run_norm(Y, XN, l * LN_L + 2)
                rotations([0, 1, 2, 3, 4])
                attention(0)
                attention(1)
                v.wait_ge(wf_in, (l + 1) * 48)
                for b in range(B):
                    v.wait_ge(f2_ps, l * B + b + 1)
                    y = Y[:, TB * b:TB * (b + 1), :]
                    link(V.tensor_tensor(y, y, bank[6 + b][:, :].rearrange("p (t d) -> p t d", t=TB), ALU.add))
                    link(V.tensor_tensor(y, y, F2B[:, :].unsqueeze(1).to_broadcast([P, TB, D]), ALU.add))
                v.sem_inc(layer_done, 1)
                assert chain["n"] == DVE_L, chain["n"]
            chain["base"], chain["n"] = NL * DVE_L + before, 0
            post_vector(v, link, run_norm)

        @block.tensor
        def _(pe):
            mm = nc.tensor.matmul
            pe.wait_ge(small_in, 16 * NSMALL)
            for i in range(3 * NL):
                for k in range(2):
                    c = (2 * i + k) * B
                    ins = mm(bank[7][:, c:c + B], NW[:, i, k * D:(k + 1) * D], condT[:, :], start=True, stop=True)
            ins.then_inc(ad_ps, 1)
            pe.wait_ge(const_ready, 2)
            pe.wait_ge(ad_ready, 2)

            def turn(src, xn_before):
                for b in range(B):
                    for t in range(TB):
                        j = TB * b + t
                        pe.wait_ge(ln_xn, xn_before + j + 1)
                        ins = nc.tensor.transpose(bank[b][:, t * P:(t + 1) * P], src[:, j, :], ident[:, :])
                    ins.then_inc(tp_ps, 1)

            pe.wait_ge(mask_dma, 48)
            with pe.Fori(0, NL) as l:
                def project(m, pair, src):
                    i, kind, b = ITEMS[m]
                    c = 2 + 2 * (m % 2)
                    if m >= 2:
                        pe.wait_ge(rot_done, l * ITEM_L + m - 1)
                    n = B * SC if i == CTX else S
                    mm(bank[c][:, 0:n], wcol(pair[0]), src, start=True, stop=True)
                    mm(bank[c + 1][:, 0:n], wcol(pair[1]), src, start=True, stop=True).then_inc(qk_ps, 1)

                def turn_batch(n, b):
                    for t in range(TB):
                        pe.wait_ge(ln_xn, l * XN_L + (n + 1) * NT + TB * b + t + 1)
                        ins = nc.tensor.transpose(bank[1][:, t * P:(t + 1) * P], XN[:, TB * b + t, :], ident[:, :])
                    ins.then_inc(tp_ps, 1)

                def hidden(n):
                    b, fc = n // 4, n % 4
                    if n == 0:
                        pe.wait_ge(wf_in, (l + 1) * 48)
                    if fc == 0:
                        pe.wait_ge(xt_ready, l * TP_L + 2 * B + b + 1)
                    if n >= 2:
                        pe.wait_ge(h_ready, l * 8 + n - 1)
                    mm(bank[2 + n % 2][:, :], WF[:, fc * P:(fc + 1) * P], XT[:, b * S:(b + 1) * S],
                       start=True, stop=True).then_inc(f1_ps, 1)

                def forward(b):
                    pe.wait_ge(h_ready, l * 8 + 4 * (b + 1))
                    for t in range(TB):
                        for fc in range(4):
                            ins = mm(bank[6 + b][:, t * P:(t + 1) * P], HL[:, 4 * b + fc, t * P:(t + 1) * P],
                                     WF[:, DFF + fc * D:DFF + (fc + 1) * D], start=(fc == 0), stop=(fc == 3))
                    ins.then_inc(f2_ps, 1)

                def attention(kind):
                    def first(j, i):
                        b, h = j // H, j % H
                        if kind == 0:
                            n = TB * j + i
                            if n >= 3:
                                pe.wait_ge(s1_max, l * S1_L + n - 2)
                            mm(bank[1 + n % 3][:, :], QS[0:ROWS1, b, h, i * P:(i + 1) * P],
                               KS[0:ROWS1, b, h, :], start=True, stop=True).then_inc(s1_ps, 1)
                        else:
                            n = B * H * TB + 2 * j + i // 2
                            if i % 2 == 0:
                                pe.wait_ge(s1_max, l * S1_L + n - 2)
                            ins = mm(bank[1 + n % 3][:, 256 * (i % 2):256 * (i % 2) + S2],
                                     QS[0:ROWS1, b, h, i * P:(i + 1) * P],
                                     KC[0:ROWS1, h, b * SC:b * SC + S2], start=True, stop=True)
                            if i % 2:
                                ins.then_inc(s1_ps, 1)

                    def second(j, i):
                        b, h, u = j // H, j % H, j // UH
                        q = QS[0:P, b, h, :]
                        if j % UH == 0 and i == 0:
                            pe.wait_ge(m_dma, (l * UNIT_L + kind * NU + u + 1) * 32)
                        if kind == 0:
                            n = TB * j + i
                            if n >= 2:
                                pe.wait_ge(s2_exp, l * S2_L + n - 1)
                            mm(bank[4 + n % 2][:, :], KS[0:P, b, h, i * P:(i + 1) * P], q,
                               start=True, stop=True).then_inc(s2_ps, 1)
                        elif i == 0:
                            n = B * H * TB + (UH + 1) * u
                            if j % UH == 0:
                                pe.wait_ge(s2_exp, l * S2_L + n - 1)
                                pe.sem_inc(apart_pe, 1)
                                for hl in range(UH):
                                    ins = mm(bank[4 + n % 2][TAIL * hl:TAIL * (hl + 1), :],
                                             KC[0:P, h + hl, b * SC + P:(b + 1) * SC],
                                             QS[0:P, b, h + hl, :], start=True, stop=True)
                                ins.then_inc(s2_ps, 1)
                            n += 1 + j % UH
                            pe.wait_ge(s2_exp, l * S2_L + n - 1)
                            mm(bank[4 + n % 2][:, :], KC[0:P, h, b * SC:b * SC + P], q,
                               start=True, stop=True).then_inc(s2_ps, 1)

                    def bank_free(u):
                        if kind * NU + u >= 2:
                            pe.wait_ge(ot_ready, l * UNIT_L + kind * NU + u - 1)

                    def values_self(step):
                        pairs = [(step - kc, kc) for kc in range(TB) if 0 <= step - kc < B * H]
                        if step % UH == 0 and step < B * H:
                            bank_free(step // UH)
                        pe.wait_ge(s2_exp, l * S2_L + max(TB * j + kc for j, kc in pairs) + 1)
                        for j, kc in pairs:
                            hl = j % UH
                            ins = mm(bank[6 + j // UH % 2][HC * hl:HC * hl + HD + 1, :], VP[:, TB * (j // H) + kc, j % H, :],
                                     PT[:, PT_AT[kc] + j % (kc + 2), :], start=(kc == 0), stop=(kc == TB - 1))
                        ins.then_inc(pv_done, 1)

                    def values_cross(u):
                        b, g = u // (H // UH), u % (H // UH)
                        bank_free(u)
                        pe.wait_ge(s2_exp, l * S2_L + B * H * TB + (UH + 1) * (u + 1))
                        mm(bank[6 + u % 2][:, :], VT[:, b, g, :, :].rearrange("p r c -> p (r c)"), PTT[:, u % 2, :],
                           start=True, stop=False)
                        for r in range(UH):
                            ins = mm(bank[6 + u % 2][HC * r:HC * r + HD + 1, :], VC[:, b, UH * g + r, :],
                                     PT[:, u % NPT * UH + r, :], start=False, stop=True)
                        ins.then_inc(pv_done, 1)

                    def turn_values(u, maxima_turned):
                        ku = kind * NU + u
                        pe.wait_ge(ot_ready, l * UNIT_L + ku + 1)
                        pe.wait_ge(m_ready, (l * UNIT_L + kind * NU + maxima_turned) * 2)
                        if ku >= 1:
                            pe.wait_ge(att_ready, l * UNIT_L + ku)
                        for t in range(TB):
                            ins = nc.tensor.transpose(bank[0][:, t * P:(t + 1) * P], OT[:, u % 2, t * P:(t + 1) * P], ident[:, :])
                        ins.then_inc(ot_ps, 1)

                    def attended(b):
                        pe.wait_ge(att_ready, l * UNIT_L + kind * NU + (b + 1) * (H // UH))
                        for t in range(TB):
                            ins = nc.tensor.transpose(bank[1][:, t * P:(t + 1) * P], att[:, TB * b + t, :], ident[:, :])
                        ins.then_inc(at_ps, 1)

                    def output(b):
                        pe.wait_ge(at_ready, l * 2 * B + kind * B + b + 1)
                        for t in range(TB):
                            ins = mm(bank[1][:, t * P:(t + 1) * P], attT[:, b * S + t * P:b * S + (t + 1) * P],
                                     wcol(WO if kind == 0 else CO), start=True, stop=True)
                        ins.then_inc(pr_ps, 1)

                    turned_units = 0
                    for slot in range(slots(kind)):
                        if slot == ATTENDED:
                            attended(0)
                        if slot == ATTENDED + 1:
                            output(0)
                        j = slot - LEAD[kind]
                        for i in range(TB):
                            if slot < B * H:
                                if i == 0 and slot % H == 0:
                                    at = RD_AT[(0 if kind == 0 else 3) + slot // H]
                                    pe.wait_ge(stack_rd, (l * RD_L + at) * 16)
                                first(slot, i)
                            if 0 <= j < B * H:
                                second(j, i)
                        if kind == 0 and 1 <= j <= STEPS:
                            values_self(j - 1)
                        if kind == 1 and j >= UH and j % UH == 0 and j // UH <= NU:
                            values_cross(j // UH - 1)
                        if slot >= UH and slot % UH == 0 and slot // UH <= NU:
                            u = slot // UH - 1
                            ku = kind * NU + u
                            pe.wait_ge(s1_max, l * S1_L + (TB * UH * (u + 1) if kind == 0 else B * H * TB + 2 * UH * (u + 1)))
                            if turned_units:
                                pe.wait_ge(att_ready, l * UNIT_L + kind * NU + turned_units)
                            if ku >= 1:
                                pe.wait_ge(m_ready, (l * UNIT_L + ku) * 2)
                            nc.tensor.transpose(bank[0][0:UH * TB, 0:P], nmax[:, u % 2, :], ident[:, :]).then_inc(m_ps, 1)
                        u = evacuated(kind, slot)
                        if u is not None:
                            turn_values(u, min(slot // UH, NU))
                            turned_units = u + 1
                        if slot == TURNED:
                            turn_batch(1 + kind, 0)
                        if kind == 0 and slot == TURNED + 1:
                            pe.wait_ge(xt_ready, l * TP_L + B + 1)
                            pe.wait_ge(s2_exp, l * S2_L + B * H * TB)
                            project(5, (CQ, CQR), XT[:, 0:S])
                        if kind == 1 and slot in (TURNED + 1, TURNED + 2):
                            hidden(slot - TURNED - 1)
                    attended(1)
                    if kind == 0:
                        output(1)
                        turn_batch(1, 1)
                        pe.wait_ge(xt_ready, l * TP_L + B + 2)
                        project(6, (CQ, CQR), XT[:, S:2 * S])
                    else:
                        hidden(2)
                        output(1)
                        hidden(3)
                        forward(0)
                        turn_batch(2, 1)
                        for n in range(4, B * 4):
                            hidden(n)
                        forward(1)

                pe.wait_ge(wa_in, (l + 1) * 16)
                for b in range(B):
                    ins = mm(bank[6][:, b * D:(b + 1) * D], ctxT[:, b, 0:P], wcol(CV), start=True, stop=True)
                ins.then_inc(v_ps, 1)
                for b in range(B):
                    for j in range(4):
                        ins = mm(bank[7][TAIL * j:TAIL * (j + 1), b * D:(b + 1) * D], ctxT[:, b, P:SC], wcol(CV),
                                 start=True, stop=True)
                ins.then_inc(v_ps, 1)
                turn(XN, l * XN_L + NT)
                for b in range(B):
                    pe.wait_ge(xt_ready, l * TP_L + b + 1)
                    xt = XT[:, b * S:(b + 1) * S]
                    project(2 * b, (WQ, WQR), xt)
                    project(2 * b + 1, (WK, WKR), xt)
                    pe.wait_ge(v_ready, l * VR_L + 1 + UH * b)
                    for t in range(TB):
                        ins = mm(bank[6 + b][:, t * P:(t + 1) * P], XT[:, b * S + t * P:b * S + (t + 1) * P], wcol(WV),
                                 start=True, stop=True)
                    ins.then_inc(v_ps, 1)
                project(4, (CK, CKR), ctxT[:, :, :].rearrange("p b s -> p (b s)"))
                pe.wait_ge(rot_done, l * ITEM_L + 5)
                pe.wait_ge(v_ready, l * VR_L + VR_L)
                attention(0)
                pe.wait_ge(rot_done, l * ITEM_L + 7)
                attention(1)
                pe.wait_ge(layer_done, l + 2)
            post_tensor(pe, turn)


def tables():
    half = HD // 2
    inv = (1.0 / 10000.0 ** (np.arange(half, dtype=np.float32) / half)).astype(np.float32)
    ang = np.arange(S, dtype=np.float32)[:, None] * inv
    cos, sin = np.cos(ang).astype(np.float32), np.sin(ang).astype(np.float32)
    rot = np.zeros((HD, H, 2, S), np.float32)
    for d in range(HD):
        rot[d, :, 0] = cos[:, d % half]
        rot[d, :, 1] = -sin[:, d] if d < half else sin[:, d - half]
    rev = np.broadcast_to(NE - np.arange(NE, dtype=np.float32), (P, NT, NE))
    return rot.reshape(P, 2, S), np.eye(P, dtype=np.float32), np.ascontiguousarray(rev)


def layout(a):
    def turned(w):
        return np.swapaxes(w, -1, -2)

    def by_channel(w, swap=False):
        w = w.reshape(NL, H, HD, D)
        if swap:
            w = np.concatenate([w[:, :, HD // 2:], w[:, :, :HD // 2]], axis=2)
        return turned(w.transpose(0, 2, 1, 3).reshape(NL, D, D))

    qkv, cq, ck = a["L0_xcond_qkv_w"], a["L0_xcond_cq_w"], a["L0_xcond_ck_w"]
    wq, wk, wv = qkv[:, :D], qkv[:, D:2 * D], qkv[:, 2 * D:]
    wa = np.concatenate([by_channel(wq), by_channel(wq, True), by_channel(wk), by_channel(wk, True), turned(wv),
                         turned(a["L0_xcond_so_w"]), by_channel(cq), by_channel(cq, True), by_channel(ck),
                         by_channel(ck, True), turned(a["L0_xcond_cv_w"]), turned(a["L0_xcond_co_w"])], axis=2)
    f1, f2 = turned(a["L0_xcond_f1_w"]), turned(a["L0_xcond_f2_w"])
    wf = np.concatenate([f1, f2.reshape(NL, 4, P, D).transpose(0, 2, 1, 3).reshape(NL, P, 4 * D)], axis=2)
    nw = np.stack([turned(a[f"L0_xcond_n{n}_w"]) for n in (1, 2, 3)], axis=1).reshape(3 * NL, D, 2 * D).transpose(1, 0, 2)
    nb = np.stack([a[f"L0_xcond_n{n}_b"] for n in (1, 2, 3)], axis=1).reshape(3 * NL, 2, D).transpose(2, 0, 1)
    rot, ident, rev = tables()
    f2b = np.broadcast_to(a["L0_xcond_f2_b"][:, None, :], (NL, P, D))
    w1 = a["L0_ffn_w1"].transpose(2, 0, 1)
    w2 = turned(a["L0_ffn_w2"]).reshape(NE, 2, P, D).transpose(2, 0, 1, 3).reshape(P, 2 * NE, D)
    eg = np.concatenate([a["L1_ffn_rt_gate"], a["L1_ffn_sh_gate"][None]]).transpose(1, 0, 2)
    eu = np.concatenate([a["L1_ffn_rt_up"], a["L1_ffn_sh_up"][None]]).transpose(1, 0, 2)
    ed = np.concatenate([a["L1_ffn_rt_down"], a["L1_ffn_sh_down"][None]]).reshape(NE + 1, 2, P, D)
    ed = ed.transpose(2, 0, 1, 3).reshape(P, 2 * (NE + 1), D)
    return {
        "x": a["x"], "cond": a["cond_1024"].T, "ctx": turned(a["ctx_1024"]), "mask": a["mask_BxS_bf0"].reshape(-1).view(np.int32)[None],
        "mask2": a["mask_BxS2_bf0"].reshape(-1).view(np.int32)[None], "rot": rot, "ident": ident, "rev": rev, "nw": nw, "nb": nb,
        "wa": wa, "wf": wf, "f1b": a["L0_xcond_f1_b"].reshape(NL, 4, P).transpose(0, 2, 1), "f2b": f2b,
        "gb": np.stack([a["L0_ffn_ln_gamma"], a["L0_ffn_ln_beta"]], axis=1),
        "mg": np.stack([a["L0_ffn_gate_w"].T, a["L1_ffn_gate_w"]], axis=1), "w1": w1, "w2": w2,
        "watt": a["L1_xcond_W_att"].reshape(2, D, D).transpose(1, 0, 2), "vatt": a["L1_xcond_V_att"],
        "wi": a["L1_xcond_Wi"].reshape(2, D, 3 * D).transpose(1, 0, 2), "uh": a["L1_xcond_Uh"],
        "sb": a["L1_xcond_b"].reshape(3, D).T, "eg": eg, "eu": eu, "ed": ed,
    }


def kernel(**inputs):
    import concourse.bacc as bacc
    from concourse.bass_utils import run_bass_kernel_spmd

    nc = bacc.Bacc("TRN2", target_bir_lowering=False, num_devices=1)
    arrays, args = {}, []
    for name, a in layout({k: np.asarray(v) for k, v in inputs.items()}).items():
        a = np.ascontiguousarray(a)
        arrays[f"in_{name}"] = a
        args.append(nc.dram_tensor(f"in_{name}", a.shape, mybir.dt.from_np(a.dtype), kind="ExternalInput").ap())
    args.append(nc.dram_tensor("out", (B, S, D), FP32, kind="ExternalOutput").ap())
    build(nc, *args)
    return run_bass_kernel_spmd(nc, [arrays], core_ids=[0]).results[0]["out"]
```
